# Optimizing a Trainium2 kernel written in Bass

```python
import numpy as np
import jax
import jax.numpy as jnp

def _softmax(x, axis=-1):
    return jax.nn.softmax(x, axis=axis)

def _gelu(x):
    return jax.nn.gelu(x, approximate=True)

def _silu(x):
    return jax.nn.silu(x)

def _sigmoid(x):
    return jax.nn.sigmoid(x)

def _layernorm(x, axis=-1, eps=1e-05):
    m = jnp.mean(x, axis=axis, keepdims=True)
    v = jnp.var(x, axis=axis, keepdims=True)
    return (x - m) / jnp.sqrt(v + eps)

def _scatter_add(tgt, idx, src, axis=0):
    return tgt.at[idx].add(src)

def _segment_sum(src, seg, n):
    return jax.ops.segment_sum(src, seg, n)
kernel_name = 'mk_xattn_ffn_d4_seqx_r4_88f6b8'

def setup_inputs(seed: int=0):
    np.random.seed(seed)
    _w = jnp.asarray

    def _rec_inputs():
        import jax
        import jax.numpy as jnp
        _rk = jax.random.key(seed)
        x = 0.0002417 + 0.9998 * jax.random.normal(jax.random.fold_in(_rk, 1), (8, 256, 256), jnp.float32)
        _lenS = 256 - jax.random.randint(jax.random.fold_in(_rk, 7), (8,), 0, max(1, 256 // 4) + 1, jnp.int32)
        _lenS2 = 256 - jax.random.randint(jax.random.fold_in(_rk, 8), (8,), 0, max(1, 256 // 4) + 1, jnp.int32)
        _ctx_1024P = jax.random.normal(jax.random.fold_in(_rk, 11), (8, 16, 256), jnp.float32)
        _ctx_1024c = jax.random.dirichlet(jax.random.fold_in(_rk, 511), 0.3 * jnp.ones((16,), jnp.float32), (8, 256))
        _ctx_1024t = jnp.einsum('bsk,bkd->bsd', _ctx_1024c, _ctx_1024P)
        _ctx_1024t = _ctx_1024t * jax.lax.rsqrt(jnp.mean(jnp.square(_ctx_1024t)) + 1e-12) * 0.953939
        ctx_1024 = 7.22013e-05 + 1.00017 * (_ctx_1024t + 0.3 * jax.random.normal(jax.random.fold_in(_rk, 611), (8, 256, 256), jnp.float32))
        _validS = jnp.arange(256)[None, :] < _lenS[:, None]
        _validS2 = jnp.arange(256)[None, :] < _lenS2[:, None]
        _causal = jnp.tril(jnp.ones((256, 256), dtype=bool))
        mask_Bx1xSxS2_if1 = jnp.where(jnp.ones((8, 1, 256, 256), dtype=bool), 1, 0).astype(jnp.int32)
        mask_BxSxS2_ff0 = jnp.where(jnp.ones((8, 256, 256), dtype=bool), 0.0, -1000000000.0).astype(jnp.float32)
        return (x, ctx_1024, _lenS2, mask_Bx1xSxS2_if1, mask_BxSxS2_ff0)
    x, ctx_1024, _lenS2, mask_Bx1xSxS2_if1, mask_BxSxS2_ff0 = _rec_inputs()

    def _L0_xattn_setup():
        import jax, jax.numpy as jnp
        import numpy as np
        N, S, E, H = (4, 512, 256, 16)
        D = E // H
        key = jax.random.key(seed)
        ks = jax.random.split(key, 9)
        scale = 1.0 / np.sqrt(E)
        return {'values': jax.random.normal(ks[0], (N, S, E), jnp.float32), 'keys': jax.random.normal(ks[1], (N, S, E), jnp.float32), 'query': jax.random.normal(ks[2], (N, S, E), jnp.float32), 'mask': jnp.ones((N, 1, S, S), jnp.int32), 'Wv': jax.random.normal(ks[3], (E, E), jnp.float32) * scale, 'Wk': jax.random.normal(ks[4], (E, E), jnp.float32) * scale, 'Wq': jax.random.normal(ks[5], (E, E), jnp.float32) * scale, 'Wo': jax.random.normal(ks[6], (E, E), jnp.float32) * scale, 'bo': jax.random.normal(ks[7], (E,), jnp.float32) * scale}
    _L0_xattn_all = _L0_xattn_setup()
    _L0_xattn_in = {k: v for k, v in _L0_xattn_all.items() if k in ('Wv', 'Wk', 'Wq', 'Wo', 'bo')}
    del _L0_xattn_all

    def _L0_ffn_setup():
        import jax, jax.numpy as jnp
        import numpy as np
        HIDDEN = 256
        N_EXPERTS = 8
        TOP_K = 2
        INTER = 352
        N_SHARED = 2
        SCALE = 1.0
        key = jax.random.key(seed)
        ks = jax.random.split(key, 9)
        s_h = 1.0 / np.sqrt(HIDDEN)
        s_i = 1.0 / np.sqrt(INTER)
        x = jax.random.normal(ks[0], (2, 512, HIDDEN), dtype=jnp.float32)
        gate_w = jax.random.uniform(ks[1], (N_EXPERTS, HIDDEN), jnp.float32, -s_h, s_h)
        wg = jax.random.uniform(ks[2], (N_EXPERTS, HIDDEN, INTER), jnp.float32, -s_h, s_h)
        wu = jax.random.uniform(ks[3], (N_EXPERTS, HIDDEN, INTER), jnp.float32, -s_h, s_h)
        wd = jax.random.uniform(ks[4], (N_EXPERTS, INTER, HIDDEN), jnp.float32, -s_i, s_i)
        si = INTER * N_SHARED
        s_si = 1.0 / np.sqrt(si)
        swg = jax.random.uniform(ks[5], (HIDDEN, si), jnp.float32, -s_h, s_h)
        swu = jax.random.uniform(ks[6], (HIDDEN, si), jnp.float32, -s_h, s_h)
        swd = jax.random.uniform(ks[7], (si, HIDDEN), jnp.float32, -s_si, s_si)
        return {'x': x, 'gate_w': gate_w, 'wg': wg, 'wu': wu, 'wd': wd, 'swg': swg, 'swu': swu, 'swd': swd}
    _L0_ffn_all = _L0_ffn_setup()
    _L0_ffn_in = {k: v for k, v in _L0_ffn_all.items() if k in ('gate_w', 'wg', 'wu', 'wd', 'swg', 'swu', 'swd')}
    del _L0_ffn_all

    def _L1_xattn_setup():
        import jax, jax.numpy as jnp
        import numpy as np
        B, S, D, H = (4, 512, 256, 256)
        key = jax.random.key(seed)
        k1, k2, k3, k4, k5, k6 = jax.random.split(key, 6)
        return {'x1': jax.random.normal(k1, (B, S, D), dtype=jnp.float32), 'x2': jax.random.normal(k2, (B, S, D), dtype=jnp.float32), 'x3': jax.random.normal(k3, (B, S, D), dtype=jnp.float32), 'mask': jnp.zeros((B, S, S), dtype=jnp.float32), 'Wq': jax.random.normal(k4, (H, D), dtype=jnp.float32) * (1.0 / np.sqrt(D)), 'Wk': jax.random.normal(k5, (H, D), dtype=jnp.float32) * (1.0 / np.sqrt(D)), 'Wv': jax.random.normal(k6, (H, D), dtype=jnp.float32) * (1.0 / np.sqrt(D))}
    _L1_xattn_all = _L1_xattn_setup()
    _L1_xattn_in = {k: v for k, v in _L1_xattn_all.items() if k in ('Wq', 'Wk', 'Wv')}
    del _L1_xattn_all

    def _L1_ffn_setup():
        import jax, jax.numpy as jnp
        import numpy as np
        D_MODEL = 256
        D_FF = 1024
        N_EXPERTS = 8
        TOP_K = 2

        def _ffn(x, w1, b1, w2, b2):
            h = jax.nn.gelu(x @ w1.T + b1)
            return h @ w2.T + b2
        key = jax.random.key(seed)
        ks = jax.random.split(key, 12)
        s = 0.02
        x = jax.random.normal(ks[0], (4, 512, D_MODEL), dtype=jnp.float32)
        shared_w1 = jax.random.normal(ks[1], (D_FF, D_MODEL), dtype=jnp.float32) * s
        shared_b1 = jnp.zeros((D_FF,), dtype=jnp.float32)
        shared_w2 = jax.random.normal(ks[2], (D_MODEL, D_FF), dtype=jnp.float32) * s
        shared_b2 = jnp.zeros((D_MODEL,), dtype=jnp.float32)
        router_w = jax.random.normal(ks[3], (N_EXPERTS, D_MODEL), dtype=jnp.float32) * s
        router_b = jnp.zeros((N_EXPERTS,), dtype=jnp.float32)
        spec_w1 = jax.random.normal(ks[4], (N_EXPERTS, D_FF, D_MODEL), dtype=jnp.float32) * s
        spec_b1 = jnp.zeros((N_EXPERTS, D_FF), dtype=jnp.float32)
        spec_w2 = jax.random.normal(ks[5], (N_EXPERTS, D_MODEL, D_FF), dtype=jnp.float32) * s
        spec_b2 = jnp.zeros((N_EXPERTS, D_MODEL), dtype=jnp.float32)
        return dict(x=x, shared_w1=shared_w1, shared_b1=shared_b1, shared_w2=shared_w2, shared_b2=shared_b2, router_w=router_w, router_b=router_b, spec_w1=spec_w1, spec_b1=spec_b1, spec_w2=spec_w2, spec_b2=spec_b2)
    _L1_ffn_all = _L1_ffn_setup()
    _L1_ffn_in = {k: v for k, v in _L1_ffn_all.items() if k in ('shared_w1', 'shared_b1', 'shared_w2', 'shared_b2', 'router_w', 'router_b', 'spec_w1', 'spec_b1', 'spec_w2', 'spec_b2')}
    del _L1_ffn_all

    def _L2_xattn_setup():
        import jax, jax.numpy as jnp
        import numpy as np
        import math
        NUM_HEADS = 16
        D_MODEL = 256
        BATCH = 4
        SEQ = 512
        NEG_INF = -1000000000.0
        key = jax.random.key(seed)
        ks = jax.random.split(key, 8)
        scale = 1.0 / math.sqrt(D_MODEL)
        return {'queries': jax.random.normal(ks[0], (BATCH, SEQ, D_MODEL), jnp.float32), 'keys': jax.random.normal(ks[1], (BATCH, SEQ, D_MODEL), jnp.float32), 'values': jax.random.normal(ks[2], (BATCH, SEQ, D_MODEL), jnp.float32), 'Wq': jax.random.normal(ks[3], (D_MODEL, D_MODEL), jnp.float32) * scale, 'Wk': jax.random.normal(ks[4], (D_MODEL, D_MODEL), jnp.float32) * scale, 'Wv': jax.random.normal(ks[5], (D_MODEL, D_MODEL), jnp.float32) * scale, 'Wo': jax.random.normal(ks[6], (D_MODEL, D_MODEL), jnp.float32) * scale, 'valid_lens': jax.random.randint(ks[7], (BATCH,), 1, SEQ + 1).astype(jnp.int64)}
    _L2_xattn_all = _L2_xattn_setup()
    _L2_xattn_in = {k: v for k, v in _L2_xattn_all.items() if k in ('Wq', 'Wk', 'Wv', 'Wo')}
    del _L2_xattn_all

    def _L2_ffn_setup():
        import math
        import jax, jax.numpy as jnp
        import numpy as np
        D_MODEL = 256
        D_FF = 1024
        E = 8
        K = 2
        CF = 1.25
        CLAMP = 10000.0
        key = jax.random.key(seed)
        k0, k1, k2, k3 = jax.random.split(key, 4)
        B, S = (4, 512)
        x = jax.random.normal(k0, (B, S, D_MODEL), dtype=jnp.float32)
        ln_gamma = jnp.ones((D_MODEL,), jnp.float32)
        ln_beta = jnp.zeros((D_MODEL,), jnp.float32)
        rb = 0.02 * math.sqrt(3.0)
        Wr = jax.random.uniform(k1, (E, D_MODEL), jnp.float32, -rb, rb)
        b12 = math.sqrt(6.0 / (D_MODEL + 2 * D_FF))
        W12 = jax.random.uniform(k2, (E, 2 * D_FF, D_MODEL), jnp.float32, -b12, b12)
        b3 = math.sqrt(6.0 / (D_FF + D_MODEL))
        W3 = jax.random.uniform(k3, (E, D_MODEL, D_FF), jnp.float32, -b3, b3)
        return {'x': x, 'ln_gamma': ln_gamma, 'ln_beta': ln_beta, 'Wr': Wr, 'W12': W12, 'W3': W3}
    _L2_ffn_all = _L2_ffn_setup()
    _L2_ffn_in = {k: v for k, v in _L2_ffn_all.items() if k in ('ln_gamma', 'ln_beta', 'Wr', 'W12', 'W3')}
    del _L2_ffn_all

    def _L3_xattn_setup():
        import jax, jax.numpy as jnp
        import numpy as np
        B, SD, SE, D, H = (4, 512, 512, 256, 16)
        HD = D // H

        def _mha(xq, xk, xv, Wq, bq, Wk, bk, Wv, bv, Wo, bo, causal):
            q = jnp.einsum('bsd,hde->bhse', xq, Wq) + bq[None, :, None, :]
            k = jnp.einsum('bsd,hde->bhse', xk, Wk) + bk[None, :, None, :]
            v = jnp.einsum('bsd,hde->bhse', xv, Wv) + bv[None, :, None, :]
            scale = 1.0 / jnp.sqrt(jnp.asarray(HD, q.dtype))
            scores = jnp.einsum('bhqe,bhke->bhqk', q, k) * scale
            if causal:
                mask = jnp.tril(jnp.ones((q.shape[2], k.shape[2]), bool))
                scores = jnp.where(mask, scores, jnp.finfo(scores.dtype).min)
            w = jax.nn.softmax(scores, axis=-1)
            out = jnp.einsum('bhqk,bhke->bhqe', w, v)
            out = out.transpose(0, 2, 1, 3).reshape(out.shape[0], out.shape[2], D)
            return out @ Wo + bo
        key = jax.random.key(seed)
        ks = jax.random.split(key, 19)
        sd = 1.0 / np.sqrt(D)
        n = lambda k, shape, s: jax.random.normal(k, shape, jnp.float32) * s
        inp = {'x': n(ks[0], (B, SD, D), 1.0), 'encoder_k': n(ks[1], (B, SE, D), 1.0), 'encoder_v': n(ks[2], (B, SE, D), 1.0), 'Wq1': n(ks[3], (H, D, HD), sd), 'bq1': jnp.zeros((H, HD), jnp.float32), 'Wk1': n(ks[4], (H, D, HD), sd), 'bk1': jnp.zeros((H, HD), jnp.float32), 'Wv1': n(ks[5], (H, D, HD), sd), 'bv1': jnp.zeros((H, HD), jnp.float32), 'Wo1': n(ks[6], (D, D), sd), 'bo1': jnp.zeros((D,), jnp.float32), 'Wq2': n(ks[7], (H, D, HD), sd), 'bq2': jnp.zeros((H, HD), jnp.float32), 'Wk2': n(ks[8], (H, D, HD), sd), 'bk2': jnp.zeros((H, HD), jnp.float32), 'Wv2': n(ks[9], (H, D, HD), sd), 'bv2': jnp.zeros((H, HD), jnp.float32), 'Wo2': n(ks[10], (D, D), sd), 'bo2': jnp.zeros((D,), jnp.float32)}
        return inp
    _L3_xattn_all = _L3_xattn_setup()
    _L3_xattn_in = {k: v for k, v in _L3_xattn_all.items() if k in ('Wq1', 'bq1', 'Wk1', 'bk1', 'Wv1', 'bv1', 'Wo1', 'bo1', 'Wq2', 'bq2', 'Wk2', 'bk2', 'Wv2', 'bv2', 'Wo2', 'bo2')}
    del _L3_xattn_all

    def _L3_ffn_setup():
        import jax, jax.numpy as jnp
        import numpy as np
        BEST_K = 2

        def _expert(xf, w1, w3, w2):
            return jax.nn.silu(xf @ w1) * (xf @ w3) @ w2
        key = jax.random.key(seed)
        ks = jax.random.split(key, 9)
        E, S_sh, D, H = (8, 2, 256, 128)
        B, S = (2, 512)
        w = lambda k, shape: jax.random.normal(k, shape, dtype=jnp.float32) * 0.02
        return {'x': jax.random.normal(ks[0], (B, S, D), dtype=jnp.float32), 'router_w': w(ks[1], (D, E)), 'router_b': jnp.zeros((E,), dtype=jnp.float32), 'routed_w1': w(ks[2], (E, D, H)), 'routed_w3': w(ks[3], (E, D, H)), 'routed_w2': w(ks[4], (E, H, D)), 'shared_w1': w(ks[5], (S_sh, D, H)), 'shared_w3': w(ks[6], (S_sh, D, H)), 'shared_w2': w(ks[7], (S_sh, H, D))}
    _L3_ffn_all = _L3_ffn_setup()
    _L3_ffn_in = {k: v for k, v in _L3_ffn_all.items() if k in ('router_w', 'router_b', 'routed_w1', 'routed_w3', 'routed_w2', 'shared_w1', 'shared_w3', 'shared_w2')}
    del _L3_ffn_all
    return {'x': x, 'ctx_1024': ctx_1024, '_lenS2': _lenS2, 'mask_Bx1xSxS2_if1': mask_Bx1xSxS2_if1, 'mask_BxSxS2_ff0': mask_BxSxS2_ff0, 'L0_xattn_Wv': _L0_xattn_in['Wv'], 'L0_xattn_Wk': _L0_xattn_in['Wk'], 'L0_xattn_Wq': _L0_xattn_in['Wq'], 'L0_xattn_Wo': _L0_xattn_in['Wo'], 'L0_xattn_bo': _L0_xattn_in['bo'], 'L0_ffn_gate_w': _L0_ffn_in['gate_w'], 'L0_ffn_wg': _L0_ffn_in['wg'], 'L0_ffn_wu': _L0_ffn_in['wu'], 'L0_ffn_wd': _L0_ffn_in['wd'], 'L0_ffn_swg': _L0_ffn_in['swg'], 'L0_ffn_swu': _L0_ffn_in['swu'], 'L0_ffn_swd': _L0_ffn_in['swd'], 'L1_xattn_Wq': _L1_xattn_in['Wq'], 'L1_xattn_Wk': _L1_xattn_in['Wk'], 'L1_xattn_Wv': _L1_xattn_in['Wv'], 'L1_ffn_shared_w1': _L1_ffn_in['shared_w1'], 'L1_ffn_shared_b1': _L1_ffn_in['shared_b1'], 'L1_ffn_shared_w2': _L1_ffn_in['shared_w2'], 'L1_ffn_shared_b2': _L1_ffn_in['shared_b2'], 'L1_ffn_router_w': _L1_ffn_in['router_w'], 'L1_ffn_router_b': _L1_ffn_in['router_b'], 'L1_ffn_spec_w1': _L1_ffn_in['spec_w1'], 'L1_ffn_spec_b1': _L1_ffn_in['spec_b1'], 'L1_ffn_spec_w2': _L1_ffn_in['spec_w2'], 'L1_ffn_spec_b2': _L1_ffn_in['spec_b2'], 'L2_xattn_Wq': _L2_xattn_in['Wq'], 'L2_xattn_Wk': _L2_xattn_in['Wk'], 'L2_xattn_Wv': _L2_xattn_in['Wv'], 'L2_xattn_Wo': _L2_xattn_in['Wo'], 'L2_ffn_ln_gamma': _L2_ffn_in['ln_gamma'], 'L2_ffn_ln_beta': _L2_ffn_in['ln_beta'], 'L2_ffn_Wr': _L2_ffn_in['Wr'], 'L2_ffn_W12': _L2_ffn_in['W12'], 'L2_ffn_W3': _L2_ffn_in['W3'], 'L3_xattn_Wq1': _L3_xattn_in['Wq1'], 'L3_xattn_bq1': _L3_xattn_in['bq1'], 'L3_xattn_Wk1': _L3_xattn_in['Wk1'], 'L3_xattn_bk1': _L3_xattn_in['bk1'], 'L3_xattn_Wv1': _L3_xattn_in['Wv1'], 'L3_xattn_bv1': _L3_xattn_in['bv1'], 'L3_xattn_Wo1': _L3_xattn_in['Wo1'], 'L3_xattn_bo1': _L3_xattn_in['bo1'], 'L3_xattn_Wq2': _L3_xattn_in['Wq2'], 'L3_xattn_bq2': _L3_xattn_in['bq2'], 'L3_xattn_Wk2': _L3_xattn_in['Wk2'], 'L3_xattn_bk2': _L3_xattn_in['bk2'], 'L3_xattn_Wv2': _L3_xattn_in['Wv2'], 'L3_xattn_bv2': _L3_xattn_in['bv2'], 'L3_xattn_Wo2': _L3_xattn_in['Wo2'], 'L3_xattn_bo2': _L3_xattn_in['bo2'], 'L3_ffn_router_w': _L3_ffn_in['router_w'], 'L3_ffn_router_b': _L3_ffn_in['router_b'], 'L3_ffn_routed_w1': _L3_ffn_in['routed_w1'], 'L3_ffn_routed_w3': _L3_ffn_in['routed_w3'], 'L3_ffn_routed_w2': _L3_ffn_in['routed_w2'], 'L3_ffn_shared_w1': _L3_ffn_in['shared_w1'], 'L3_ffn_shared_w3': _L3_ffn_in['shared_w3'], 'L3_ffn_shared_w2': _L3_ffn_in['shared_w2']}

def reference(x, ctx_1024, _lenS2, mask_Bx1xSxS2_if1, mask_BxSxS2_ff0, L0_xattn_Wv, L0_xattn_Wk, L0_xattn_Wq, L0_xattn_Wo, L0_xattn_bo, L0_ffn_gate_w, L0_ffn_wg, L0_ffn_wu, L0_ffn_wd, L0_ffn_swg, L0_ffn_swu, L0_ffn_swd, L1_xattn_Wq, L1_xattn_Wk, L1_xattn_Wv, L1_ffn_shared_w1, L1_ffn_shared_b1, L1_ffn_shared_w2, L1_ffn_shared_b2, L1_ffn_router_w, L1_ffn_router_b, L1_ffn_spec_w1, L1_ffn_spec_b1, L1_ffn_spec_w2, L1_ffn_spec_b2, L2_xattn_Wq, L2_xattn_Wk, L2_xattn_Wv, L2_xattn_Wo, L2_ffn_ln_gamma, L2_ffn_ln_beta, L2_ffn_Wr, L2_ffn_W12, L2_ffn_W3, L3_xattn_Wq1, L3_xattn_bq1, L3_xattn_Wk1, L3_xattn_bk1, L3_xattn_Wv1, L3_xattn_bv1, L3_xattn_Wo1, L3_xattn_bo1, L3_xattn_Wq2, L3_xattn_bq2, L3_xattn_Wk2, L3_xattn_bk2, L3_xattn_Wv2, L3_xattn_bv2, L3_xattn_Wo2, L3_xattn_bo2, L3_ffn_router_w, L3_ffn_router_b, L3_ffn_routed_w1, L3_ffn_routed_w3, L3_ffn_routed_w2, L3_ffn_shared_w1, L3_ffn_shared_w3, L3_ffn_shared_w2):
    import jax
    import jax.numpy as jnp

    def _L0_xattn_ref(values, keys, query, mask, Wv, Wk, Wq, Wo, bo):
        import jax, jax.numpy as jnp
        import numpy as np
        N, S, E, H = (4, 512, 256, 16)
        D = E // H
        n, q_len = (query.shape[0], query.shape[1])
        v = (values @ Wv.T).reshape(n, -1, H, D)
        k = (keys @ Wk.T).reshape(n, -1, H, D)
        q = (query @ Wq.T).reshape(n, q_len, H, D)
        energy = jnp.einsum('nqhd,nkhd->nhqk', q, k)
        energy = jnp.where(mask == 0, jnp.float32(-1e+20), energy)
        attn = jax.nn.softmax(energy / np.sqrt(D), axis=3)
        out = jnp.einsum('nhqk,nkhd->nqhd', attn, v).reshape(n, q_len, E)
        return out @ Wo.T + bo

    def _L0_ffn_ref(x, gate_w, wg, wu, wd, swg, swu, swd):
        import jax, jax.numpy as jnp
        import numpy as np
        HIDDEN = 256
        N_EXPERTS = 8
        TOP_K = 2
        INTER = 352
        N_SHARED = 2
        SCALE = 1.0
        B, S, H = x.shape
        xf = x.reshape(-1, H)
        T = xf.shape[0]
        logits = xf.astype(jnp.float32) @ gate_w.astype(jnp.float32).T
        scores = jax.nn.softmax(logits, axis=-1)
        topw, topi = jax.lax.top_k(scores, TOP_K)
        denom = topw.sum(axis=-1, keepdims=True) + 1e-20
        topw = topw / denom * SCALE
        wdense = jnp.zeros((T, N_EXPERTS), jnp.float32).at[jnp.arange(T)[:, None], topi].set(topw)
        hg = jnp.einsum('th,ehi->eti', xf, wg)
        hu = jnp.einsum('th,ehi->eti', xf, wu)
        eo = jnp.einsum('eti,eih->eth', jax.nn.silu(hg) * hu, wd)
        y = jnp.einsum('te,eth->th', wdense, eo)
        shared = jax.nn.silu(xf @ swg) * (xf @ swu) @ swd
        return (y + shared).reshape(B, S, H)

    def _L1_xattn_ref(x1, x2, x3, mask, Wq, Wk, Wv):
        import jax, jax.numpy as jnp
        import numpy as np
        B, S, D, H = (4, 512, 256, 256)
        q = jnp.einsum('bsd,hd->bsh', x1, Wq)
        k = jnp.einsum('bsd,hd->bsh', x2, Wk)
        v = jnp.einsum('bsd,hd->bsh', x3, Wv)
        scale = 1.0 / jnp.sqrt(jnp.float32(H))
        scores = jnp.einsum('bqh,bkh->bqk', q, k) * scale
        weights = jax.nn.softmax(scores + mask, axis=-1)
        out = jnp.einsum('bqk,bkh->bqh', weights, v)
        return out

    def _L1_ffn_ref(x, shared_w1, shared_b1, shared_w2, shared_b2, router_w, router_b, spec_w1, spec_b1, spec_w2, spec_b2):
        import jax, jax.numpy as jnp
        import numpy as np
        D_MODEL = 256
        D_FF = 1024
        N_EXPERTS = 8
        TOP_K = 2

        def _ffn(x, w1, b1, w2, b2):
            h = jax.nn.gelu(x @ w1.T + b1)
            return h @ w2.T + b2
        B, T, D = x.shape
        xf = x.reshape(-1, D)
        U = xf.shape[0]
        logits = xf @ router_w.T + router_b
        routing = jax.nn.softmax(logits, axis=-1)
        sel_w, sel_idx = jax.lax.top_k(routing, TOP_K)
        sel_w = sel_w / sel_w.sum(axis=-1, keepdims=True)
        comb = jnp.zeros_like(routing).at[jnp.arange(U)[:, None], sel_idx].set(sel_w)
        shared_out = _ffn(xf, shared_w1, shared_b1, shared_w2, shared_b2)

        def body(acc, params):
            w1, b1, w2, b2, we = params
            return (acc + we[:, None] * _ffn(xf, w1, b1, w2, b2), None)
        acc0 = jnp.zeros_like(shared_out)
        acc, _ = jax.lax.scan(body, acc0, (spec_w1, spec_b1, spec_w2, spec_b2, comb.T))
        return (shared_out + acc).reshape(B, T, D)

    def _L2_xattn_ref(queries, keys, values, Wq, Wk, Wv, Wo, valid_lens):
        import jax, jax.numpy as jnp
        import numpy as np
        import math
        NUM_HEADS = 16
        D_MODEL = 256
        BATCH = 4
        SEQ = 512
        NEG_INF = -1000000000.0
        B, S, D = queries.shape
        H = NUM_HEADS
        dh = D // H

        def split_heads(x, W):
            y = jnp.einsum('bsd,od->bso', x, W)
            return y.reshape(B, S, H, dh).transpose(0, 2, 1, 3)
        q = split_heads(queries, Wq)
        k = split_heads(keys, Wk)
        v = split_heads(values, Wv)
        scores = jnp.einsum('bhqd,bhkd->bhqk', q, k) / math.sqrt(dh)
        mask = jnp.arange(S)[None, None, None, :] >= valid_lens[:, None, None, None]
        scores = jnp.where(mask, NEG_INF, scores)
        attn = jax.nn.softmax(scores, axis=-1)
        out = jnp.einsum('bhqk,bhkd->bhqd', attn, v)
        out = out.transpose(0, 2, 1, 3).reshape(B, S, D)
        return jnp.einsum('bsd,od->bso', out, Wo)

    def _L2_ffn_ref(x, ln_gamma, ln_beta, Wr, W12, W3):
        import math
        import jax, jax.numpy as jnp
        import numpy as np
        D_MODEL = 256
        D_FF = 1024
        E = 8
        K = 2
        CF = 1.25
        CLAMP = 10000.0
        B, S, D = x.shape
        T = B * S
        xf = x.reshape(T, D)
        mu = xf.mean(-1, keepdims=True)
        var = ((xf - mu) ** 2).mean(-1, keepdims=True)
        xn = (xf - mu) / jnp.sqrt(var + 1e-05) * ln_gamma + ln_beta
        logits = jnp.clip(xn @ Wr.T, -CLAMP, CLAMP)
        m = logits.max(-1, keepdims=True)
        ex = jnp.exp(logits - m)
        probs = ex / (ex.sum(-1, keepdims=True) + 1e-12)
        top_p, top_i = jax.lax.top_k(probs, K)
        Sslots = T * K
        experts = top_i.reshape(-1)
        weights = top_p.reshape(-1)
        tokens = jnp.repeat(jnp.arange(T, dtype=jnp.int32), K)
        order = jnp.argsort(experts, stable=True)
        e_s = experts[order]
        w_s = weights[order]
        t_s = tokens[order]
        counts = jnp.bincount(e_s, length=E)
        offsets = jnp.concatenate([jnp.zeros((1,), counts.dtype), jnp.cumsum(counts)])
        rank = jnp.arange(Sslots, dtype=counts.dtype) - offsets[e_s]
        cap = max(1, math.ceil(math.ceil(T * K * CF) / E))
        kept = rank < cap
        pos = jnp.where(kept, rank, cap)
        buf = jnp.zeros((E, cap, D), x.dtype).at[e_s, pos].set(xn[t_s], mode='drop')
        gu = jnp.einsum('ecd,efd->ecf', buf, W12)
        g, u = (gu[..., :D_FF], gu[..., D_FF:])
        h = jax.nn.silu(g) * u
        y = jnp.einsum('ecf,edf->ecd', h, W3)
        y_slot = y[e_s, jnp.minimum(pos, cap - 1)] * (w_s * kept.astype(x.dtype))[:, None]
        out = jnp.zeros((T, D), x.dtype).at[t_s].add(y_slot)
        return out.reshape(B, S, D)

    def _L3_xattn_ref(x, encoder_k, encoder_v, Wq1, bq1, Wk1, bk1, Wv1, bv1, Wo1, bo1, Wq2, bq2, Wk2, bk2, Wv2, bv2, Wo2, bo2):
        import jax, jax.numpy as jnp
        import numpy as np
        B, SD, SE, D, H = (4, 512, 512, 256, 16)
        HD = D // H

        def _mha(xq, xk, xv, Wq, bq, Wk, bk, Wv, bv, Wo, bo, causal):
            q = jnp.einsum('bsd,hde->bhse', xq, Wq) + bq[None, :, None, :]
            k = jnp.einsum('bsd,hde->bhse', xk, Wk) + bk[None, :, None, :]
            v = jnp.einsum('bsd,hde->bhse', xv, Wv) + bv[None, :, None, :]
            scale = 1.0 / jnp.sqrt(jnp.asarray(HD, q.dtype))
            scores = jnp.einsum('bhqe,bhke->bhqk', q, k) * scale
            if causal:
                mask = jnp.tril(jnp.ones((q.shape[2], k.shape[2]), bool))
                scores = jnp.where(mask, scores, jnp.finfo(scores.dtype).min)
            w = jax.nn.softmax(scores, axis=-1)
            out = jnp.einsum('bhqk,bhke->bhqe', w, v)
            out = out.transpose(0, 2, 1, 3).reshape(out.shape[0], out.shape[2], D)
            return out @ Wo + bo
        h = _mha(x, x, x, Wq1, bq1, Wk1, bk1, Wv1, bv1, Wo1, bo1, causal=True)
        out = _mha(h, encoder_k, encoder_v, Wq2, bq2, Wk2, bk2, Wv2, bv2, Wo2, bo2, causal=False)
        return out

    def _L3_ffn_ref(x, router_w, router_b, routed_w1, routed_w3, routed_w2, shared_w1, shared_w3, shared_w2):
        import jax, jax.numpy as jnp
        import numpy as np
        BEST_K = 2

        def _expert(xf, w1, w3, w2):
            return jax.nn.silu(xf @ w1) * (xf @ w3) @ w2
        B, S, D = x.shape
        T = B * S
        xf = x.reshape(T, D)
        logits = xf @ router_w + router_b
        topk_vals, topk_idx = jax.lax.top_k(logits, BEST_K)
        sparse = jnp.full_like(logits, -jnp.inf)
        sparse = sparse.at[jnp.arange(T)[:, None], topk_idx].set(topk_vals)
        gates = jax.nn.softmax(sparse, axis=-1)
        routed = jax.vmap(_expert, in_axes=(None, 0, 0, 0))(xf, routed_w1, routed_w3, routed_w2)
        routed_out = jnp.einsum('etd,te->td', routed, gates)
        shared_out = jax.vmap(_expert, in_axes=(None, 0, 0, 0))(xf, shared_w1, shared_w3, shared_w2).sum(axis=0)
        return (routed_out + shared_out).reshape(B, S, D)
    x = x + _L0_xattn_ref(ctx_1024, ctx_1024, _layernorm(x, axis=-1), mask_Bx1xSxS2_if1, L0_xattn_Wv, L0_xattn_Wk, L0_xattn_Wq, L0_xattn_Wo, L0_xattn_bo)
    x = x + _L0_ffn_ref(_layernorm(x, axis=-1), L0_ffn_gate_w, L0_ffn_wg, L0_ffn_wu, L0_ffn_wd, L0_ffn_swg, L0_ffn_swu, L0_ffn_swd)
    x = x + _L1_xattn_ref(_layernorm(x, axis=-1), ctx_1024, ctx_1024, mask_BxSxS2_ff0, L1_xattn_Wq, L1_xattn_Wk, L1_xattn_Wv)
    x = x + _L1_ffn_ref(_layernorm(x, axis=-1), L1_ffn_shared_w1, L1_ffn_shared_b1, L1_ffn_shared_w2, L1_ffn_shared_b2, L1_ffn_router_w, L1_ffn_router_b, L1_ffn_spec_w1, L1_ffn_spec_b1, L1_ffn_spec_w2, L1_ffn_spec_b2)
    x = x + _L2_xattn_ref(_layernorm(x, axis=-1), ctx_1024, ctx_1024, L2_xattn_Wq, L2_xattn_Wk, L2_xattn_Wv, L2_xattn_Wo, _lenS2)
    x = x + _L2_ffn_ref(_layernorm(x, axis=-1), L2_ffn_ln_gamma, L2_ffn_ln_beta, L2_ffn_Wr, L2_ffn_W12, L2_ffn_W3)
    x = x + _L3_xattn_ref(_layernorm(x, axis=-1), ctx_1024, ctx_1024, L3_xattn_Wq1, L3_xattn_bq1, L3_xattn_Wk1, L3_xattn_bk1, L3_xattn_Wv1, L3_xattn_bv1, L3_xattn_Wo1, L3_xattn_bo1, L3_xattn_Wq2, L3_xattn_bq2, L3_xattn_Wk2, L3_xattn_bk2, L3_xattn_Wv2, L3_xattn_bv2, L3_xattn_Wo2, L3_xattn_bo2)
    x = x + _L3_ffn_ref(_layernorm(x, axis=-1), L3_ffn_router_w, L3_ffn_router_b, L3_ffn_routed_w1, L3_ffn_routed_w3, L3_ffn_routed_w2, L3_ffn_shared_w1, L3_ffn_shared_w3, L3_ffn_shared_w2)
    return x

_drawn_inputs = setup_inputs


def setup_inputs(seed=0):
    import zlib

    import numpy as np

    out = dict(_drawn_inputs(seed))
    spreads = {'L1_ffn_shared_b1': (0.0, 0.336),
     'L1_ffn_shared_b2': (0.0, 0.1),
     'L1_ffn_router_b': (0.0, 0.1),
     'L1_ffn_spec_b1': (0.0, 0.454),
     'L1_ffn_spec_b2': (0.0, 0.1),
     'L2_ffn_ln_gamma': (1.0, 0.6),
     'L2_ffn_ln_beta': (0.0, 0.8),
     'L3_xattn_bq1': (0.0, 0.8),
     'L3_xattn_bk1': (0.0, 0.8),
     'L3_xattn_bv1': (0.0, 0.566),
     'L3_xattn_bo1': (0.0, 0.607),
     'L3_xattn_bq2': (0.0, 0.581),
     'L3_xattn_bk2': (0.0, 0.8),
     'L3_xattn_bv2': (0.0, 0.1),
     'L3_xattn_bo2': (0.0, 0.1),
     'L3_ffn_router_b': (0.0, 0.8)}
    factors = {'L3_xattn_Wq1': 4.502,
     'L3_xattn_Wk1': 4.546,
     'L3_ffn_router_w': 8.0,
     'L3_ffn_routed_w1': 8.0,
     'L3_ffn_routed_w3': 8.0,
     'L3_ffn_routed_w2': 8.0,
     'L3_ffn_shared_w1': 5.137,
     'L3_ffn_shared_w3': 5.09,
     'L3_ffn_shared_w2': 5.039}
    for name, (base, spread) in spreads.items():
        noise = np.random.default_rng([zlib.crc32(name.encode()), seed]).standard_normal(out[name].shape)
        drawn = base * np.exp(spread * noise) if base else spread * noise
        out[name] = jnp.asarray(drawn.astype(out[name].dtype))
    for name, factor in factors.items():
        out[name] = (out[name] * factor).astype(out[name].dtype)
    return out
```

```python
import concourse.bass as bass
from concourse import mybir
from contextlib import ExitStack

F32 = mybir.dt.float32
BF16 = mybir.dt.bfloat16
I32 = mybir.dt.int32
ALU = mybir.AluOpType
ACT = mybir.ActivationFunctionType
AX = mybir.AxisListType

P = 128
B, S, D = 8, 256, 256
T = B * S
NT = T // P
KC = D // P
QT = S // P
H, DH = 16, 16
HG = 4
NG = H // HG
HP = 32
EPS = 1e-5
MASKED = -1e20

E = 8
TK = 2
ST = 256
RT = TK * T // ST + E
XT = T // ST
XW = D + 2
NOWHERE = 1 << 20

L0Q, L0K, L0V, L0O, L1Q, L1K, L1V, L2Q, L2K, L2V, L2O = range(11)
AQ, AK, AV, AO, BQ, BK, BV, BO = range(11, 19)
NW = 19


class Ffn:

    def __init__(self, name, blocks, gated, shared, func):
        self.name = name
        self.blocks = blocks
        self.gated = gated
        self.shared = shared
        self.func = func
        self.up = (2 if gated else 1) * KC * blocks * P
        self.b1 = 0 if gated else blocks
        self.cols = self.up + blocks * D + self.b1
        self.groups = blocks if gated else blocks // 2
        self.banks = {4: 4, 3: 3, 8: 4, 1: 2}[self.groups]
        self.tiles = shared * XT + RT


FFNS = [Ffn("L0f", 3, True, 2, ACT.Silu), Ffn("L1f", 8, False, 1, ACT.Gelu_apprx_tanh),
        Ffn("L2f", 8, True, 0, ACT.Silu), Ffn("L3f", 1, True, 2, ACT.Silu)]
CAP = -(-(-(-T * TK * 5 // 4)) // E)


def is_int(n):
    return isinstance(n, int)


def nth(n, par):
    return 8 * (n - par) + 16


def nth2(n, par):
    return 16 * (n - par)


class Chain:

    def __init__(self, eng, sem):
        self.eng, self.sem, self.n = eng, sem, 0

    def __call__(self, ins):
        self.n += 1
        ins.then_inc(self.sem, 1)
        self.eng.wait_ge(self.sem, self.n)


class Stage:

    def __init__(self, nc, name):
        self.nc, self.sems, self.name, self.ctx = nc, [], name, ExitStack()

    def sb(self, name, shape, dt=F32):
        return self.ctx.enter_context(self.nc.sbuf_tensor(f"{self.name}_{name}", shape, dt))

    def pb(self, name, shape, dt=F32):
        return self.ctx.enter_context(self.nc.psum_tensor(f"{self.name}_{name}", shape, dt))

    def sem(self, name):
        handle = self.nc.alloc_semaphore(name=f"{self.name}_{name}")
        self.sems.append(handle)
        return handle

    def close(self):
        self.nc.clear_and_free_semaphores(self.sems)
        self.nc.all_engine_barrier()


def layer_norm_stats(nc, v, link, src, stats, mv, sq_ready, sq_done, seen):
    with v.Fori(0, NT) as t:
        nc.vector.bn_stats(stats[:, bass.ds(t, 1), :], src[:, bass.ds(t, 1), 0:D]).then_inc(sq_ready, 1)
    v.wait_ge(sq_ready, (seen - 1) * (NT + 1) + NT)
    me, mo = stats[:, :, 1], stats[:, :, 4]
    link(nc.vector.tensor_tensor(mv[:, 1, :], me, mo, ALU.add))
    link(nc.vector.tensor_tensor(mv[:, 2, :], me, mo, ALU.subtract))
    link(nc.vector.tensor_tensor(mv[:, 2, :], mv[:, 2, :], mv[:, 2, :], ALU.mult))
    link(nc.vector.tensor_tensor(mv[:, 0, :], stats[:, :, 2], stats[:, :, 5], ALU.add))
    link(nc.vector.tensor_scalar(mv[:, 0, :], mv[:, 0, :], 1.0 / D, EPS, ALU.mult, ALU.add))
    link(nc.vector.scalar_tensor_tensor(out=mv[:, 0, :], in0=mv[:, 2, :], scalar=0.25, in1=mv[:, 0, :],
                                        op0=ALU.mult, op1=ALU.add))
    nc.vector.memset(mv[:, 3, :], 0.0).then_inc(sq_ready, 1)
    v.wait_ge(sq_done, seen)
    link(nc.vector.reciprocal(mv[:, 0, :], mv[:, 3, :]))
    link(nc.vector.scalar_tensor_tensor(out=mv[:, 1, :], in0=mv[:, 1, :], scalar=-0.5, in1=mv[:, 0, :],
                                        op0=ALU.mult, op1=ALU.mult))


def layer_norm_root(nc, act, mv, sq_ready, sq_done, seen):
    act.wait_ge(sq_ready, seen * (NT + 1))
    nc.scalar.activation(mv[:, 3, :], mv[:, 0, :], ACT.Sqrt).then_inc(sq_done, 1)


def constants(nc, k, dram):
    st = Stage(nc, "const")
    built, link_v, loaded = st.sem("built"), st.sem("dve_step"), st.sem("loaded")
    casts = st.sem("casts")
    raw = st.sb("mask_raw", [P, NT, S], I32)
    lens = st.sb("lens_raw", [P, B], I32)
    lensf = st.sb("lens", [P, B])
    keys = st.sb("key_index", [P, S], I32)
    keysf = st.sb("key_index_f", [P, S])
    modi = st.sb("mod_i", [P, 1], I32)
    modf = st.sb("mod_f", [P, 1])
    expi = st.sb("expert_i", [P, NT, E], I32)
    thri = st.sb("threshold_i", [P, E, E], I32)
    tili = st.sb("tile_i", [P, RT, E], I32)
    with st.ctx, nc.Block() as block:
        @block.sync
        def _(sp):
            sp.dma_start(k.x[:, :, :], dram["x"].rearrange("(t p) d -> p t d", p=P)).then_inc(loaded, 16)
            sp.dma_start(k.attn_w[:, :, :], dram["attn_w"]).then_inc(loaded, 16)
            sp.dma_start(raw[:, :, :], dram["mask0"].rearrange("(t p) s -> p t s", p=P)).then_inc(loaded, 16)
            sp.dma_start(lens[:, :], dram["lens"].partition_broadcast(P)).then_inc(loaded, 16)
            sp.dma_start(k.attn_bcol[:, :], dram["attn_bcol"]).then_inc(loaded, 16)
            sp.dma_start(k.attn_brow[:, :, :], dram["attn_brow"]).then_inc(loaded, 16)
            sp.wait_ge(loaded, 6 * 16)

        @block.gpsimd
        def _(gp):
            link = Chain(gp, built)
            link(nc.gpsimd.memset(k.ident[:, :], 0.0))
            link(nc.gpsimd.affine_select(out=k.ident[:, :], in_=k.ident[:, :], compare_op=ALU.not_equal, fill=1.0,
                                         base=0, pattern=[[-1, P]], channel_multiplier=1))
            link(nc.gpsimd.memset(k.ones[:, :], 1.0))
            link(nc.gpsimd.memset(k.before[:, :], 0.0))
            link(nc.gpsimd.affine_select(out=k.before[:, :], in_=k.before[:, :], compare_op=ALU.is_ge, fill=1.0,
                                         base=0, pattern=[[-1, P]], channel_multiplier=1))
            link(nc.gpsimd.memset(k.earlier[:, :, :], 1.0))
            link(nc.gpsimd.affine_select(out=k.earlier[:, :, :], in_=k.earlier[:, :, :], compare_op=ALU.is_gt,
                                         fill=0.0, base=0, pattern=[[E, NT], [0, E]], channel_multiplier=-1))
            link(nc.gpsimd.memset(k.causal[:, :, :], 0.0))
            for qt in range(QT):
                link(nc.gpsimd.affine_select(out=k.causal[:, qt, :], in_=k.causal[:, qt, :], compare_op=ALU.is_ge,
                                             fill=MASKED, base=P * qt, pattern=[[-1, S]], channel_multiplier=1))
            link(nc.gpsimd.iota(keys[:, :], [[1, S]], base=0, channel_multiplier=0))
            link(nc.gpsimd.iota(modi[:, :], [[0, 1]], base=0, channel_multiplier=1))
            link(nc.gpsimd.iota(expi[:, :, :], [[0, NT], [1, E]], base=0, channel_multiplier=0))
            link(nc.gpsimd.iota(thri[:, :, :], [[0, E], [ST, E]], base=0, channel_multiplier=0))
            link(nc.gpsimd.iota(tili[:, :, :], [[1, RT], [0, E]], base=0, channel_multiplier=0))
            link(nc.gpsimd.memset(k.pad[:, 0:D], 0.0))
            link(nc.gpsimd.memset(k.pad[:, D:D + 1].bitcast(I32), NOWHERE))
            link(nc.gpsimd.memset(k.pad[:, D + 1:XW], 0.0))
            link(nc.gpsimd.iota(k.tmp_i[:, :], [[0, 1]], base=0, channel_multiplier=1))

        @block.vector
        def _(v):
            link = Chain(v, link_v)
            v.wait_ge(loaded, 6 * 16)
            v.wait_ge(built, 19)
            link(nc.vector.tensor_copy(k.ident16[:, :], k.ident[:, :]))
            link(nc.vector.tensor_scalar(k.mask0[:, :, :], raw[:, :, :], 0.0, MASKED, ALU.is_equal, ALU.mult))
            link(nc.vector.tensor_copy(lensf[:, :], lens[:, :]))
            link(nc.vector.tensor_copy(keysf[:, :], keys[:, :]))
            for b in range(B):
                link(nc.vector.tensor_scalar(k.mask2[:, b, :], keysf[:, :], lensf[:, b:b + 1], MASKED,
                                             ALU.is_ge, ALU.mult))
            link(nc.vector.tensor_scalar(modi[:, :], modi[:, :], E - 1, None, ALU.bitwise_and))
            link(nc.vector.tensor_copy(modf[:, :], modi[:, :]))
            link(nc.vector.tensor_copy(k.expert[:, :, :], expi[:, :, :]))
            link(nc.vector.tensor_scalar(k.same[:, :], k.expert[:, 0, :], modf[:, 0:1], None, ALU.is_equal))
            link(nc.vector.tensor_tensor(k.earlier[:, :, :], k.earlier[:, :, :],
                                         k.same[:, :].unsqueeze(1).to_broadcast([P, NT, E]), ALU.mult))
            link(nc.vector.tensor_scalar(k.expert[:, :, :], k.expert[:, :, :], -1.0, float(E), ALU.mult, ALU.add))
            link(nc.vector.tensor_copy(k.threshold[:, :, :], thri[:, :, :]))
            link(nc.vector.tensor_copy(k.tile_no[:, :, :], tili[:, :, :]))
            link(nc.vector.tensor_scalar(k.tmp_i[:, :], k.tmp_i[:, :], 4, 1, ALU.logical_shift_right, ALU.bitwise_and))
            link(nc.vector.tensor_copy(k.parity[:, 1:2], k.tmp_i[:, :]))
            link(nc.vector.tensor_scalar(k.parity[:, 0:1], k.parity[:, 1:2], -1.0, 1.0, ALU.mult, ALU.add))
    st.close()


def attention16(nc, k, dram, name, wq, wk, wv, wo, kv_self=False, norm=True, mask=None, bias=None, out_bias=None,
                add=True, src=None, dst=None, ffn=None):
    st = Stage(nc, name)
    sem = st.sem
    ln_step, sq_ready, sq_done = sem("ln_step"), sem("sq_ready"), sem("sq_done")
    ctx_loaded, xn_ready = [sem(f"ctx{i}_loaded") for i in range(2)], sem("xn_ready")
    xT_ready, xT_copied = sem("xT_ready"), sem("xT_copied")
    q_ready, q_copied = sem("q_ready"), sem("q_copied")
    k_ready, k_copied = sem("k_ready"), sem("k_copied")
    v_ready, v_copied = sem("v_ready"), sem("v_copied")
    s_ready, max_ready, negmax_ready = sem("scores_ready"), sem("max_ready"), sem("negmax_ready")
    p_ready = sem("probs_ready")
    pt_ready, pt_copied_v, pt_copied_a = sem("probsT_ready"), sem("probsT0_copied"), sem("probsT1_copied")
    pv_ready, o_copied = sem("pv_ready"), sem("o_copied")
    ot_ready, rs_ready, on_ready = sem("otok_ready"), sem("recip_ready"), sem("onorm_ready")
    ont_ready, ont_copied = sem("onormT_ready"), sem("onormT_copied")
    y_ready, y_added = sem("y_ready"), sem("y_added")
    pads, v_padded = sem("pads_written"), sem("v_padded")

    stats = st.sb("stats", [P, NT, 6])
    mv = st.sb("mv", [P, 4, NT])
    ctxT = [st.sb(f"ctxT{i}", [P, KC, S]) for i in range(2)]
    xn = [st.sb(f"xn{i}", [P, QT, D]) for i in range(2)]
    xT = st.sb("xT", [P, KC, S])
    qT = [st.sb(f"qT{i}", [P, 2, S]) for i in range(2)]
    kT = [[st.sb(f"kT{i}{j}", [P, 2, S]) for j in range(2)] for i in range(2)]
    vv = [st.sb(f"v{i}", [P, QT, H, HP]) for i in range(2)]
    probs = [st.sb(f"probs{i}", [P, HG, S]) for i in range(2)]
    probsT = [st.sb(f"probsT{i}", [P, QT, HG, P]) for i in range(2)]
    rowmax = [st.sb(f"max{i}", [P, HG]) for i in range(2)]
    negmax = [st.sb(f"negmax{i}", [P, HG]) for i in range(2)]
    osum = st.sb("o", [P, NG, P])
    recip = st.sb("recip", [P, H])
    onorm = st.sb("onorm", [P, H, DH])
    onormT = st.sb("onormT", [P, KC, P])
    pS = [st.pb(f"pS{i}", [P, HG, S]) for i in range(2)]
    pT = [st.pb(f"pT{i}", [P, HG, P]) for i in range(2)]
    pO = st.pb("pO", [P, NG, P])
    pM = st.pb("pM", [P, 512])
    pM2 = pM[:, :].rearrange("p (a n) -> p a n", a=2)

    SLOTS = QT * NG
    scale = DH ** -0.5
    W = k.attn_w

    def head(g, j):
        h = HG * g + j
        return h // 8, 32 * ((h % 8) // 2), h % 2

    with st.ctx, nc.Block() as block:
        @block.sync
        def _(sp):
            def load(b, par, waits):
                if waits:
                    sp.wait_ge(v_ready, b - 1)
                sp.dma_start(ctxT[par][:, :, :], dram["ctxT"][:, :, bass.ds(b * S, S)]).then_inc(ctx_loaded[par], 16)
            if not kv_self:
                load(0, 0, False)
                load(1, 1, False)
            if ffn is not None:
                rows = dram[ffn.name + "_xs"][ffn.shared and T:, :].rearrange("(n p) w -> p n w", p=P)
                n = rows.shape[1]
                sp.dma_start(rows, k.pad[:, :].unsqueeze(1).to_broadcast([P, n, XW])).then_inc(pads, 16)
                if ffn.name == "L2f":
                    rows = dram["L2f_yk"].rearrange("(n p) w -> p n w", p=P)
                    sp.dma_start(rows, k.pad[:, 0:D].unsqueeze(1).to_broadcast([P, TK * NT, D])).then_inc(pads, 16)
            if not kv_self:
                with sp.Fori(1, B // 2) as i:
                    load(2 * i, 0, True)
                    load(2 * i + 1, 1, True)
            if ffn is not None:
                sp.wait_ge(pads, 32 if ffn.name == "L2f" else 16)

        @block.tensor
        def _(pe):
            def project_x(b, par):
                pe.wait_ge(xn_ready, b + 1)
                for t in range(QT):
                    for c in range(KC):
                        last = nc.tensor.transpose(pM2[:, c, t * P:(t + 1) * P],
                                                   xn[par][:, t, c * P:(c + 1) * P], k.ident[:, :])
                last.then_inc(xT_ready, 1)

            def project_q(b, par):
                pe.wait_ge(xT_copied, b + 1)
                for f in range(2):
                    for c in range(KC):
                        last = nc.tensor.matmul(pM2[:, f, :], W[:, wq * KC + c, f * P:(f + 1) * P], xT[:, c, :],
                                                start=(c == 0), stop=(c == KC - 1))
                last.then_inc(q_ready, 1)

            def project_k(b, par):
                if not kv_self:
                    pe.wait_ge(ctx_loaded[par], nth(b, par))
                kv = xT if kv_self else ctxT[par]
                for f in range(2):
                    for c in range(KC):
                        last = nc.tensor.matmul(pM2[:, f, :], W[:, wk * KC + c, f * P:(f + 1) * P], kv[:, c, :],
                                                start=(c == 0), stop=(c == KC - 1))
                last.then_inc(k_ready, 1)

            def project_v(b, par):
                kv = xT if kv_self else ctxT[par]
                for t in range(QT):
                    for c in range(KC):
                        last = nc.tensor.matmul(pM2[:, t, :], kv[:, c, t * P:(t + 1) * P], W[:, wv * KC + c, :],
                                                start=(c == 0), stop=(c == KC - 1 and bias is None))
                    if bias is not None:
                        last = nc.tensor.matmul(pM2[:, t, :], k.ones[0:1, :], k.attn_brow[0:1, bias, :],
                                                start=False, stop=True)
                last.then_inc(v_ready, 1)

            def scores(s, b, par, sl):
                qt, g = divmod(sl, NG)
                if sl == 0:
                    pe.wait_ge(q_copied, b + 1)
                    pe.wait_ge(k_copied, 2 * (b + 1))
                if not (is_int(s) and s < 2):
                    pe.wait_ge(p_ready, HG * (s - 1))
                out = pS[sl % 2]
                m = {None: None, "pair": k.mask0, "batch": k.mask2, "causal": k.causal}[mask]
                if m is not None:
                    at = {"pair": b * QT + qt, "batch": b, "causal": qt}[mask]
                    for j in range(HG):
                        nc.tensor.matmul(out[:, j, :], k.ident16[:, :], m[:, bass.ds(at, 1), :],
                                         start=(j % 2 == 0), stop=False, skip_group_check=True)
                for j in range(HG):
                    f, r, odd = head(g, j)
                    last = nc.tensor.matmul(out[:, j, :], qT[par][r:r + 32, f, qt * P:(qt + 1) * P],
                                            kT[par][odd][r:r + 32, f, :],
                                            start=(m is None and j % 2 == 0), stop=True, skip_group_check=True)
                last.then_inc(s_ready, 1)

            def transpose_probs(s, sl):
                pe.wait_ge(p_ready, HG * (s + 1))
                for t in range(QT):
                    if not (is_int(s) and s == 0):
                        pe.wait_ge(pt_copied_v if t == 0 else pt_copied_a, s)
                    for j in range(HG):
                        last = nc.tensor.transpose(pT[t][:, j, :], probs[sl % 2][:, j, t * P:(t + 1) * P],
                                                   k.ident[:, :])
                    last.then_inc(pt_ready, 1)

            def weighted(s, u, sl, par):
                g = sl % NG
                pe.wait_ge(pt_copied_v, s + 1)
                pe.wait_ge(pt_copied_a, s + 1)
                if is_int(s) and s == 0:
                    pe.wait_ge(v_padded, 4)
                if g == 0 and not (is_int(u) and u == 0):
                    pe.wait_ge(o_copied, u)
                for t in range(QT):
                    for j in range(HG):
                        last = nc.tensor.matmul(pO[HP * j:HP * (j + 1), g, :], vv[par][:, t, HG * g + j, :],
                                                probsT[sl % 2][:, t, j, :], start=(g == 0 and t == 0),
                                                stop=(t == QT - 1), skip_group_check=True)
                if g == NG - 1:
                    last.then_inc(pv_ready, 1)

            def tokens_of_o(u):
                pe.wait_ge(o_copied, u + 1)
                for g in range(NG):
                    last = nc.tensor.transpose(pM[:, g * P:(g + 1) * P], osum[:, g, :], k.ident[:, :])
                last.then_inc(ot_ready, 1)

            def features_of_o(u):
                pe.wait_ge(on_ready, u + 1)
                for c in range(KC):
                    last = nc.tensor.transpose(pM[:, c * P:(c + 1) * P],
                                               onorm[:, 8 * c:8 * c + 8, :].rearrange("p h d -> p (h d)"),
                                               k.ident[:, :])
                last.then_inc(ont_ready, 1)

            def output(u):
                pe.wait_ge(ont_copied, u + 1)
                for c in range(KC):
                    last = nc.tensor.matmul(pM2[:, 0, :], onormT[:, c, :], W[:, wo * KC + c, :],
                                            start=(c == 0), stop=(c == KC - 1 and out_bias is None))
                if out_bias is not None:
                    last = nc.tensor.matmul(pM2[:, 0, :], k.ones[0:1, :], k.attn_brow[0:1, out_bias, :],
                                            start=False, stop=True)
                last.then_inc(y_ready, 1)

            def batch(b, par, first, last):
                for sl in range(SLOTS):
                    s = b * SLOTS + sl
                    u = b * QT
                    if not (last and sl == SLOTS - 1):
                        nb = b if sl < SLOTS - 1 else b + 1
                        scores(s + 1, nb, par if sl < SLOTS - 1 else 1 - par, (sl + 1) % SLOTS)
                    if sl == 0 and not last:
                        if first:
                            pe.wait_ge(v_copied, 1)
                        else:
                            pe.wait_ge(y_added, u - 1)
                        project_x(b + 1, 1 - par)
                    if sl == 1 and not first:
                        if last:
                            pe.wait_ge(y_added, u - 1)
                        else:
                            pe.wait_ge(xT_copied, b + 2)
                        tokens_of_o(u - 1)
                    if sl == 2 and not first:
                        features_of_o(u - 1)
                    if sl == 3 and not first:
                        if not last:
                            pe.wait_ge(q_copied, b + 2)
                        output(u - 1)
                    if sl == 4 and not last:
                        if first:
                            pe.wait_ge(q_copied, b + 2)
                        else:
                            pe.wait_ge(y_added, u)
                        project_k(b + 1, 1 - par)
                    if sl == 5:
                        if last:
                            pe.wait_ge(y_added, u)
                        else:
                            pe.wait_ge(k_copied, 2 * (b + 2))
                        tokens_of_o(u)
                    if sl == 6:
                        features_of_o(u)
                    if sl == 7:
                        if not last:
                            pe.wait_ge(v_copied, b + 2)
                        output(u)
                    if not (first and sl == 0):
                        weighted(s - 1, u + (sl - 1) // NG, (sl - 1) % SLOTS, par if sl else 1 - par)
                    if sl == 2 and not last:
                        if not first:
                            pe.wait_ge(ont_copied, u)
                        project_q(b + 1, 1 - par)
                    if sl == 6 and not last:
                        pe.wait_ge(ont_copied, u + 1)
                        project_v(b + 1, 1 - par)
                    transpose_probs(s, sl)

            project_x(0, 0)
            project_q(0, 0)
            pe.wait_ge(q_copied, 1)
            project_k(0, 0)
            pe.wait_ge(k_copied, 2)
            project_v(0, 0)
            scores(0, 0, 0, 0)
            batch(0, 0, True, False)
            batch(1, 1, False, False)
            with pe.Fori(1, B // 2 - 1) as i:
                batch(2 * i, 0, False, False)
                batch(2 * i + 1, 1, False, False)
            batch(B - 2, 0, False, False)
            batch(B - 1, 1, False, True)
            U = B * QT
            weighted(B * SLOTS - 1, U - 1, SLOTS - 1, 1)
            tokens_of_o(U - 1)
            features_of_o(U - 1)
            output(U - 1)

        @block.vector
        def _(v):
            if norm:
                layer_norm_stats(nc, v, Chain(v, ln_step), k.x, stats, mv, sq_ready, sq_done, 1)

            def normalise(b, par):
                if not (is_int(b) and b < 2):
                    v.wait_ge(xT_ready, b - 1)
                for t in range(QT):
                    at = bass.ds(b * QT + t, 1)
                    if norm:
                        ins = nc.vector.tensor_scalar(xn[par][:, t, :], k.x[:, at, :], mv[:, 0, at],
                                                      mv[:, 1, at], ALU.mult, ALU.add)
                    else:
                        ins = nc.vector.tensor_copy(xn[par][:, t, :], src[:, at, :])
                ins.then_inc(xn_ready, 1)

            def copy_xT(b, par):
                v.wait_ge(xT_ready, b + 1)
                nc.vector.tensor_copy(xT[:, :, :], pM2).then_inc(xT_copied, 1)

            def copy_k(b, par):
                v.wait_ge(k_ready, b + 1)
                for odd in range(2):
                    if bias is None:
                        nc.vector.tensor_scalar(kT[par][odd][:, :, :], pM2, k.parity[:, odd:odd + 1], None,
                                                ALU.mult).then_inc(k_copied, 1)
                    else:
                        for f in range(2):
                            at = 4 * bias + 2 + f
                            ins = nc.vector.tensor_scalar(kT[par][odd][:, f, :], pM2[:, f, :],
                                                          k.attn_bcol[:, at:at + 1], k.parity[:, odd:odd + 1],
                                                          ALU.add, ALU.mult)
                        ins.then_inc(k_copied, 1)

            def maxima(s, sl):
                v.wait_ge(s_ready, s + 1)
                nc.vector.tensor_reduce(rowmax[sl % 2][:, :], pS[sl % 2][:, :, :], AX.X, ALU.max)\
                  .then_inc(max_ready, 1)
                v.wait_ge(max_ready, s + 1)
                nc.vector.tensor_scalar(negmax[sl % 2][:, :], rowmax[sl % 2][:, :], -scale, None, ALU.mult)\
                  .then_inc(negmax_ready, 1)

            def copy_probsT(s, sl):
                v.wait_ge(pt_ready, 2 * s + 1)
                nc.vector.tensor_copy(probsT[sl % 2][:, 0, :, :], pT[0][:, :, :]).then_inc(pt_copied_v, 1)

            def normalise_o(u):
                v.wait_ge(ot_ready, u + 1)
                o = pM[:, :].rearrange("p (h d) -> p h d", d=HP)
                nc.vector.reciprocal(recip[:, :], o[:, :, DH]).then_inc(rs_ready, 1)
                v.wait_ge(rs_ready, u + 1)
                nc.vector.tensor_tensor(onorm[:, :, :], o[:, :, 0:DH],
                                        recip[:, :].unsqueeze(2).to_broadcast([P, H, DH]), ALU.mult)\
                  .then_inc(on_ready, 1)

            def take_output(u):
                v.wait_ge(y_ready, u + 1)
                at = bass.ds(u, 1)
                if add:
                    nc.vector.tensor_tensor(k.x[:, at, :], k.x[:, at, :], pM2[:, 0:1, :], ALU.add)\
                      .then_inc(y_added, 1)
                else:
                    nc.vector.tensor_copy(dst[:, at, :], pM2[:, 0:1, :]).then_inc(y_added, 1)

            def batch(b, par, first, last):
                for sl in range(SLOTS):
                    s = b * SLOTS + sl
                    u = b * QT
                    if not (last and sl == SLOTS - 1):
                        maxima(s + 1, (sl + 1) % SLOTS)
                    if sl == 0 and not last:
                        copy_xT(b + 1, 1 - par)
                    if sl == 1 and not first:
                        normalise_o(u - 1)
                    if sl == 3 and not first:
                        take_output(u - 1)
                    if sl == 4 and not last:
                        copy_k(b + 1, 1 - par)
                    if sl == 5:
                        normalise_o(u)
                    if sl == 7:
                        take_output(u)
                    copy_probsT(s, sl)
                    if sl == 3 and not last and not (is_int(b) and b == B - 2):
                        normalise(b + 2, par)

            normalise(0, 0)
            normalise(1, 1)
            for par in range(2):
                nc.vector.memset(vv[par][:, :, :, DH + 1:HP], 0.0).then_inc(v_padded, 1)
                nc.vector.memset(vv[par][:, :, :, DH:DH + 1], 1.0).then_inc(v_padded, 1)
            copy_xT(0, 0)
            copy_k(0, 0)
            maxima(0, 0)
            batch(0, 0, True, False)
            batch(1, 1, False, False)
            with v.Fori(1, B // 2 - 1) as i:
                batch(2 * i, 0, False, False)
                batch(2 * i + 1, 1, False, False)
            batch(B - 2, 0, False, False)
            batch(B - 1, 1, False, True)
            normalise_o(B * QT - 1)
            take_output(B * QT - 1)

        @block.scalar
        def _(act):
            if norm:
                layer_norm_root(nc, act, mv, sq_ready, sq_done, 1)

            def copy_q(b, par):
                act.wait_ge(q_ready, b + 1)
                if bias is None:
                    nc.scalar.copy(qT[par][:, :, :], pM2).then_inc(q_copied, 1)
                else:
                    for f in range(2):
                        at = 4 * bias + f
                        ins = nc.scalar.activation(qT[par][:, f, :], pM2[:, f, :], ACT.Identity,
                                                   bias=k.attn_bcol[:, at:at + 1])
                    ins.then_inc(q_copied, 1)

            def copy_v(b, par):
                act.wait_ge(v_ready, b + 1)
                nc.scalar.copy(vv[par][:, :, :, 0:DH].rearrange("p t h d -> p (t h) d"),
                               pM[:, :].rearrange("p (n d) -> p n d", d=DH)).then_inc(v_copied, 1)

            def probabilities(s, sl):
                act.wait_ge(negmax_ready, s + 1)
                if not (is_int(s) and s < 2):
                    act.wait_ge(pt_ready, 2 * (s - 1))
                for j in range(HG):
                    nc.scalar.activation(probs[sl % 2][:, j, :], pS[sl % 2][:, j, :], ACT.Exp,
                                         bias=negmax[sl % 2][:, j:j + 1], scale=scale).then_inc(p_ready, 1)

            def copy_probsT(s, sl):
                act.wait_ge(pt_ready, 2 * (s + 1))
                nc.scalar.copy(probsT[sl % 2][:, 1, :, :], pT[1][:, :, :]).then_inc(pt_copied_a, 1)

            def copy_o(u):
                act.wait_ge(pv_ready, u + 1)
                nc.scalar.copy(osum[:, :, :], pO[:, :, :]).then_inc(o_copied, 1)

            def copy_onormT(u):
                act.wait_ge(ont_ready, u + 1)
                nc.scalar.copy(onormT[:, :, :], pM2[:, 0, :].rearrange("p (c n) -> p c n", c=KC))\
                  .then_inc(ont_copied, 1)

            def batch(b, par, first, last):
                for sl in range(SLOTS):
                    s = b * SLOTS + sl
                    u = b * QT
                    if not (last and sl == SLOTS - 1):
                        probabilities(s + 1, (sl + 1) % SLOTS)
                    if sl == 0 and not first:
                        copy_o(u - 1)
                    if sl == 2:
                        if not first:
                            copy_onormT(u - 1)
                        if not last:
                            copy_q(b + 1, 1 - par)
                    if sl == 4:
                        copy_o(u)
                    if sl == 6:
                        copy_onormT(u)
                        if not last:
                            copy_v(b + 1, 1 - par)
                    copy_probsT(s, sl)

            copy_q(0, 0)
            copy_v(0, 0)
            probabilities(0, 0)
            batch(0, 0, True, False)
            batch(1, 1, False, False)
            with act.Fori(1, B // 2 - 1) as i:
                batch(2 * i, 0, False, False)
                batch(2 * i + 1, 1, False, False)
            batch(B - 2, 0, False, False)
            batch(B - 1, 1, False, True)
            copy_o(B * QT - 1)
            copy_onormT(B * QT - 1)
    st.close()


def attention1(nc, k, dram, name, wq, wk, wv):
    st = Stage(nc, name)
    sem = st.sem
    ln_step, sq_ready, sq_done = sem("ln_step"), sem("sq_ready"), sem("sq_done")
    ctx_loaded, mask_loaded = [sem(f"ctx{i}_loaded") for i in range(2)], [sem(f"mask{i}_loaded") for i in range(2)]
    xn_ready = sem("xn_ready")
    xT_ready, xT_copied = sem("xT_ready"), sem("xT_copied")
    q_ready, q_copied = sem("q_ready"), sem("q_copied")
    k_ready, k_copied = sem("k_ready"), sem("k_copied")
    v_ready, v_copied = sem("v_ready"), sem("v_copied")
    s_ready, s_masked, negmax_ready = sem("scores_ready"), sem("scores_masked"), sem("negmax_ready")
    p_ready, pt_ready, pt_copied = sem("probs_ready"), sem("probsT_ready"), sem("probsT_copied")
    o_ready, recip_ready, o_scaled, o_added = sem("o_ready"), sem("recip_ready"), sem("o_scaled"), sem("o_added")
    pads = sem("pads_written")

    stats = st.sb("stats", [P, NT, 6])
    mv = st.sb("mv", [P, 4, NT])
    ctxT = [st.sb(f"ctxT{i}", [P, KC, S]) for i in range(2)]
    bias = [st.sb(f"mask{i}", [P, QT, S]) for i in range(2)]
    xn = [st.sb(f"xn{i}", [P, QT, D]) for i in range(2)]
    xT = st.sb("xT", [P, KC, S])
    qT = [st.sb(f"qT{i}", [P, KC, S]) for i in range(2)]
    kT = [st.sb(f"kT{i}", [P, KC, S]) for i in range(2)]
    vv = [st.sb(f"v{i}", [P, QT, D]) for i in range(2)]
    sm = [st.sb(f"scores{i}", [P, S]) for i in range(QT)]
    probs = [st.sb(f"probs{i}", [P, S]) for i in range(QT)]
    probsT = [st.sb(f"probsT{i}", [P, QT, P]) for i in range(QT)]
    stat = [st.sb(f"stat{i}", [P, 4]) for i in range(QT)]
    oo = [st.sb(f"o{i}", [P, D]) for i in range(QT)]
    pS = [st.pb(f"pS{i}", [P, 512]) for i in range(QT)]
    pT = [st.pb(f"pT{i}", [P, 512]) for i in range(QT)]
    pO = [st.pb(f"pO{i}", [P, 512]) for i in range(QT)]
    pM = [st.pb(f"pM{i}", [P, 2, S]) for i in range(2)]
    W = k.attn_w
    scale = D ** -0.5
    ffn = FFNS[1]

    with st.ctx, nc.Block() as block:
        @block.sync
        def _(sp):
            def load(b, par, waits):
                if waits:
                    sp.wait_ge(s_masked, QT * (b - 1))
                sp.dma_start(ctxT[par][:, :, :], dram["ctxT"][:, :, bass.ds(b * S, S)]).then_inc(ctx_loaded[par], 16)
                sp.dma_start(bias[par][:, :, :], dram["mask1"][:, bass.ds(b * QT, QT), :]).then_inc(mask_loaded[par], 16)
            load(0, 0, False)
            load(1, 1, False)
            rows = dram[ffn.name + "_xs"][T:, :].rearrange("(n p) w -> p n w", p=P)
            sp.dma_start(rows, k.pad[:, :].unsqueeze(1).to_broadcast([P, rows.shape[1], XW])).then_inc(pads, 16)
            with sp.Fori(1, B // 2) as i:
                load(2 * i, 0, True)
                load(2 * i + 1, 1, True)
            sp.wait_ge(pads, 16)

        @block.tensor
        def _(pe):
            def project_x(b, par):
                pe.wait_ge(xn_ready, b + 1)
                if not (is_int(b) and b == 0):
                    pe.wait_ge(k_copied, b)
                for t in range(QT):
                    for c in range(KC):
                        last = nc.tensor.transpose(pM[0][:, c, t * P:(t + 1) * P],
                                                   xn[par][:, t, c * P:(c + 1) * P], k.ident[:, :])
                last.then_inc(xT_ready, 1)

            def project(out, w, src, ready):
                for f in range(KC):
                    for c in range(KC):
                        last = nc.tensor.matmul(out[:, f, :], W[:, w * KC + c, f * P:(f + 1) * P], src[:, c, :],
                                                start=(c == 0), stop=(c == KC - 1))
                last.then_inc(ready, 1)

            def project_q(b, par):
                pe.wait_ge(xT_copied, b + 1)
                if not (is_int(b) and b == 0):
                    pe.wait_ge(v_copied, b)
                project(pM[1], wq, xT, q_ready)

            def project_k(b, par):
                pe.wait_ge(ctx_loaded[par], nth(b, par))
                project(pM[0], wk, ctxT[par], k_ready)

            def project_v(b, par):
                pe.wait_ge(q_copied, b + 1)
                for t in range(QT):
                    for c in range(KC):
                        last = nc.tensor.matmul(pM[1][:, t, :], ctxT[par][:, c, t * P:(t + 1) * P],
                                                W[:, wv * KC + c, :], start=(c == 0), stop=(c == KC - 1))
                last.then_inc(v_ready, 1)

            def scores(b, par, qt):
                if not (is_int(b) and b == 0):
                    pe.wait_ge(s_masked, QT * b - 1 + qt)
                for c in range(KC):
                    last = nc.tensor.matmul(pS[qt][:, 0:S], qT[par][:, c, qt * P:(qt + 1) * P], kT[par][:, c, :],
                                            start=(c == 0), stop=(c == KC - 1))
                last.then_inc(s_ready, 1)

            def transpose_probs(b, qt):
                pe.wait_ge(p_ready, QT * b + qt + 1)
                for t in range(QT):
                    last = nc.tensor.transpose(pT[qt][:, t * P:(t + 1) * P], probs[qt][:, t * P:(t + 1) * P],
                                               k.ident[:, :])
                last.then_inc(pt_ready, 1)

            def weighted(b, par, qt):
                pe.wait_ge(pt_copied, QT * b + qt + 1)
                if not (is_int(b) and b == 0):
                    pe.wait_ge(o_scaled, QT * b - 1 + qt)
                for t in range(QT):
                    last = nc.tensor.matmul(pO[qt][:, 0:D], probsT[qt][:, t, :], vv[par][:, t, :],
                                            start=(t == 0), stop=(t == QT - 1))
                last.then_inc(o_ready, 1)

            def batch(b, par, last):
                pe.wait_ge(q_copied, b + 1)
                pe.wait_ge(k_copied, b + 1)
                scores(b, par, 0)
                scores(b, par, 1)
                if not last:
                    project_x(b + 1, 1 - par)
                transpose_probs(b, 0)
                if not last:
                    project_q(b + 1, 1 - par)
                transpose_probs(b, 1)
                if not last:
                    project_k(b + 1, 1 - par)
                pe.wait_ge(v_copied, b + 1)
                weighted(b, par, 0)
                if not last:
                    project_v(b + 1, 1 - par)
                weighted(b, par, 1)

            project_x(0, 0)
            project_q(0, 0)
            project_k(0, 0)
            project_v(0, 0)
            batch(0, 0, False)
            with pe.Fori(0, B // 2 - 1) as i:
                batch(2 * i + 1, 1, False)
                batch(2 * i + 2, 0, False)
            batch(B - 1, 1, True)

        @block.vector
        def _(v):
            layer_norm_stats(nc, v, Chain(v, ln_step), k.x, stats, mv, sq_ready, sq_done, 1)

            def normalise(b, par):
                if not (is_int(b) and b < 2):
                    v.wait_ge(xT_ready, b - 1)
                for t in range(QT):
                    at = bass.ds(b * QT + t, 1)
                    ins = nc.vector.tensor_scalar(xn[par][:, t, :], k.x[:, at, :], mv[:, 0, at], mv[:, 1, at],
                                                  ALU.mult, ALU.add)
                ins.then_inc(xn_ready, 1)

            def copy_xT(b):
                v.wait_ge(xT_ready, b + 1)
                nc.vector.tensor_copy(xT[:, :, :], pM[0][:, :, :]).then_inc(xT_copied, 1)

            def copy_k(b, par):
                v.wait_ge(k_ready, b + 1)
                nc.vector.tensor_copy(kT[par][:, :, :], pM[0][:, :, :]).then_inc(k_copied, 1)

            def mask_and_max(b, par, qt):
                n = QT * b + qt + 1
                v.wait_ge(mask_loaded[par], nth(b, par))
                v.wait_ge(s_ready, n)
                nc.vector.scalar_tensor_tensor(out=sm[qt][:, :], in0=pS[qt][:, 0:S], scalar=scale,
                                               in1=bias[par][:, qt, :], op0=ALU.mult, op1=ALU.add)\
                  .then_inc(s_masked, 1)
                v.wait_ge(s_masked, n)
                nc.vector.tensor_reduce(stat[qt][:, 0:1], sm[qt][:, :], AX.X, ALU.max).then_inc(negmax_ready, 1)
                v.wait_ge(negmax_ready, 2 * n - 1)
                nc.vector.tensor_scalar(stat[qt][:, 1:2], stat[qt][:, 0:1], -1.0, None, ALU.mult)\
                  .then_inc(negmax_ready, 1)

            def take_output(b, qt):
                n = QT * b + qt + 1
                v.wait_ge(o_ready, n)
                nc.vector.reciprocal(stat[qt][:, 3:4], stat[qt][:, 2:3]).then_inc(recip_ready, 1)
                v.wait_ge(recip_ready, n)
                at = bass.ds(b * QT + qt, 1)
                nc.vector.scalar_tensor_tensor(out=k.x[:, at, :], in0=pO[qt][:, 0:D].unsqueeze(1),
                                               scalar=stat[qt][:, 3:4], in1=k.x[:, at, :],
                                               op0=ALU.mult, op1=ALU.add).then_inc(o_scaled, 1)

            def batch(b, par, last):
                mask_and_max(b, par, 0)
                mask_and_max(b, par, 1)
                if not last:
                    copy_xT(b + 1)
                    copy_k(b + 1, 1 - par)
                    if not (is_int(b) and b == B - 2):
                        normalise(b + 2, par)
                take_output(b, 0)
                take_output(b, 1)

            normalise(0, 0)
            normalise(1, 1)
            copy_xT(0)
            copy_k(0, 0)
            batch(0, 0, False)
            with v.Fori(0, B // 2 - 2) as i:
                batch(2 * i + 1, 1, False)
                batch(2 * i + 2, 0, False)
            batch(B - 3, 1, False)
            batch(B - 2, 0, False)
            batch(B - 1, 1, True)

        @block.scalar
        def _(act):
            layer_norm_root(nc, act, mv, sq_ready, sq_done, 1)

            def copy_q(b, par):
                act.wait_ge(q_ready, b + 1)
                nc.scalar.copy(qT[par][:, :, :], pM[1][:, :, :]).then_inc(q_copied, 1)

            def copy_v(b, par):
                act.wait_ge(v_ready, b + 1)
                nc.scalar.copy(vv[par][:, :, :], pM[1][:, :, :]).then_inc(v_copied, 1)

            def probabilities(b, qt):
                act.wait_ge(negmax_ready, 2 * (QT * b + qt + 1))
                if not (is_int(b) and b == 0):
                    act.wait_ge(o_scaled, QT * b - 1 + qt)
                nc.scalar.activation(probs[qt][:, :], sm[qt][:, :], ACT.Exp, bias=stat[qt][:, 1:2],
                                     accum_out=stat[qt][:, 2:3]).then_inc(p_ready, 1)

            def copy_probsT(b, qt):
                act.wait_ge(pt_ready, QT * b + qt + 1)
                nc.scalar.copy(probsT[qt][:, :, :], pT[qt][:, 0:S].rearrange("p (t n) -> p t n", t=QT))\
                  .then_inc(pt_copied, 1)

            def batch(b, par, last):
                probabilities(b, 0)
                probabilities(b, 1)
                copy_probsT(b, 0)
                if not last:
                    copy_q(b + 1, 1 - par)
                copy_probsT(b, 1)
                if not last:
                    copy_v(b + 1, 1 - par)

            copy_q(0, 0)
            copy_v(0, 0)
            batch(0, 0, False)
            with act.Fori(0, B // 2 - 1) as i:
                batch(2 * i + 1, 1, False)
                batch(2 * i + 2, 0, False)
            batch(B - 1, 1, True)
    st.close()


def feed_forward(nc, k, dram, f):
    L1, L2, L3 = f.name == "L1f", f.name == "L2f", f.name == "L3f"
    st = Stage(nc, f.name)
    sem = st.sem
    sq_ready, sq_done, dve_step = sem("sq_ready"), sem("sq_done"), sem("dve_step")
    small_loaded, xn_ready, rows_written = sem("small_loaded"), sem("xn_ready"), sem("shared_rows_written")
    xt_ready, xt_copied, logits_ready = sem("router_xT_ready"), sem("router_xT_copied"), sem("logits_ready")
    exp_in, exp_out = sem("exp_input_ready"), sem("exp_done")
    chosen, counted, counted_c = sem("experts_chosen"), sem("counts_ready"), sem("counts_copied")
    ranked, placed, dispatched = sem("ranks_ready"), sem("slots_placed"), sem("rows_dispatched")
    second = sem("second_copy")
    second_norm = sem("second_norm")
    x_loaded, w_loaded = [sem(f"x_tile{i}_loaded") for i in range(2)], [sem(f"weights{i}_loaded") for i in range(2)]
    b2_loaded = [sem(f"b2_{i}_loaded") for i in range(2)]
    tT_ready, tT_copied, meta_copied = sem("tileT_ready"), sem("tileT_copied"), sem("meta_copied")
    up_ready, act_done, h_ready = sem("up_ready"), sem("activated"), sem("hidden_ready")
    y_ready, y_copied, y_sent = sem("y_ready"), sem("y_copied"), [sem(f"y{i}_sent") for i in range(2)]
    back_loaded, back_added = [sem(f"back{i}_loaded") for i in range(2)], sem("back_added")

    stats = st.sb("stats", [P, NT, 6])
    mv = st.sb("mv", [P, 4, NT])
    rows = st.sb("rows", [P, TK, NT, XW])
    wr = st.sb("router", [P, KC, E])
    rb = st.sb("router_b", [P, E])
    gb = st.sb("gamma_beta", [P, 2, D]) if L2 else None
    xrT = [st.sb(f"router_xT{i}", [P, KC, P]) for i in range(2)]
    lg = st.sb("logits", [P, NT, E])
    sc = st.sb("score", [P, NT, E])
    one = [st.sb(f"choice{i}", [P, NT, E]) for i in range(TK)]
    ex = st.sb("exp", [P, NT, E])
    tot = st.sb("totals", [P, P])
    r16 = [st.sb(f"row{i}", [P, NT]) for i in range(8)]
    r8 = [st.sb(f"seg{i}", [P, E]) for i in range(6)]
    big8 = st.sb("seg_cmp", [P, E, E])
    bigt = st.sb("tile_cmp", [P, RT, E])
    tef = st.sb("tile_expert_f", [P, RT])
    te = st.sb("tile_expert", [P, RT], I32)
    pos = st.sb("slot", [P, TK, NT], I32)
    xin = [st.sb(f"x_tile{i}", [P, 2, XW]) for i in range(2)]
    meta = [st.sb(f"meta{i}", [P, 2, 2]) for i in range(2)]
    tT = [st.sb(f"tileT{i}", [P, KC, ST]) for i in range(2)]
    wt = [st.sb(f"weights{i}", [P, f.cols]) for i in range(2)]
    b2 = [st.sb(f"b2_{i}", [1, D]) for i in range(2)] if L1 else None
    hid = [st.sb(f"hidden{i}", [P, f.blocks, ST]) for i in range(2)]
    gate = [st.sb(f"gate{i}", [P, ST]) for i in range(2)] if f.gated else None
    yy = [st.sb(f"y{i}", [P, 2, D]) for i in range(2)]

    pU = [st.pb(f"pU{i}", [P, 2, ST]) for i in range(f.banks)]
    pX = st.pb("pX", [P, KC, ST])
    pY = [st.pb(f"pY{i}", [P, 2, D]) for i in range(2)]
    pR = st.pb("pR", [P, 512])

    G, NB = f.groups, f.banks
    J, JS = f.tiles, f.shared * XT
    shared_rows = f.shared and T
    xs = dram[f.name + "_xs"]
    yk = dram[f.name + "_yk"]
    wd = dram[f.name + "_w"]
    bc16 = lambda a: a.unsqueeze(2).to_broadcast([P, NT, E])
    bc8 = lambda a: a.unsqueeze(1).to_broadcast([P, NT, E])

    def back(par, c):
        return (yy if c == 0 else tT)[par][:, :, :]

    with st.ctx, nc.Block() as block:
        @block.sync
        def _(sp):
            sp.dma_start(wr[:, :, :], dram[f.name + "_router"]).then_inc(small_loaded, 16)
            n = 1
            if L1 or L3:
                sp.dma_start(rb[:, :], dram[f.name + "_rb"].partition_broadcast(P)).then_inc(small_loaded, 16)
            if L2:
                sp.dma_start(gb[:, :, :], dram["L2f_gb"].partition_broadcast(P)).then_inc(small_loaded, 16)

            def load_weights(j, par, expert):
                if not (is_int(j) and j < 2):
                    sp.wait_ge(y_ready, j - 1)
                sp.dma_start(wt[par][:, :], wd[bass.ds(expert, 1), :, :].rearrange("a p n -> (a p) n"))\
                  .then_inc(w_loaded[par], 16)
                if L1:
                    sp.dma_start(b2[par][:, :], dram["L1f_b2"][bass.ds(expert, 1), :]).then_inc(b2_loaded[par], 16)

            def load_tile(j, par, row, routed):
                if not (is_int(j) and j < 2):
                    sp.wait_ge(tT_copied, j - 1)
                w = XW if routed else D
                sp.dma_start(xin[par][:, :, 0:w], xs[bass.ds(row, ST), 0:w].rearrange("(t p) w -> p t w", p=P))\
                  .then_inc(x_loaded[par], 16)

            if f.shared:
                load_weights(0, 0, E)
                load_weights(1, 1, E)
                sp.wait_ge(xn_ready, NT)
                sp.dma_start(xs[0:T, 0:D].rearrange("(t p) w -> p t w", p=P), rows[:, 0, :, 0:D])\
                  .then_inc(rows_written, 16)
                sp.wait_ge(rows_written, 16)
                for par in range(2):
                    load_tile(par, par, par * ST, False)
                for n in range(f.shared):
                    with sp.Fori(0 if n else 1, XT // 2) as i:
                        for par in range(2):
                            load_weights(n * XT + 2 * i + par, par, E + n)
                            load_tile(n * XT + 2 * i + par, par, (2 * i + par) * ST, False)
            sp.wait_ge(placed, 2)
            sp.wait_ge(dispatched, 16 * TK * NT)

            def routed_pair(i):
                for par in range(2):
                    expert = sp.value_load(te[0:1, bass.ds(2 * i + par, 1)], min_val=0, max_val=E - 1)
                    load_weights(JS + 2 * i + par, par, expert)
                    load_tile(JS + 2 * i + par, par, shared_rows + (2 * i + par) * ST, True)
            routed_pair(0)
            with sp.Fori(1, RT // 2) as i:
                routed_pair(i)
            for par in range(2):
                sp.wait_ge(y_sent[par], 16 * RT)

            def load_back(n, par):
                for c in range(TK):
                    sp.dma_start(back(par, c), yk[bass.ds(c * T + n * ST, ST), :]
                                 .rearrange("(t p) w -> p t w", p=P)).then_inc(back_loaded[par], 16)
            load_back(0, 0)
            load_back(1, 1)
            with sp.Fori(1, XT // 2) as i:
                for par in range(2):
                    sp.wait_ge(back_added, 2 * (2 * i + par - 1))
                    load_back(2 * i + par, par)

        @block.gpsimd
        def _(gp):
            gp.iota(rows[:, :, :, D:D + 1].bitcast(I32), [[T, TK], [P, NT], [1, 1]], base=0, channel_multiplier=1)\
              .then_inc(second, 1)
            for q in range(4):
                gp.wait_ge(xn_ready, 4 * (q + 1))
                gp.tensor_copy(rows[:, 1, 4 * q:4 * q + 4, 0:D], rows[:, 0, 4 * q:4 * q + 4, 0:D]).then_inc(second, 1)
            last_slot, rows_out = gp.to_reg(shared_rows + RT * ST - 1), gp.to_reg(TK * T)
            bound = gp.alloc_register(f.name + "_row_bound")
            gp.wait_ge(second, 5)
            gp.wait_ge(placed, 1)
            for c in range(TK):
                for t in range(NT):
                    gp.indirect_dma_start(xs[:, :], bass.IndirectOffsetOnAxis(ap=pos[:, c, t:t + 1], axis=0),
                                          rows[:, c, t, :], None, bounds_check=last_slot,
                                          oob_is_err=False).then_inc(dispatched, 16)

            def send(j, par):
                gp.wait_ge(y_copied, 2 * (j + 1))
                gp.reg_add(bound, rows_out, -1)
                for t in range(2):
                    gp.indirect_dma_start(yk[:, :], bass.IndirectOffsetOnAxis(
                        ap=meta[par][:, t, 0:1].bitcast(I32), axis=0), yy[par][:, t, :], None,
                        bounds_check=bound, oob_is_err=False).then_inc(y_sent[par], 16)
            with gp.Fori(JS // 2, J // 2) as i:
                send(2 * i, 0)
                send(2 * i + 1, 1)
            gp.free_register(bound)

        @block.tensor
        def _(pe):
            pe.wait_ge(small_loaded, 16 * (1 + (L1 or L3) + L2))
            for t in range(NT + 1):
                if t < NT:
                    pe.wait_ge(xn_ready, t + 1)
                    if t >= 2:
                        pe.wait_ge(xt_copied, t - 1)
                    for c in range(KC):
                        last = nc.tensor.transpose(pU[t % 2][:, 0, c * P:(c + 1) * P],
                                                   rows[:, 0, t, c * P:(c + 1) * P], k.ident[:, :])
                    last.then_inc(xt_ready, 1)
                if t == 0:
                    continue
                pe.wait_ge(xt_copied, t)
                for c in range(KC):
                    last = nc.tensor.matmul(pR[:, E * (t - 1):E * t], xrT[(t - 1) % 2][:, c, :], wr[:, c, :],
                                            start=(c == 0), stop=(c == KC - 1), skip_group_check=True)
            last.then_inc(logits_ready, 1)
            pe.wait_ge(chosen, 1)
            nc.tensor.matmul(pR[:, 0:P], sc[:, :, :].rearrange("p t e -> p (t e)"), k.ones[:, :],
                             start=True, stop=True).then_inc(counted, 1)
            pe.wait_ge(counted_c, 1)
            nc.tensor.matmul(pR[:, 0:P], k.before[:, :], sc[:, :, :].rearrange("p t e -> p (t e)"),
                             start=True, stop=False, skip_group_check=True)
            nc.tensor.matmul(pR[:, 0:P], tot[:, :], k.earlier[:, :, :].rearrange("p t e -> p (t e)"),
                             start=False, stop=True, skip_group_check=True)
            nc.tensor.matmul(pR[:, P:P + E], tot[:, :], k.same[:, :], start=False, stop=True,
                             skip_group_check=True).then_inc(ranked, 1)

            def transpose_tile(j, par):
                pe.wait_ge(x_loaded[par], nth(j, par))
                if not (is_int(j) and j == 0):
                    pe.wait_ge(tT_copied, j)
                for t in range(2):
                    for c in range(KC):
                        last = nc.tensor.transpose(pX[:, c, t * P:(t + 1) * P], xin[par][:, t, c * P:(c + 1) * P],
                                                   k.ident[:, :])
                last.then_inc(tT_ready, 1)

            def up(j, par):
                pe.wait_ge(tT_copied, j + 1)
                pe.wait_ge(w_loaded[par], nth(j, par))
                for g in range(G):
                    if not (is_int(j) and j * G + g < NB):
                        pe.wait_ge(h_ready, (1 if f.gated else 2) * (j * G + g - NB + 1))
                    bank = pU[(par * G + g) % NB]
                    for half in range(2):
                        m, blk = (half, g) if f.gated else (0, 2 * g + half)
                        for c in range(KC):
                            at = ((m * KC + c) * f.blocks + blk) * P
                            last = nc.tensor.matmul(bank[:, half, :], wt[par][:, at:at + P], tT[par][:, c, :],
                                                    start=(c == 0), stop=(c == KC - 1))
                    last.then_inc(up_ready, 1)

            def down(j, par):
                if not (is_int(j) and j < 2):
                    pe.wait_ge(y_copied, 2 * (j - 1))
                for t in range(2):
                    for blk in range(f.blocks):
                        if t == 0 and (f.gated or blk % 2 == 0):
                            n = blk if f.gated else blk // 2
                            pe.wait_ge(h_ready, (1 if f.gated else 2) * (j * G + n + 1))
                        last = nc.tensor.matmul(pY[par][:, t, :], hid[par][:, blk, t * P:(t + 1) * P],
                                                wt[par][:, f.up + blk * D:f.up + (blk + 1) * D],
                                                start=(blk == 0), stop=(blk == f.blocks - 1 and not L1))
                    if L1:
                        pe.wait_ge(b2_loaded[par], nth(j, par))
                        last = nc.tensor.matmul(pY[par][:, t, :], k.ones[0:1, :], b2[par][0:1, :],
                                                start=False, stop=True)
                last.then_inc(y_ready, 1)

            def pair(i, last):
                for par in range(2):
                    j = 2 * i + par
                    up(j, par)
                    if not (last and par):
                        transpose_tile(j + 1, 1 - par)
                    down(j, par)

            transpose_tile(0, 0)
            pair(0, False)
            with pe.Fori(1, J // 2 - 1) as i:
                pair(i, False)
            pair(J // 2 - 1, True)

        @block.vector
        def _(v):
            link = Chain(v, dve_step)
            layer_norm_stats(nc, v, link, k.x, stats, mv, sq_ready, sq_done, 1)

            def normalise(src, done):
                with v.Fori(0, NT) as t:
                    at = bass.ds(t, 1)
                    nc.vector.tensor_scalar(rows[:, 0, at, 0:D], src[:, at, 0:D], mv[:, 0, at], mv[:, 1, at],
                                            ALU.mult, ALU.add).then_inc(done, 1)
            if L2:
                normalise(k.x, second_norm)
                v.wait_ge(second_norm, NT)
                layer_norm_stats(nc, v, link, rows[:, 0, :, :], stats, mv, sq_ready, sq_done, 2)
                normalise(rows[:, 0, :, :], second_norm)
                v.wait_ge(second_norm, 2 * NT)
                v.wait_ge(small_loaded, 32)
                for half in range(2):
                    at = rows[:, 0, 8 * half:8 * half + 8, 0:D]
                    link(nc.vector.tensor_tensor(at, at, gb[:, 0:1, :].to_broadcast([P, 8, D]), ALU.mult))
                    nc.vector.tensor_tensor(at, at, gb[:, 1:2, :].to_broadcast([P, 8, D]), ALU.add)\
                      .then_inc(xn_ready, 8)
            else:
                normalise(k.x, xn_ready)

            v.wait_ge(logits_ready, 1)
            pr = pR[:, 0:P].rearrange("p (t e) -> p t e", e=E)
            if L1 or L3:
                link(nc.vector.tensor_tensor(lg[:, :, :], pr, bc8(rb[:, :]), ALU.add))
            elif L2:
                link(nc.vector.tensor_scalar(lg[:, :, :], pr, 10000.0, -10000.0, ALU.min, ALU.max))
            else:
                link(nc.vector.tensor_copy(lg[:, :, :], pr))
            m, val, e1, e2, z = r16[0], r16[1], r16[2], r16[3], r16[4]
            link(nc.vector.tensor_reduce(m[:, :], lg[:, :, :], AX.X, ALU.max))
            nc.vector.tensor_tensor(ex[:, :, :], lg[:, :, :], bc16(m[:, :]), ALU.subtract).then_inc(exp_in, 1)

            def choose(c):
                link(nc.vector.tensor_tensor(sc[:, :, :], lg[:, :, :], bc16(m[:, :]), ALU.is_equal))
                link(nc.vector.tensor_tensor(sc[:, :, :], sc[:, :, :], k.expert[:, :, :], ALU.mult))
                link(nc.vector.tensor_reduce(val[:, :], sc[:, :, :], AX.X, ALU.max))
                link(nc.vector.tensor_tensor(one[c][:, :, :], sc[:, :, :], bc16(val[:, :]), ALU.is_equal))
            choose(0)
            link(nc.vector.scalar_tensor_tensor(out=lg[:, :, :], in0=one[0][:, :, :], scalar=-1e30, in1=lg[:, :, :],
                                                op0=ALU.mult, op1=ALU.add))
            link(nc.vector.tensor_reduce(m[:, :], lg[:, :, :], AX.X, ALU.max))
            choose(1)
            nc.vector.tensor_tensor(sc[:, :, :], one[0][:, :, :], one[1][:, :, :], ALU.add).then_inc(chosen, 1)
            v.wait_ge(exp_out, 1)
            for c, out in ((0, e1), (1, e2)):
                link(nc.vector.tensor_tensor(lg[:, :, :], ex[:, :, :], one[c][:, :, :], ALU.mult))
                link(nc.vector.tensor_reduce(out[:, :], lg[:, :, :], AX.X, ALU.add))
            if not L3:
                link(nc.vector.tensor_reduce(z[:, :], ex[:, :, :], AX.X, ALU.add))
                if L2:
                    link(nc.vector.tensor_scalar(z[:, :], z[:, :], 1e-12, None, ALU.add))
                link(nc.vector.reciprocal(z[:, :], z[:, :]))
                for out in (e1, e2):
                    link(nc.vector.tensor_tensor(out[:, :], out[:, :], z[:, :], ALU.mult))
            if not L2:
                link(nc.vector.tensor_tensor(z[:, :], e1[:, :], e2[:, :], ALU.add))
                if f.name == "L0f":
                    link(nc.vector.tensor_scalar(z[:, :], z[:, :], 1e-20, None, ALU.add))
                link(nc.vector.reciprocal(z[:, :], z[:, :]))
                for out in (e1, e2):
                    link(nc.vector.tensor_tensor(out[:, :], out[:, :], z[:, :], ALU.mult))
            v.wait_ge(counted, 1)
            nc.vector.tensor_copy(tot[:, :], pR[:, 0:P]).then_inc(counted_c, 1)
            v.wait_ge(ranked, 1)
            count, tiles, end, start, ones8 = r8[0], r8[1], r8[2], r8[3], r8[4]
            link(nc.vector.tensor_scalar(count[:, :], pR[:, P:P + E], float(CAP if L2 else T), None, ALU.min))
            link(nc.vector.tensor_tensor(big8[:, :, :], count[:, :].unsqueeze(2).to_broadcast([P, E, E]),
                                         k.threshold[:, :, :], ALU.is_gt))
            link(nc.vector.tensor_reduce(tiles[:, :], big8[:, :, :], AX.X, ALU.add))
            link(nc.vector.memset(ones8[:, :], 1.0))
            link(nc.vector.tensor_tensor_scan(end[:, :], ones8[:, :], tiles[:, :], 0.0, ALU.mult, ALU.add))
            link(nc.vector.tensor_tensor(start[:, :], end[:, :], tiles[:, :], ALU.subtract))
            link(nc.vector.tensor_scalar(start[:, :], start[:, :], float(ST), float(shared_rows), ALU.mult, ALU.add))
            for c in range(TK):
                rk, seg, w = r16[5], r16[6], (e1, e2)[c]
                link(nc.vector.tensor_tensor(lg[:, :, :], pr, one[c][:, :, :], ALU.mult))
                link(nc.vector.tensor_reduce(rk[:, :], lg[:, :, :], AX.X, ALU.add))
                link(nc.vector.tensor_tensor(lg[:, :, :], one[c][:, :, :], bc8(start[:, :]), ALU.mult))
                link(nc.vector.tensor_reduce(seg[:, :], lg[:, :, :], AX.X, ALU.add))
                link(nc.vector.tensor_tensor(seg[:, :], seg[:, :], rk[:, :], ALU.add))
                if L2:
                    link(nc.vector.tensor_scalar(rk[:, :], rk[:, :], float(CAP), float(NOWHERE), ALU.is_ge, ALU.mult))
                    link(nc.vector.tensor_tensor(seg[:, :], seg[:, :], rk[:, :], ALU.add))
                link(nc.vector.tensor_copy(pos[:, c, :], seg[:, :]))
                ins = nc.vector.tensor_copy(rows[:, c, :, D + 1], w[:, :])
                if c == 0:
                    link(ins)
            ins.then_inc(placed, 1)
            link(nc.vector.tensor_tensor(bigt[:, :, :], end[:, :].unsqueeze(1).to_broadcast([P, RT, E]),
                                         k.tile_no[:, :, :], ALU.is_le))
            link(nc.vector.tensor_reduce(tef[:, :], bigt[:, :, :], AX.X, ALU.add))
            link(nc.vector.tensor_scalar(tef[:, :], tef[:, :], float(E - 1), None, ALU.min))
            nc.vector.tensor_copy(te[:, :], tef[:, :]).then_inc(placed, 1)

            def copy_tile(j, par, routed, reused):
                v.wait_ge(x_loaded[par], nth(j, par))
                if routed:
                    if reused:
                        v.wait_ge(y_sent[par], nth2(j - JS, par))
                    nc.vector.tensor_copy(meta[par][:, :, :], xin[par][:, :, D:XW]).then_inc(meta_copied, 1)
                v.wait_ge(tT_ready, j + 1)
                nc.vector.tensor_copy(tT[par][:, :, :], pX[:, :, :]).then_inc(tT_copied, 1)

            def gates_times(j, par):
                for g in range(G):
                    v.wait_ge(act_done, j * G + g + 1)
                    nc.vector.tensor_tensor(hid[par][:, g, :], gate[(par * G + g) % 2][:, :],
                                            pU[(par * G + g) % NB][:, 1, :], ALU.mult).then_inc(h_ready, 1)

            def take(j, par, n, routed):
                v.wait_ge(y_ready, j + 1)
                if routed:
                    v.wait_ge(meta_copied, j - JS + 1)
                for t in range(2):
                    if routed:
                        ins = nc.vector.tensor_scalar(yy[par][:, t, :], pY[par][:, t, :], meta[par][:, t, 1:2], None,
                                                      ALU.mult)
                    else:
                        at = bass.ds(2 * n + t, 1)
                        ins = nc.vector.tensor_tensor(k.x[:, at, :], k.x[:, at, :], pY[par][:, t:t + 1, :], ALU.add)
                    ins.then_inc(y_copied, 1)

            def pair(j0, n0, routed, next_routed, first=False, last=False):
                for par in range(2):
                    if f.gated:
                        gates_times(j0 + par, par)
                    if not (last and par):
                        copy_tile(j0 + par + 1, 1 - par, next_routed if par else routed,
                                  routed and not (first and par == 0))
                    take(j0 + par, par, n0 + par, routed)

            copy_tile(0, 0, not f.shared, False)
            for n in range(f.shared):
                with v.Fori(0, XT // 2 - 1) as i:
                    pair(n * XT + 2 * i, 2 * i, False, False)
                pair((n + 1) * XT - 2, XT - 2, False, n == f.shared - 1)
            pair(JS, 0, True, True, first=True)
            with v.Fori(1, RT // 2 - 1) as i:
                pair(JS + 2 * i, 2 * i, True, True)
            pair(J - 2, RT - 2, True, True, last=True)

            with v.Fori(0, XT // 2) as i:
                for par in range(2):
                    v.wait_ge(back_loaded[par], 32 * (i + 1))
                    at = bass.ds(4 * i + 2 * par, 2)
                    for c in range(TK):
                        if c or par:
                            v.wait_ge(back_added, 4 * i + 2 * par + c)
                        nc.vector.tensor_tensor(k.x[:, at, :], k.x[:, at, :], back(par, c), ALU.add)\
                          .then_inc(back_added, 1)

        @block.scalar
        def _(act):
            layer_norm_root(nc, act, mv, sq_ready, sq_done, 1)
            if L2:
                layer_norm_root(nc, act, mv, sq_ready, sq_done, 2)
            for t in range(NT):
                act.wait_ge(xt_ready, t + 1)
                nc.scalar.copy(xrT[t % 2][:, :, :], pU[t % 2][:, 0, :].rearrange("p (c n) -> p c n", c=KC))\
                  .then_inc(xt_copied, 1)
            act.wait_ge(exp_in, 1)
            nc.scalar.activation(ex[:, :, :], ex[:, :, :], ACT.Exp).then_inc(exp_out, 1)

            def activate(j, par):
                for g in range(G):
                    n = j * G + g
                    act.wait_ge(up_ready, n + 1)
                    bank = pU[(par * G + g) % NB]
                    if f.gated:
                        if not (is_int(n) and n < 2):
                            act.wait_ge(h_ready, n - 1)
                        nc.scalar.activation(gate[(par * G + g) % 2][:, :], bank[:, 0, :], f.func)\
                          .then_inc(act_done, 1)
                    else:
                        for half in range(2):
                            blk = 2 * g + half
                            at = f.up + f.blocks * D + blk
                            nc.scalar.activation(hid[par][:, blk, :], bank[:, half, :], f.func,
                                                 bias=wt[par][:, at:at + 1]).then_inc(h_ready, 1)

            activate(0, 0)
            activate(1, 1)
            with act.Fori(1, J // 2) as i:
                activate(2 * i, 0)
                activate(2 * i + 1, 1)
    st.close()


class Resident:

    def __init__(self, nc, ctx):
        def sb(name, shape, dt=F32):
            return ctx.enter_context(nc.sbuf_tensor(name, shape, dt))
        self.x = sb("x_sb", [P, NT, D])
        self.attn_w = sb("attn_w_sb", [P, NW * KC, D])
        self.attn_bcol = sb("attn_bcol_sb", [P, 8])
        self.attn_brow = sb("attn_brow_sb", [1, 5, D])
        self.ident, self.ident16 = sb("ident", [P, P]), sb("ident16", [P, P], BF16)
        self.ones, self.before = sb("ones", [P, P]), sb("before", [P, P])
        self.earlier, self.same = sb("earlier", [P, NT, E]), sb("same", [P, E])
        self.expert, self.threshold = sb("expert_rev", [P, NT, E]), sb("threshold", [P, E, E])
        self.tile_no = sb("tile_no", [P, RT, E])
        self.parity, self.tmp_i = sb("parity", [P, 2]), sb("tmp_i", [P, 1], I32)
        self.mask0 = sb("mask0_sb", [P, NT, S], BF16)
        self.mask2 = sb("mask2_sb", [P, B, S], BF16)
        self.causal = sb("causal", [P, QT, S], BF16)
        self.pad = sb("pad", [P, XW])


def store(nc, k, dram):
    with nc.semaphore("x_stored") as stored, nc.Block() as block:
        @block.sync
        def _(sp):
            sp.dma_start(dram["out"].rearrange("(t p) d -> p t d", p=P), k.x[:, :, :]).then_inc(stored, 16)
            sp.wait_ge(stored, 16)


STAGES = "a0 f0 a1 f1 a2 f2 a3 f3".split()


def program(nc, dram, stages=STAGES):
    for f in FFNS:
        rows = (T if f.shared else 0) + RT * ST
        dram[f.name + "_xs"] = nc.dram_tensor(f.name + "_xs", [rows, XW], F32, kind="Internal").ap()
        dram[f.name + "_yk"] = nc.dram_tensor(f.name + "_yk", [TK * T, D], F32, kind="Internal").ap()
    with ExitStack() as mem:
        k = Resident(nc, mem)
        constants(nc, k, dram)
        for s in stages:
            if s == "a0":
                attention16(nc, k, dram, "L0a", L0Q, L0K, L0V, L0O, mask="pair", out_bias=4, ffn=FFNS[0])
            elif s == "a1":
                attention1(nc, k, dram, "L1a", L1Q, L1K, L1V)
            elif s == "a2":
                attention16(nc, k, dram, "L2a", L2Q, L2K, L2V, L2O, mask="batch", ffn=FFNS[2])
            elif s == "a3":
                with nc.sbuf_tensor("self_attended", [P, NT, D], F32) as h:
                    attention16(nc, k, dram, "L3a", AQ, AK, AV, AO, kv_self=True, mask="causal", bias=0, out_bias=2,
                                add=False, dst=h)
                    attention16(nc, k, dram, "L3b", BQ, BK, BV, BO, norm=False, bias=1, out_bias=3, src=h, ffn=FFNS[3])
            else:
                feed_forward(nc, k, dram, FFNS[int(s[1])])
        store(nc, k, dram)


def layout(inputs):
    import numpy as np
    a = {n: np.asarray(v) for n, v in inputs.items()}

    def chunks(w):
        return w.reshape(-1, P, w.shape[-1]).transpose(1, 0, 2)

    def heads(w):
        return w.transpose(1, 0, 2).reshape(D, D)

    out = {"x": a["x"].reshape(T, D), "mask0": a["mask_Bx1xSxS2_if1"].reshape(T, S),
           "mask1": a["mask_BxSxS2_ff0"].reshape(NT, P, S).transpose(1, 0, 2), "lens": a["_lenS2"].reshape(B),
           "ctxT": chunks(a["ctx_1024"].reshape(T, D).T)}
    mats = [a[f"L0_xattn_W{m}"].T for m in "qkvo"] + [a[f"L1_xattn_W{m}"].T for m in "qkv"] \
        + [a[f"L2_xattn_W{m}"].T for m in "qkvo"]
    for n in "12":
        mats += [heads(a[f"L3_xattn_W{m}{n}"]) for m in "qkv"] + [a[f"L3_xattn_Wo{n}"]]
    out["attn_w"] = np.concatenate([chunks(m) for m in mats], axis=1)
    cols = [a[f"L3_xattn_b{m}{n}"].reshape(KC, P).T for n in "12" for m in "qk"]
    out["attn_bcol"] = np.concatenate(cols, axis=1)
    brow = [a[f"L3_xattn_b{m}{n}"].reshape(D) for m in "vo" for n in "12"] + [a["L0_xattn_bo"]]
    out["attn_brow"] = np.stack(brow)[None]

    def ups(w, f):
        w = np.pad(w, ((0, 0), (0, f.blocks * P - w.shape[1])))
        return chunks(w).reshape(P, -1)

    def downs(w, f):
        return chunks(np.pad(w, ((0, f.blocks * P - w.shape[0]), (0, 0)))).reshape(P, -1)

    def gated(g, u, d, f):
        return np.concatenate([ups(g, f), ups(u, f), downs(d, f)], axis=1)

    f0, f1, f2, f3 = FFNS
    e0 = [gated(a["L0_ffn_wg"][e], a["L0_ffn_wu"][e], a["L0_ffn_wd"][e], f0) for e in range(E)]
    n = a["L0_ffn_swd"].shape[0] // f0.shared
    e0 += [gated(a["L0_ffn_swg"][:, n * i:n * i + n], a["L0_ffn_swu"][:, n * i:n * i + n],
                 a["L0_ffn_swd"][n * i:n * i + n], f0) for i in range(f0.shared)]
    out["L0f_w"] = np.stack(e0)
    w1 = list(a["L1_ffn_spec_w1"]) + [a["L1_ffn_shared_w1"]]
    w2 = list(a["L1_ffn_spec_w2"]) + [a["L1_ffn_shared_w2"]]
    b1 = list(a["L1_ffn_spec_b1"]) + [a["L1_ffn_shared_b1"]]
    out["L1f_w"] = np.stack([np.concatenate([ups(u.T, f1), downs(d.T, f1), b.reshape(f1.blocks, P).T], axis=1)
                             for u, d, b in zip(w1, w2, b1)])
    out["L1f_b2"] = np.concatenate([a["L1_ffn_spec_b2"], a["L1_ffn_shared_b2"][None]])
    F = f2.blocks * P
    out["L2f_w"] = np.stack([gated(w[:F].T, w[F:].T, d.T, f2) for w, d in zip(a["L2_ffn_W12"], a["L2_ffn_W3"])])
    out["L2f_gb"] = np.stack([a["L2_ffn_ln_gamma"], a["L2_ffn_ln_beta"]])
    names = [("routed_w", e) for e in range(E)] + [("shared_w", e) for e in range(f3.shared)]
    out["L3f_w"] = np.stack([gated(a[f"L3_ffn_{n}1"][e], a[f"L3_ffn_{n}3"][e], a[f"L3_ffn_{n}2"][e], f3)
                             for n, e in names])
    for f, w in zip(FFNS, (a["L0_ffn_gate_w"].T, a["L1_ffn_router_w"].T, a["L2_ffn_Wr"].T, a["L3_ffn_router_w"])):
        out[f.name + "_router"] = chunks(w)
    out["L1f_rb"], out["L3f_rb"] = a["L1_ffn_router_b"], a["L3_ffn_router_b"]
    return {n: np.ascontiguousarray(v) for n, v in out.items()}


def kernel(**inputs):
    import concourse.bacc as bacc
    from concourse.bass_utils import run_bass_kernel_spmd

    nc = bacc.Bacc("TRN2", target_bir_lowering=False, num_devices=1)
    arrays = layout(inputs)
    dram = {n: nc.dram_tensor("in_" + n, v.shape, mybir.dt.from_np(v.dtype), kind="ExternalInput").ap()
            for n, v in arrays.items()}
    dram["out"] = nc.dram_tensor("x_out", [T, D], F32, kind="ExternalOutput").ap()
    program(nc, dram)
    r = run_bass_kernel_spmd(nc, [{"in_" + n: v for n, v in arrays.items()}], core_ids=[0])
    return r.results[0]["x_out"].reshape(B, S, D)
```

```python
import concourse.bass as bass
from concourse import mybir
from contextlib import ExitStack

F32 = mybir.dt.float32
BF16 = mybir.dt.bfloat16
I32 = mybir.dt.int32
ALU = mybir.AluOpType
ACT = mybir.ActivationFunctionType
AX = mybir.AxisListType

P = 128
B, S, D = 8, 256, 256
T = B * S
NT = T // P
KC = D // P
QT = S // P
H, DH = 16, 16
HG = 4
NG = H // HG
NPART, NPROD = 3, 6
HP = 32
EPS = 1e-5
MASKED = -1e20

E = 8
TK = 2
ST = 256
RT = TK * T // ST + E
XT = T // ST
XW = D + 2
NOWHERE = 1 << 20

L0Q, L0K, L0V, L0O, L1Q, L1K, L1V, L2Q, L2K, L2V, L2O = range(11)
AQ, AK, AV, AO, BQ, BK, BV, BO = range(11, 19)
NW = 19


class Ffn:

    def __init__(self, name, blocks, gated, shared, func):
        self.name = name
        self.blocks = blocks
        self.gated = gated
        self.shared = shared
        self.func = func
        self.up = (2 if gated else 1) * KC * blocks * P
        self.b1 = 0 if gated else blocks
        self.cols = self.up + blocks * D + self.b1
        self.groups = blocks if gated else blocks // 2
        self.banks = {4: 4, 3: 3, 8: 4, 1: 2}[self.groups]
        self.tiles = shared * XT + RT


FFNS = [Ffn("L0f", 3, True, 2, ACT.Silu), Ffn("L1f", 8, False, 1, ACT.Gelu_apprx_tanh),
        Ffn("L2f", 8, True, 0, ACT.Silu), Ffn("L3f", 1, True, 2, ACT.Silu)]
CAP = -(-(-(-T * TK * 5 // 4)) // E)


def is_int(n):
    return isinstance(n, int)


def nth(n, par):
    return 8 * (n - par) + 16


def nth2(n, par):
    return 16 * (n - par)


class Chain:

    def __init__(self, eng, sem):
        self.eng, self.sem, self.n = eng, sem, 0

    def __call__(self, ins):
        self.n += 1
        ins.then_inc(self.sem, 1)
        self.eng.wait_ge(self.sem, self.n)


class Stage:

    def __init__(self, nc, name):
        self.nc, self.sems, self.name, self.ctx = nc, [], name, ExitStack()

    def sb(self, name, shape, dt=F32):
        return self.ctx.enter_context(self.nc.sbuf_tensor(f"{self.name}_{name}", shape, dt))

    def pb(self, name, shape, dt=F32):
        return self.ctx.enter_context(self.nc.psum_tensor(f"{self.name}_{name}", shape, dt))

    def sem(self, name):
        handle = self.nc.alloc_semaphore(name=f"{self.name}_{name}")
        self.sems.append(handle)
        return handle

    def close(self):
        self.nc.clear_and_free_semaphores(self.sems)
        self.nc.all_engine_barrier()


def token_stats(nc, k, tile):
    for t in range(QT):
        at = bass.ds(tile + t, 1)
        ins = nc.vector.bn_stats(k.stats[:, at, :], k.x[:, at, :])
    return ins


def layer_norm_scale(nc, k, v, link, mv, sq_ready, sq_done, twice=False):
    gain, floor = (1.0 + EPS, EPS * EPS) if twice else (1.0, EPS)
    me, mo = k.stats[:, :, 1], k.stats[:, :, 4]
    link(nc.vector.tensor_tensor(mv[:, 2, :], me, mo, ALU.subtract))
    nc.vector.tensor_tensor(mv[:, 1, :], me, mo, ALU.add)
    link(nc.vector.tensor_tensor(mv[:, 0, :], k.stats[:, :, 2], k.stats[:, :, 5], ALU.add))
    nc.vector.tensor_tensor(mv[:, 2, :], mv[:, 2, :], mv[:, 2, :], ALU.mult)
    link(nc.vector.tensor_scalar(mv[:, 0, :], mv[:, 0, :], gain / D, floor, ALU.mult, ALU.add))
    nc.vector.scalar_tensor_tensor(out=mv[:, 3, :], in0=mv[:, 2, :], scalar=0.25 * gain, in1=mv[:, 0, :],
                                   op0=ALU.mult, op1=ALU.add).then_inc(sq_ready, 1)
    v.wait_ge(sq_done, 1)
    link(nc.vector.reciprocal(mv[:, 0, :], mv[:, 3, :]))
    link(nc.vector.scalar_tensor_tensor(out=mv[:, 1, :], in0=mv[:, 1, :], scalar=-0.5, in1=mv[:, 0, :],
                                        op0=ALU.mult, op1=ALU.mult))


def layer_norm_root(nc, act, mv, sq_ready, sq_done):
    act.wait_ge(sq_ready, 1)
    nc.scalar.activation(mv[:, 3, :], mv[:, 3, :], ACT.Sqrt).then_inc(sq_done, 1)


def constants(nc, k, dram):
    st = Stage(nc, "const")
    built, link_v, loaded = st.sem("built"), st.sem("dve_step"), st.sem("loaded")
    mask_loaded = st.sem("mask_loaded")
    raw = st.sb("mask_raw", [P, NT, S], I32)
    bits, mod8 = st.sb("row_i", [P, 1], I32), st.sb("row_mod_8", [P, 1], I32)
    with st.ctx, nc.Block() as block:
        @block.sync
        def _(sp):
            sp.dma_start(raw[:, :, :], dram["mask0"].rearrange("(t p) s -> p t s", p=P)).then_inc(mask_loaded, 16)
            sp.dma_start(k.x[:, :, :], dram["x"].rearrange("(t p) d -> p t d", p=P)).then_inc(loaded, 16)
            n = 4 * KC
            sp.dma_start(k.attn_w[:, 0:n, :], dram["attn_w"][:, 0:n, :]).then_inc(loaded, 16)
            sp.dma_start(k.attn_brow[:, :, :], dram["attn_brow"]).then_inc(loaded, 16)
            sp.wait_ge(loaded, 3 * 16)

        @block.gpsimd
        def _(gp):
            link = Chain(gp, built)
            link(nc.gpsimd.iota(bits[:, :], [[0, 1]], base=0, channel_multiplier=1))
            link(nc.gpsimd.memset(k.ident[:, :], 0.0))
            link(nc.gpsimd.affine_select(out=k.ident[:, :], in_=k.ident[:, :], compare_op=ALU.not_equal, fill=1.0,
                                         base=0, pattern=[[-1, P]], channel_multiplier=1))
            link(nc.gpsimd.memset(k.ones[:, :], 1.0))
            link(nc.gpsimd.memset(k.pad[:, 0:D], 0.0))
            link(nc.gpsimd.memset(k.pad[:, D:D + 1].bitcast(I32), NOWHERE))
            link(nc.gpsimd.memset(k.pad[:, D + 1:XW], 0.0))

        @block.vector
        def _(v):
            link = Chain(v, link_v)
            v.wait_ge(built, 3)
            link(nc.vector.tensor_scalar(mod8[:, :], bits[:, :], E - 1, None, ALU.bitwise_and))
            link(nc.vector.tensor_copy(k.row_expert[:, :], mod8[:, :]))
            link(nc.vector.tensor_copy(k.ident16[:, :], k.ident[:, :]))
            v.wait_ge(loaded, 3 * 16)
            for t in range(NT):
                ins = nc.vector.bn_stats(k.stats[:, t, :], k.x[:, t, :])
            link(ins)
            v.wait_ge(mask_loaded, 16)
            link(nc.vector.tensor_scalar(k.mask0[:, :, :], raw[:, :, :], 0.0, MASKED, ALU.is_equal, ALU.mult))
    st.close()


def late_constants(nc, k, dram, gp, st, lens_loaded):
    built = st.sem("late_built")
    lens = st.sb("lens_raw", [P, B], I32)
    lensf = st.sb("lens", [P, B])
    keys = st.sb("key_index", [P, S], I32)
    keysf = st.sb("key_index_f", [P, S])
    expi = st.sb("expert_i", [P, NT, E], I32)
    thri = st.sb("threshold_i", [P, E, E], I32)
    tili = st.sb("tile_i", [P, RT, E], I32)
    link = Chain(gp, built)
    g = nc.gpsimd
    link(g.memset(k.before[:, :], 0.0))
    link(g.affine_select(out=k.before[:, :], in_=k.before[:, :], compare_op=ALU.is_ge, fill=1.0,
                         base=0, pattern=[[-1, P]], channel_multiplier=1))
    link(g.memset(k.causal[:, :, :], 0.0))
    for qt in range(QT):
        link(g.affine_select(out=k.causal[:, qt, :], in_=k.causal[:, qt, :], compare_op=ALU.is_ge,
                             fill=MASKED, base=P * qt, pattern=[[-1, S]], channel_multiplier=1))
    link(g.iota(keys[:, :], [[1, S]], base=0, channel_multiplier=0))
    link(g.iota(expi[:, :, :], [[0, NT], [1, E]], base=0, channel_multiplier=0))
    link(g.iota(thri[:, :, :], [[0, E], [ST, E]], base=0, channel_multiplier=0))
    link(g.iota(tili[:, :, :], [[1, RT], [0, E]], base=0, channel_multiplier=0))
    link(g.memset(k.earlier[:, :, :], 1.0))
    link(g.affine_select(out=k.earlier[:, :, :], in_=k.earlier[:, :, :], compare_op=ALU.is_gt,
                         fill=0.0, base=0, pattern=[[E, NT], [0, E]], channel_multiplier=-1))
    link(g.tensor_copy(k.expert[:, :, :], expi[:, :, :]))
    link(g.tensor_scalar(k.same[:, :], k.expert[:, 0, :], k.row_expert[:, 0:1], None, ALU.is_equal))
    link(g.tensor_tensor(k.earlier[:, :, :], k.earlier[:, :, :],
                         k.same[:, :].unsqueeze(1).to_broadcast([P, NT, E]), ALU.mult))
    link(g.tensor_scalar(k.expert[:, :, :], k.expert[:, :, :], -1.0, float(E), ALU.mult, ALU.add))
    link(g.tensor_copy(k.threshold[:, :, :], thri[:, :, :]))
    link(g.tensor_copy(k.tile_no[:, :, :], tili[:, :, :]))
    gp.dma_start(lens[:, :], dram["lens"].partition_broadcast(P)).then_inc(lens_loaded, 16)
    gp.wait_ge(lens_loaded, 16)
    link(g.tensor_copy(lensf[:, :], lens[:, :]))
    link(g.tensor_copy(keysf[:, :], keys[:, :]))
    for b in range(B):
        link(g.tensor_scalar(k.mask2[:, b, :], keysf[:, :], lensf[:, b:b + 1], MASKED, ALU.is_ge, ALU.mult))


def attention16(nc, k, dram, name, wq, wk, wv, wo, kv_self=False, norm=True, mask=None, bias=None, out_bias=None,
                add=True, src=None, dst=None, ffn=None):
    st = Stage(nc, name)
    sem = st.sem
    ln_step, sq_ready, sq_done = sem("ln_step"), sem("sq_ready"), sem("sq_done")
    ctx_loaded, xn_ready = [sem(f"ctx{i}_loaded") for i in range(2)], sem("xn_ready")
    xT_ready, xT_copied = sem("xT_ready"), sem("xT_copied")
    q_ready, q_copied = sem("q_ready"), sem("q_copied")
    k_ready, k_copied = sem("k_ready"), sem("k_copied")
    v_ready, v_copied = sem("v_ready"), sem("v_copied")
    split_step, split_done, parts_written = sem("split_step"), [sem("q_split"), sem("k_split")], \
        [sem("q_parts_written"), sem("k_parts_written")]
    stacked = [[sem(f"{n}_stacked{i}") for i in range(2)] for n in "qk"]
    s_ready, max_ready, negmax_ready = sem("scores_ready"), sem("max_ready"), sem("negmax_ready")
    p_ready = sem("probs_ready")
    pt_ready, pt_copied_v, pt_copied_a = sem("probsT_ready"), sem("probsT0_copied"), sem("probsT1_copied")
    pv_ready, o_copied = sem("pv_ready"), sem("o_copied")
    ot_ready, rs_ready, on_ready = sem("otok_ready"), sem("recip_ready"), sem("onorm_ready")
    ont_ready, ont_copied = sem("onormT_ready"), sem("onormT_copied")
    y_ready, y_added = sem("y_ready"), sem("y_added")
    pads, v_padded = sem("pads_written"), sem("v_padded")
    first_stage = name == "L0a"
    if first_stage:
        late_loaded, lens_loaded = sem("late_loaded"), sem("lens_loaded")

    mv = st.sb("mv", [P, 4, NT])
    ctxT = [st.sb(f"ctxT{i}", [P, KC, S]) for i in range(2)]
    xn = [st.sb(f"xn{i}", [P, QT, D]) for i in range(2)]
    xT = st.sb("xT", [P, KC, S])
    qT = [st.sb(f"qT{i}", [P, 2, S]) for i in range(2)]
    kT = [st.sb(f"kT{i}", [P, 2, S]) for i in range(2)]
    rest = st.sb("rest", [P, 2, S])
    parts = [st.sb(f"parts{i}", [P, NPART, 2, S], BF16) for i in range(2)]
    q6 = [st.sb(f"q6_{i}", [NPROD * DH, H, S], BF16) for i in range(2)]
    k6 = [st.sb(f"k6_{i}", [NPROD * DH, H, S], BF16) for i in range(2)]
    vv = [st.sb(f"v{i}", [P, QT, H, HP]) for i in range(2)]
    probs = [st.sb(f"probs{i}", [P, HG, S]) for i in range(2)]
    probsT = [st.sb(f"probsT{i}", [P, QT, HG, P]) for i in range(2)]
    rowmax = [st.sb(f"max{i}", [P, HG]) for i in range(2)]
    negmax = [st.sb(f"negmax{i}", [P, HG]) for i in range(2)]
    osum = st.sb("o", [P, NG, P])
    recip = st.sb("recip", [P, H])
    onorm = st.sb("onorm", [P, H, DH])
    onormT = st.sb("onormT", [P, KC, P])
    pS = [st.pb(f"pS{i}", [P, HG, S]) for i in range(2)]
    pT = [st.pb(f"pT{i}", [P, HG, P]) for i in range(2)]
    pO = st.pb("pO", [P, NG, P])
    pM = st.pb("pM", [P, 512])
    pM2 = pM[:, :].rearrange("p (a n) -> p a n", a=2)

    SLOTS = QT * NG
    scale = DH ** -0.5
    W = k.attn_w
    splits = dram["splits"]

    def stacked_value(b, par):
        return 24 * (b - par) + 48

    with st.ctx, nc.Block() as block:
        @block.sync
        def _(sp):
            def load(b, par, waits):
                if waits:
                    sp.wait_ge(v_ready, b - 1)
                sp.dma_start(ctxT[par][:, :, :], dram["ctxT"][:, :, bass.ds(b * S, S)]).then_inc(ctx_loaded[par], 16)

            def stack(b, par, x):
                sp.wait_ge(split_done[x], b + 1)
                for part in range(NPART):
                    sp.dma_start(splits[x, par, part, :, :, :].rearrange("d (f h) s -> h d f s", f=2),
                                 parts[x][:, part, :, :]).then_inc(parts_written[x], 16)
                sp.wait_ge(parts_written[x], 48 * (b + 1))
                to = (q6, k6)[x][par]
                at = 0
                for n in (3, 2, 1):
                    part = 0 if x else 3 - n
                    src = splits[x, par, part:part + n if x else part + 1].rearrange("r d h s -> r d (h s)")
                    if not x:
                        src = src.to_broadcast([n, DH, H * S])
                    sp.dma_start(to[at:at + n * DH, :, :].rearrange("p h s -> p (h s)"), src)\
                      .then_inc(stacked[x][par], 16)
                    at += n * DH

            if not kv_self:
                load(0, 0, False)
                load(1, 1, False)
                stack(0, 0, 1)
            stack(0, 0, 0)
            if kv_self:
                stack(0, 0, 1)
            def pair(i, pars=(1, 0)):
                for par in pars:
                    b = 2 * i + 2 - par
                    if not kv_self:
                        load(b + 1, 1 - par, True)
                    stack(b, par, 0)
                    stack(b, par, 1)

            for par in (1, 0):
                pair(0, (par,))
                if first_stage:
                    n = (NW - 4) * KC // 2
                    at = 4 * KC + (1 - par) * n
                    sp.dma_start(k.attn_w[:, at:at + n, :], dram["attn_w"][:, at:at + n, :]).then_inc(late_loaded, 16)
            if first_stage:
                sp.dma_start(k.attn_bcol[:, :], dram["attn_bcol"]).then_inc(late_loaded, 16)
            if ffn is not None:
                fills = [(dram[ffn.name + "_xs"], XW)]
                if ffn.name == "L2f":
                    fills.append((dram["L2f_yk"], D))
            with sp.Fori(1, B // 2 - 1) as i:
                for par in (1, 0):
                    pair(i, (par,))
                    if ffn is not None:
                        for rows, w in fills:
                            n = rows.shape[0] // 4
                            sp.dma_start(rows[bass.ds((2 * i - 1 - par) * n, n), :]
                                         .rearrange("(n p) w -> p n w", p=P),
                                         k.pad[:, 0:w].unsqueeze(1).to_broadcast([P, n // P, w])).then_inc(pads, 16)
            stack(B - 1, 1, 0)
            stack(B - 1, 1, 1)
            if ffn is not None:
                sp.wait_ge(pads, 4 * 16 * len(fills))
            if first_stage:
                sp.wait_ge(late_loaded, 3 * 16)

        @block.gpsimd
        def _(gp):
            zero = k.pad[:, 0:S].unsqueeze(1).to_broadcast([P, 2, S])

            def split(b, par, x, m):
                src, out = (qT, kT)[x][par][:, :, :], parts[x]
                gp.wait_ge((q_copied, k_copied)[x], b + 1)
                if not (is_int(b) and b == 0):
                    gp.wait_ge(parts_written[x], 48 * b)
                nc.gpsimd.tensor_tensor(out[:, 0, :, :], src, zero, ALU.add).then_inc(split_step, 1)
                gp.wait_ge(split_step, 3 * m + 1)
                nc.gpsimd.tensor_tensor(rest[:, :, :], src, out[:, 0, :, :], ALU.subtract).then_inc(split_step, 1)
                gp.wait_ge(split_step, 3 * m + 2)
                nc.gpsimd.tensor_tensor(out[:, 1, :, :], rest[:, :, :], zero, ALU.add).then_inc(split_step, 1)
                gp.wait_ge(split_step, 3 * m + 3)
                nc.gpsimd.tensor_tensor(out[:, 2, :, :], rest[:, :, :], out[:, 1, :, :], ALU.subtract)\
                  .then_inc(split_done[x], 1)

            if not kv_self:
                split(0, 0, 1, 0)
            split(0, 0, 0, 0 if kv_self else 1)
            if kv_self:
                split(0, 0, 1, 1)

            def pair(i):
                for par in (1, 0):
                    b = 2 * i + 2 - par
                    for x in range(2):
                        split(b, par, x, 2 * b + x)

            pair(0)
            if first_stage:
                late_constants(nc, k, dram, gp, st, lens_loaded)
            with gp.Fori(1, B // 2 - 1) as i:
                pair(i)
            for x in range(2):
                split(B - 1, 1, x, 2 * (B - 1) + x)

        @block.tensor
        def _(pe):
            def project_x(b, par):
                pe.wait_ge(xn_ready, b + 1)
                for t in range(QT):
                    for c in range(KC):
                        last = nc.tensor.transpose(pM2[:, c, t * P:(t + 1) * P],
                                                   xn[par][:, t, c * P:(c + 1) * P], k.ident[:, :])
                last.then_inc(xT_ready, 1)

            def project_q(b, par):
                pe.wait_ge(xT_copied, b + 1)
                for f in range(2):
                    for c in range(KC):
                        last = nc.tensor.matmul(pM2[:, f, :], W[:, wq * KC + c, f * P:(f + 1) * P], xT[:, c, :],
                                                start=(c == 0), stop=(c == KC - 1))
                last.then_inc(q_ready, 1)

            def project_k(b, par):
                if not kv_self:
                    pe.wait_ge(ctx_loaded[par], nth(b, par))
                kv = xT if kv_self else ctxT[par]
                for f in range(2):
                    for c in range(KC):
                        last = nc.tensor.matmul(pM2[:, f, :], W[:, wk * KC + c, f * P:(f + 1) * P], kv[:, c, :],
                                                start=(c == 0), stop=(c == KC - 1))
                last.then_inc(k_ready, 1)

            def project_v(b, par):
                kv = xT if kv_self else ctxT[par]
                for t in range(QT):
                    for c in range(KC):
                        last = nc.tensor.matmul(pM2[:, t, :], kv[:, c, t * P:(t + 1) * P], W[:, wv * KC + c, :],
                                                start=(c == 0), stop=(c == KC - 1 and bias is None))
                    if bias is not None:
                        last = nc.tensor.matmul(pM2[:, t, :], k.ones[0:1, :], k.attn_brow[0:1, bias, :],
                                                start=False, stop=True)
                last.then_inc(v_ready, 1)

            def scores(s, b, par, sl):
                qt, g = divmod(sl, NG)
                if sl == 0:
                    for x in range(2):
                        pe.wait_ge(stacked[x][par], stacked_value(b, par))
                if not (is_int(s) and s < 2):
                    pe.wait_ge(p_ready, HG * (s - 1))
                out = pS[sl % 2]
                m = {None: None, "pair": k.mask0, "batch": k.mask2, "causal": k.causal}[mask]
                if m is not None:
                    at = {"pair": b * QT + qt, "batch": b, "causal": qt}[mask]
                    for j in range(HG):
                        nc.tensor.matmul(out[:, j, :], k.ident16[:, :], m[:, bass.ds(at, 1), :],
                                         start=(j % 2 == 0), stop=False, skip_group_check=True)
                for j in range(HG):
                    h = HG * g + j
                    last = nc.tensor.matmul(out[:, j, :], q6[par][:, h, qt * P:(qt + 1) * P], k6[par][:, h, :],
                                            start=(m is None and j % 2 == 0), stop=True, skip_group_check=True)
                last.then_inc(s_ready, 1)

            def transpose_probs(s, sl):
                pe.wait_ge(p_ready, HG * (s + 1))
                for t in range(QT):
                    if not (is_int(s) and s == 0):
                        pe.wait_ge(pt_copied_v if t == 0 else pt_copied_a, s)
                    for j in range(HG):
                        last = nc.tensor.transpose(pT[t][:, j, :], probs[sl % 2][:, j, t * P:(t + 1) * P],
                                                   k.ident[:, :])
                    last.then_inc(pt_ready, 1)

            def weighted(s, u, sl, par):
                g = sl % NG
                pe.wait_ge(pt_copied_v, s + 1)
                pe.wait_ge(pt_copied_a, s + 1)
                if is_int(s) and s == 0:
                    pe.wait_ge(v_padded, 4)
                if g == 0 and not (is_int(u) and u == 0):
                    pe.wait_ge(o_copied, u)
                for t in range(QT):
                    for j in range(HG):
                        last = nc.tensor.matmul(pO[HP * j:HP * (j + 1), g, :], vv[par][:, t, HG * g + j, :],
                                                probsT[sl % 2][:, t, j, :], start=(g == 0 and t == 0),
                                                stop=(t == QT - 1), skip_group_check=True)
                if g == NG - 1:
                    last.then_inc(pv_ready, 1)

            def tokens_of_o(u):
                pe.wait_ge(o_copied, u + 1)
                for g in range(NG):
                    last = nc.tensor.transpose(pM[:, g * P:(g + 1) * P], osum[:, g, :], k.ident[:, :])
                last.then_inc(ot_ready, 1)

            def features_of_o(u):
                pe.wait_ge(on_ready, u + 1)
                for c in range(KC):
                    last = nc.tensor.transpose(pM[:, c * P:(c + 1) * P],
                                               onorm[:, 8 * c:8 * c + 8, :].rearrange("p h d -> p (h d)"),
                                               k.ident[:, :])
                last.then_inc(ont_ready, 1)

            def output(u):
                pe.wait_ge(ont_copied, u + 1)
                for c in range(KC):
                    last = nc.tensor.matmul(pM2[:, 0, :], onormT[:, c, :], W[:, wo * KC + c, :],
                                            start=(c == 0), stop=(c == KC - 1 and out_bias is None))
                if out_bias is not None:
                    last = nc.tensor.matmul(pM2[:, 0, :], k.ones[0:1, :], k.attn_brow[0:1, out_bias, :],
                                            start=False, stop=True)
                last.then_inc(y_ready, 1)

            def batch(b, par, first, last):
                for sl in range(SLOTS):
                    s = b * SLOTS + sl
                    u = b * QT
                    if not (last and sl == SLOTS - 1):
                        nb = b if sl < SLOTS - 1 else b + 1
                        scores(s + 1, nb, par if sl < SLOTS - 1 else 1 - par, (sl + 1) % SLOTS)
                    transpose_probs(s, sl)
                    if sl == 0 and not last:
                        if first and kv_self:
                            pe.wait_ge(v_copied, 1)
                        elif first:
                            pe.wait_ge(q_copied, 1)
                        else:
                            pe.wait_ge(y_added, u - 1)
                        project_x(b + 1, 1 - par)
                    if sl == 1 and not first:
                        if last:
                            pe.wait_ge(y_added, u - 1)
                        else:
                            pe.wait_ge(xT_copied, b + 2)
                        tokens_of_o(u - 1)
                    if sl == 2 and not first:
                        features_of_o(u - 1)
                    if sl == 3 and not first:
                        if not last:
                            pe.wait_ge(q_copied, b + 2)
                        output(u - 1)
                    if sl == 5:
                        if last:
                            pe.wait_ge(y_added, u)
                        else:
                            pe.wait_ge(k_copied, b + 2)
                        tokens_of_o(u)
                    if sl == 6:
                        features_of_o(u)
                    if sl == 7:
                        if not last:
                            pe.wait_ge(v_copied, b + 2)
                        output(u)
                    if not (first and sl == 0):
                        weighted(s - 1, u + (sl - 1) // NG, (sl - 1) % SLOTS, par if sl else 1 - par)
                    if sl == 2 and not last:
                        if not first:
                            pe.wait_ge(ont_copied, u)
                        project_q(b + 1, 1 - par)
                    if sl == 3 and not last:
                        if first:
                            pe.wait_ge(q_copied, b + 2)
                        else:
                            pe.wait_ge(y_added, u)
                        project_k(b + 1, 1 - par)
                    if sl == 6 and not last:
                        pe.wait_ge(ont_copied, u + 1)
                        project_v(b + 1, 1 - par)

            def project_kv():
                project_k(0, 0)
                pe.wait_ge(k_copied, 1)
                project_v(0, 0)

            if kv_self:
                project_x(0, 0)
                project_q(0, 0)
                pe.wait_ge(q_copied, 1)
                project_kv()
            else:
                project_kv()
                pe.wait_ge(v_copied, 1)
                project_x(0, 0)
                project_q(0, 0)
            scores(0, 0, 0, 0)
            batch(0, 0, True, False)
            batch(1, 1, False, False)
            with pe.Fori(1, B // 2 - 1) as i:
                batch(2 * i, 0, False, False)
                batch(2 * i + 1, 1, False, False)
            batch(B - 2, 0, False, False)
            batch(B - 1, 1, False, True)
            U = B * QT
            weighted(B * SLOTS - 1, U - 1, SLOTS - 1, 1)
            pe.wait_ge(y_added, U - 1)
            tokens_of_o(U - 1)
            features_of_o(U - 1)
            output(U - 1)

        @block.vector
        def _(v):
            def normalise(b, par):
                if not (is_int(b) and b < 2):
                    v.wait_ge(xT_ready, b - 1)
                for t in range(QT):
                    at = bass.ds(b * QT + t, 1)
                    if norm:
                        ins = nc.vector.tensor_scalar(xn[par][:, t, :], k.x[:, at, :], mv[:, 0, at],
                                                      mv[:, 1, at], ALU.mult, ALU.add)
                    else:
                        ins = nc.vector.tensor_copy(xn[par][:, t, :], src[:, at, :])
                ins.then_inc(xn_ready, 1)

            def copy_xT(b, par):
                v.wait_ge(xT_ready, b + 1)
                nc.vector.tensor_copy(xT[:, :, :], pM2).then_inc(xT_copied, 1)

            def copy_k(b, par):
                v.wait_ge(k_ready, b + 1)
                if not (is_int(b) and b < 2):
                    v.wait_ge(split_done[1], b - 1)
                if bias is None:
                    nc.vector.tensor_copy(kT[par][:, :, :], pM2).then_inc(k_copied, 1)
                else:
                    for f in range(2):
                        at = 4 * bias + 2 + f
                        ins = nc.vector.tensor_scalar(kT[par][:, f, :], pM2[:, f, :], k.attn_bcol[:, at:at + 1], None,
                                                      ALU.add)
                    ins.then_inc(k_copied, 1)

            def maxima(s, sl):
                v.wait_ge(s_ready, s + 1)
                nc.vector.tensor_reduce(rowmax[sl % 2][:, :], pS[sl % 2][:, :, :], AX.X, ALU.max)\
                  .then_inc(max_ready, 1)
                v.wait_ge(max_ready, s + 1)
                nc.vector.tensor_scalar(negmax[sl % 2][:, :], rowmax[sl % 2][:, :], -scale, None, ALU.mult)\
                  .then_inc(negmax_ready, 1)

            def copy_probsT(s, sl):
                v.wait_ge(pt_ready, 2 * s + 1)
                nc.vector.tensor_copy(probsT[sl % 2][:, 0, :, :], pT[0][:, :, :]).then_inc(pt_copied_v, 1)

            def normalise_o(u):
                v.wait_ge(ot_ready, u + 1)
                o = pM[:, :].rearrange("p (h d) -> p h d", d=HP)
                nc.vector.reciprocal(recip[:, :], o[:, :, DH]).then_inc(rs_ready, 1)
                v.wait_ge(rs_ready, u + 1)
                nc.vector.tensor_tensor(onorm[:, :, :], o[:, :, 0:DH],
                                        recip[:, :].unsqueeze(2).to_broadcast([P, H, DH]), ALU.mult)\
                  .then_inc(on_ready, 1)

            def take_output(u):
                v.wait_ge(y_ready, u + 1)
                at = bass.ds(u, 1)
                if add:
                    nc.vector.tensor_tensor(k.x[:, at, :], k.x[:, at, :], pM2[:, 0:1, :], ALU.add)\
                      .then_inc(y_added, 1)
                else:
                    nc.vector.tensor_copy(dst[:, at, :], pM2[:, 0:1, :]).then_inc(y_added, 1)

            def batch(b, par, first, last):
                for sl in range(SLOTS):
                    s = b * SLOTS + sl
                    u = b * QT
                    if not (last and sl == SLOTS - 1):
                        maxima(s + 1, (sl + 1) % SLOTS)
                    if sl == 4 and add and not first:
                        v.wait_ge(y_added, u)
                    copy_probsT(s, sl)
                    if sl == 4 and add and not first:
                        token_stats(nc, k, u - QT)
                    if sl == 0 and not last:
                        copy_xT(b + 1, 1 - par)
                    if sl == 1 and not first:
                        normalise_o(u - 1)
                    if sl == 3 and not first:
                        take_output(u - 1)
                    if sl == 3 and not last:
                        copy_k(b + 1, 1 - par)
                    if sl == 5:
                        normalise_o(u)
                    if sl == 7:
                        take_output(u)
                    if sl == 3 and not last and not (is_int(b) and b == B - 2):
                        normalise(b + 2, par)

            for par in range(2):
                nc.vector.memset(vv[par][:, :, :, DH + 1:HP], 0.0).then_inc(v_padded, 1)
                nc.vector.memset(vv[par][:, :, :, DH:DH + 1], 1.0).then_inc(v_padded, 1)
            if not kv_self:
                copy_k(0, 0)
            if norm:
                layer_norm_scale(nc, k, v, Chain(v, ln_step), mv, sq_ready, sq_done)
            normalise(0, 0)
            normalise(1, 1)
            copy_xT(0, 0)
            if kv_self:
                copy_k(0, 0)
            maxima(0, 0)
            batch(0, 0, True, False)
            batch(1, 1, False, False)
            with v.Fori(1, B // 2 - 1) as i:
                batch(2 * i, 0, False, False)
                batch(2 * i + 1, 1, False, False)
            batch(B - 2, 0, False, False)
            batch(B - 1, 1, False, True)
            normalise_o(B * QT - 1)
            take_output(B * QT - 1)
            if add:
                v.wait_ge(y_added, B * QT)
                token_stats(nc, k, (B - 1) * QT)

        @block.scalar
        def _(act):
            def copy_q(b, par):
                act.wait_ge(q_ready, b + 1)
                if not (is_int(b) and b < 2):
                    act.wait_ge(split_done[0], b - 1)
                if bias is None:
                    nc.scalar.copy(qT[par][:, :, :], pM2).then_inc(q_copied, 1)
                else:
                    for f in range(2):
                        at = 4 * bias + f
                        ins = nc.scalar.activation(qT[par][:, f, :], pM2[:, f, :], ACT.Identity,
                                                   bias=k.attn_bcol[:, at:at + 1])
                    ins.then_inc(q_copied, 1)

            def copy_v(b, par):
                act.wait_ge(v_ready, b + 1)
                nc.scalar.copy(vv[par][:, :, :, 0:DH].rearrange("p t h d -> p (t h) d"),
                               pM[:, :].rearrange("p (n d) -> p n d", d=DH)).then_inc(v_copied, 1)

            def probabilities(s, sl):
                act.wait_ge(negmax_ready, s + 1)
                if not (is_int(s) and s < 2):
                    act.wait_ge(pt_ready, 2 * (s - 1))
                for j in range(HG):
                    nc.scalar.activation(probs[sl % 2][:, j, :], pS[sl % 2][:, j, :], ACT.Exp,
                                         bias=negmax[sl % 2][:, j:j + 1], scale=scale).then_inc(p_ready, 1)

            def copy_probsT(s, sl):
                act.wait_ge(pt_ready, 2 * (s + 1))
                nc.scalar.copy(probsT[sl % 2][:, 1, :, :], pT[1][:, :, :]).then_inc(pt_copied_a, 1)

            def copy_o(u):
                act.wait_ge(pv_ready, u + 1)
                nc.scalar.copy(osum[:, :, :], pO[:, :, :]).then_inc(o_copied, 1)

            def copy_onormT(u):
                act.wait_ge(ont_ready, u + 1)
                nc.scalar.copy(onormT[:, :, :], pM2[:, 0, :].rearrange("p (c n) -> p c n", c=KC))\
                  .then_inc(ont_copied, 1)

            def batch(b, par, first, last):
                for sl in range(SLOTS):
                    s = b * SLOTS + sl
                    u = b * QT
                    copy_probsT(s, sl)
                    if sl == 2 and not first:
                        copy_onormT(u - 1)
                    if sl == 6:
                        copy_onormT(u)
                    if not (last and sl == SLOTS - 1):
                        probabilities(s + 1, (sl + 1) % SLOTS)
                    if sl == 0 and not first:
                        copy_o(u - 1)
                    if sl == 2 and not last:
                        copy_q(b + 1, 1 - par)
                    if sl == 4:
                        copy_o(u)
                    if sl == 6 and not last:
                        copy_v(b + 1, 1 - par)

            if not kv_self:
                copy_v(0, 0)
            if norm:
                layer_norm_root(nc, act, mv, sq_ready, sq_done)
            copy_q(0, 0)
            if kv_self:
                copy_v(0, 0)
            probabilities(0, 0)
            batch(0, 0, True, False)
            batch(1, 1, False, False)
            with act.Fori(1, B // 2 - 1) as i:
                batch(2 * i, 0, False, False)
                batch(2 * i + 1, 1, False, False)
            batch(B - 2, 0, False, False)
            batch(B - 1, 1, False, True)
            copy_o(B * QT - 1)
            copy_onormT(B * QT - 1)
    st.close()


def attention1(nc, k, dram, name, wq, wk, wv):
    st = Stage(nc, name)
    sem = st.sem
    ln_step, sq_ready, sq_done = sem("ln_step"), sem("sq_ready"), sem("sq_done")
    ctx_loaded, mask_loaded = [sem(f"ctx{i}_loaded") for i in range(2)], [sem(f"mask{i}_loaded") for i in range(2)]
    xn_ready = sem("xn_ready")
    xT_ready, xT_copied = sem("xT_ready"), sem("xT_copied")
    q_ready, q_copied = sem("q_ready"), sem("q_copied")
    k_ready, k_copied = sem("k_ready"), sem("k_copied")
    v_ready, v_copied = sem("v_ready"), sem("v_copied")
    s_ready, s_masked, negmax_ready = sem("scores_ready"), sem("scores_masked"), sem("negmax_ready")
    p_ready, pt_ready, pt_copied = sem("probs_ready"), sem("probsT_ready"), sem("probsT_copied")
    o_ready, recip_ready, o_scaled, o_added = sem("o_ready"), sem("recip_ready"), sem("o_scaled"), sem("o_added")
    pads = sem("pads_written")

    mv = st.sb("mv", [P, 4, NT])
    ctxT = [st.sb(f"ctxT{i}", [P, KC, S]) for i in range(2)]
    bias = [st.sb(f"mask{i}", [P, QT, S]) for i in range(2)]
    xn = [st.sb(f"xn{i}", [P, QT, D]) for i in range(2)]
    xT = st.sb("xT", [P, KC, S])
    qT = [st.sb(f"qT{i}", [P, KC, S]) for i in range(2)]
    kT = [st.sb(f"kT{i}", [P, KC, S]) for i in range(2)]
    vv = [st.sb(f"v{i}", [P, QT, D]) for i in range(2)]
    sm = [st.sb(f"scores{i}", [P, S]) for i in range(QT)]
    probs = [st.sb(f"probs{i}", [P, S]) for i in range(QT)]
    probsT = [st.sb(f"probsT{i}", [P, QT, P]) for i in range(QT)]
    stat = [st.sb(f"stat{i}", [P, 4]) for i in range(QT)]
    oo = [st.sb(f"o{i}", [P, D]) for i in range(QT)]
    pS = [st.pb(f"pS{i}", [P, 512]) for i in range(QT)]
    pT = [st.pb(f"pT{i}", [P, 512]) for i in range(QT)]
    pO = [st.pb(f"pO{i}", [P, 512]) for i in range(QT)]
    pM = [st.pb(f"pM{i}", [P, 2, S]) for i in range(2)]
    W = k.attn_w
    scale = D ** -0.5
    ffn = FFNS[1]

    with st.ctx, nc.Block() as block:
        @block.sync
        def _(sp):
            def load(b, par, waits):
                if waits:
                    sp.wait_ge(s_masked, QT * (b - 1))
                sp.dma_start(ctxT[par][:, :, :], dram["ctxT"][:, :, bass.ds(b * S, S)]).then_inc(ctx_loaded[par], 16)
                sp.dma_start(bias[par][:, :, :], dram["mask1"][:, bass.ds(b * QT, QT), :]).then_inc(mask_loaded[par], 16)
            load(0, 0, False)
            load(1, 1, False)
            rows = dram[ffn.name + "_xs"].rearrange("(n p) w -> p n w", p=P)
            sp.dma_start(rows, k.pad[:, :].unsqueeze(1).to_broadcast([P, rows.shape[1], XW])).then_inc(pads, 16)
            with sp.Fori(1, B // 2) as i:
                load(2 * i, 0, True)
                load(2 * i + 1, 1, True)
            sp.wait_ge(pads, 16)

        @block.tensor
        def _(pe):
            def project_x(b, par):
                pe.wait_ge(xn_ready, b + 1)
                if not (is_int(b) and b == 0):
                    pe.wait_ge(k_copied, b)
                for t in range(QT):
                    for c in range(KC):
                        last = nc.tensor.transpose(pM[0][:, c, t * P:(t + 1) * P],
                                                   xn[par][:, t, c * P:(c + 1) * P], k.ident[:, :])
                last.then_inc(xT_ready, 1)

            def project(out, w, src, ready):
                for f in range(KC):
                    for c in range(KC):
                        last = nc.tensor.matmul(out[:, f, :], W[:, w * KC + c, f * P:(f + 1) * P], src[:, c, :],
                                                start=(c == 0), stop=(c == KC - 1))
                last.then_inc(ready, 1)

            def project_q(b, par):
                pe.wait_ge(xT_copied, b + 1)
                if not (is_int(b) and b == 0):
                    pe.wait_ge(v_copied, b)
                project(pM[1], wq, xT, q_ready)

            def project_k(b, par):
                pe.wait_ge(ctx_loaded[par], nth(b, par))
                project(pM[0], wk, ctxT[par], k_ready)

            def project_v(b, par):
                pe.wait_ge(q_copied, b + 1)
                for t in range(QT):
                    for c in range(KC):
                        last = nc.tensor.matmul(pM[1][:, t, :], ctxT[par][:, c, t * P:(t + 1) * P],
                                                W[:, wv * KC + c, :], start=(c == 0), stop=(c == KC - 1))
                last.then_inc(v_ready, 1)

            def scores(b, par, qt):
                if not (is_int(b) and b == 0):
                    pe.wait_ge(s_masked, QT * b - 1 + qt)
                for c in range(KC):
                    last = nc.tensor.matmul(pS[qt][:, 0:S], qT[par][:, c, qt * P:(qt + 1) * P], kT[par][:, c, :],
                                            start=(c == 0), stop=(c == KC - 1))
                last.then_inc(s_ready, 1)

            def transpose_probs(b, qt):
                pe.wait_ge(p_ready, QT * b + qt + 1)
                for t in range(QT):
                    last = nc.tensor.transpose(pT[qt][:, t * P:(t + 1) * P], probs[qt][:, t * P:(t + 1) * P],
                                               k.ident[:, :])
                last.then_inc(pt_ready, 1)

            def weighted(b, par, qt):
                pe.wait_ge(pt_copied, QT * b + qt + 1)
                if not (is_int(b) and b == 0):
                    pe.wait_ge(o_scaled, QT * b - 1 + qt)
                for t in range(QT):
                    last = nc.tensor.matmul(pO[qt][:, 0:D], probsT[qt][:, t, :], vv[par][:, t, :],
                                            start=(t == 0), stop=(t == QT - 1))
                last.then_inc(o_ready, 1)

            def batch(b, par, last):
                pe.wait_ge(q_copied, b + 1)
                pe.wait_ge(k_copied, b + 1)
                scores(b, par, 0)
                scores(b, par, 1)
                if not last:
                    project_x(b + 1, 1 - par)
                transpose_probs(b, 0)
                if not last:
                    project_q(b + 1, 1 - par)
                transpose_probs(b, 1)
                if not last:
                    project_k(b + 1, 1 - par)
                pe.wait_ge(v_copied, b + 1)
                weighted(b, par, 0)
                if not last:
                    project_v(b + 1, 1 - par)
                weighted(b, par, 1)

            project_x(0, 0)
            project_q(0, 0)
            project_k(0, 0)
            project_v(0, 0)
            batch(0, 0, False)
            with pe.Fori(0, B // 2 - 1) as i:
                batch(2 * i + 1, 1, False)
                batch(2 * i + 2, 0, False)
            batch(B - 1, 1, True)

        @block.vector
        def _(v):
            layer_norm_scale(nc, k, v, Chain(v, ln_step), mv, sq_ready, sq_done)

            def normalise(b, par):
                if not (is_int(b) and b < 2):
                    v.wait_ge(xT_ready, b - 1)
                for t in range(QT):
                    at = bass.ds(b * QT + t, 1)
                    ins = nc.vector.tensor_scalar(xn[par][:, t, :], k.x[:, at, :], mv[:, 0, at], mv[:, 1, at],
                                                  ALU.mult, ALU.add)
                ins.then_inc(xn_ready, 1)

            def copy_xT(b):
                v.wait_ge(xT_ready, b + 1)
                nc.vector.tensor_copy(xT[:, :, :], pM[0][:, :, :]).then_inc(xT_copied, 1)

            def copy_k(b, par):
                v.wait_ge(k_ready, b + 1)
                nc.vector.tensor_copy(kT[par][:, :, :], pM[0][:, :, :]).then_inc(k_copied, 1)

            def mask_and_max(b, par, qt):
                n = QT * b + qt + 1
                v.wait_ge(mask_loaded[par], nth(b, par))
                v.wait_ge(s_ready, n)
                nc.vector.scalar_tensor_tensor(out=sm[qt][:, :], in0=pS[qt][:, 0:S], scalar=scale,
                                               in1=bias[par][:, qt, :], op0=ALU.mult, op1=ALU.add)\
                  .then_inc(s_masked, 1)
                v.wait_ge(s_masked, n)
                nc.vector.tensor_reduce(stat[qt][:, 0:1], sm[qt][:, :], AX.X, ALU.max).then_inc(negmax_ready, 1)
                v.wait_ge(negmax_ready, 2 * n - 1)
                nc.vector.tensor_scalar(stat[qt][:, 1:2], stat[qt][:, 0:1], -1.0, None, ALU.mult)\
                  .then_inc(negmax_ready, 1)

            def take_output(b, qt):
                n = QT * b + qt + 1
                v.wait_ge(o_ready, n)
                nc.vector.reciprocal(stat[qt][:, 3:4], stat[qt][:, 2:3]).then_inc(recip_ready, 1)
                v.wait_ge(recip_ready, n)
                at = bass.ds(b * QT + qt, 1)
                nc.vector.scalar_tensor_tensor(out=k.x[:, at, :], in0=pO[qt][:, 0:D].unsqueeze(1),
                                               scalar=stat[qt][:, 3:4], in1=k.x[:, at, :],
                                               op0=ALU.mult, op1=ALU.add).then_inc(o_scaled, 1)

            def batch(b, par, last):
                first = is_int(b) and b == 0
                if not first:
                    v.wait_ge(o_scaled, QT * b)
                mask_and_max(b, par, 0)
                mask_and_max(b, par, 1)
                if not first:
                    token_stats(nc, k, (b - 1) * QT)
                if not last:
                    copy_xT(b + 1)
                    copy_k(b + 1, 1 - par)
                    if not (is_int(b) and b == B - 2):
                        normalise(b + 2, par)
                take_output(b, 0)
                take_output(b, 1)

            normalise(0, 0)
            normalise(1, 1)
            copy_xT(0)
            copy_k(0, 0)
            batch(0, 0, False)
            with v.Fori(0, B // 2 - 2) as i:
                batch(2 * i + 1, 1, False)
                batch(2 * i + 2, 0, False)
            batch(B - 3, 1, False)
            batch(B - 2, 0, False)
            batch(B - 1, 1, True)
            v.wait_ge(o_scaled, QT * B)
            token_stats(nc, k, (B - 1) * QT)

        @block.scalar
        def _(act):
            layer_norm_root(nc, act, mv, sq_ready, sq_done)

            def copy_q(b, par):
                act.wait_ge(q_ready, b + 1)
                nc.scalar.copy(qT[par][:, :, :], pM[1][:, :, :]).then_inc(q_copied, 1)

            def copy_v(b, par):
                act.wait_ge(v_ready, b + 1)
                nc.scalar.copy(vv[par][:, :, :], pM[1][:, :, :]).then_inc(v_copied, 1)

            def probabilities(b, qt):
                act.wait_ge(negmax_ready, 2 * (QT * b + qt + 1))
                if not (is_int(b) and b == 0):
                    act.wait_ge(o_scaled, QT * b - 1 + qt)
                nc.scalar.activation(probs[qt][:, :], sm[qt][:, :], ACT.Exp, bias=stat[qt][:, 1:2],
                                     accum_out=stat[qt][:, 2:3]).then_inc(p_ready, 1)

            def copy_probsT(b, qt):
                act.wait_ge(pt_ready, QT * b + qt + 1)
                nc.scalar.copy(probsT[qt][:, :, :], pT[qt][:, 0:S].rearrange("p (t n) -> p t n", t=QT))\
                  .then_inc(pt_copied, 1)

            def batch(b, par, last):
                probabilities(b, 0)
                probabilities(b, 1)
                copy_probsT(b, 0)
                if not last:
                    copy_q(b + 1, 1 - par)
                copy_probsT(b, 1)
                if not last:
                    copy_v(b + 1, 1 - par)

            copy_q(0, 0)
            copy_v(0, 0)
            batch(0, 0, False)
            with act.Fori(0, B // 2 - 1) as i:
                batch(2 * i + 1, 1, False)
                batch(2 * i + 2, 0, False)
            batch(B - 1, 1, True)
    st.close()


def feed_forward(nc, k, dram, f):
    L1, L2, L3 = f.name == "L1f", f.name == "L2f", f.name == "L3f"
    st = Stage(nc, f.name)
    sem = st.sem
    sq_ready, sq_done, dve_step = sem("sq_ready"), sem("sq_done"), sem("dve_step")
    small_loaded, xn_ready = sem("small_loaded"), sem("xn_ready")
    xt_ready, xt_copied, logits_ready = sem("xT_ready"), sem("xT_copied"), sem("logits_ready")
    exp_in, exp_out = sem("exp_input_ready"), sem("exp_done")
    chosen, counted, counted_c = sem("experts_chosen"), sem("counts_ready"), sem("counts_copied")
    ranked, placed, dispatched = sem("ranks_ready"), sem("slots_placed"), sem("rows_dispatched")
    second = sem("second_copy")
    second_norm = sem("second_norm")
    x_loaded, w_loaded = [sem(f"x_tile{i}_loaded") for i in range(2)], [sem(f"weights{i}_loaded") for i in range(2)]
    b2_loaded = [sem(f"b2_{i}_loaded") for i in range(2)]
    tT_ready, tT_copied, meta_copied = sem("tileT_ready"), sem("tileT_copied"), sem("meta_copied")
    up_ready, act_done, h_ready = sem("up_ready"), sem("activated"), sem("hidden_ready")
    y_ready, y_copied, y_sent = sem("y_ready"), sem("y_copied"), [sem(f"y{i}_sent") for i in range(2)]
    back_loaded, back_added = [sem(f"back{i}_loaded") for i in range(4)], sem("back_added")

    mv = st.sb("mv", [P, 4, NT])
    rows = st.sb("rows", [P, TK, NT, XW])
    wr = st.sb("router", [P, KC, E])
    rb = st.sb("router_b", [P, E])
    gb = st.sb("gamma_beta", [P, 2, D]) if L2 else None
    XTN = NT if f.shared else 2
    xT = st.sb("xT", [P, KC, XTN * P])
    at_tile = lambda t: slice(t % XTN * P, (t % XTN + 1) * P)
    lg = st.sb("logits", [P, NT, E])
    sc = st.sb("score", [P, NT, E])
    one = [st.sb(f"choice{i}", [P, NT, E]) for i in range(TK)]
    ex = st.sb("exp", [P, NT, E])
    tot = st.sb("totals", [P, P])
    r16 = [st.sb(f"row{i}", [P, NT]) for i in range(8)]
    r8 = [st.sb(f"seg{i}", [P, E]) for i in range(6)]
    big8 = st.sb("seg_cmp", [P, E, E])
    bigt = st.sb("tile_cmp", [P, RT, E])
    tef = st.sb("tile_expert_f", [P, RT])
    te = st.sb("tile_expert", [P, RT], I32)
    pos = st.sb("slot", [P, TK, NT], I32)
    xin = [st.sb(f"x_tile{i}", [P, 2, XW]) for i in range(2)]
    meta = [st.sb(f"meta{i}", [P, 2, 2]) for i in range(2)]
    tT = [st.sb(f"tileT{i}", [P, KC, ST]) for i in range(2)]
    wt = [st.sb(f"weights{i}", [P, f.cols]) for i in range(2)]
    b2 = [st.sb(f"b2_{i}", [1, D]) for i in range(2)] if L1 else None
    hid = [st.sb(f"hidden{i}", [P, f.blocks, ST]) for i in range(2)]
    gate = [st.sb(f"gate{i}", [P, ST]) for i in range(2)] if f.gated else None
    yy = [st.sb(f"y{i}", [P, 2, D]) for i in range(2)]

    pU = [st.pb(f"pU{i}", [P, 2, ST]) for i in range(f.banks)]
    pX = st.pb("pX", [P, KC, ST])
    pY = [st.pb(f"pY{i}", [P, 2, D]) for i in range(2)]
    pR = st.pb("pR", [P, 512])

    G, NB = f.groups, f.banks
    J, JS = f.tiles, f.shared * XT
    xs = dram[f.name + "_xs"]
    yk = dram[f.name + "_yk"]
    wd = dram[f.name + "_w"]
    bc16 = lambda a: a.unsqueeze(2).to_broadcast([P, NT, E])
    bc8 = lambda a: a.unsqueeze(1).to_broadcast([P, NT, E])

    with st.ctx, nc.Block() as block:
        @block.sync
        def _(sp):
            sp.dma_start(wr[:, :, :], dram[f.name + "_router"]).then_inc(small_loaded, 16)
            n = 1
            if L1 or L3:
                sp.dma_start(rb[:, :], dram[f.name + "_rb"].partition_broadcast(P)).then_inc(small_loaded, 16)
            if L2:
                sp.dma_start(gb[:, :, :], dram["L2f_gb"].partition_broadcast(P)).then_inc(small_loaded, 16)

            def load_weights(j, par, expert):
                if not (is_int(j) and j < 2):
                    sp.wait_ge(y_ready, j - 1)
                sp.dma_start(wt[par][:, :], wd[bass.ds(expert, 1), :, :].rearrange("a p n -> (a p) n"))\
                  .then_inc(w_loaded[par], 16)
                if L1:
                    sp.dma_start(b2[par][:, :], dram["L1f_b2"][bass.ds(expert, 1), :]).then_inc(b2_loaded[par], 16)

            def load_tile(r, par):
                if not (is_int(r) and r < 2):
                    sp.wait_ge(tT_copied, r - 1)
                sp.dma_start(xin[par][:, :, :], xs[bass.ds(r * ST, ST), :].rearrange("(t p) w -> p t w", p=P))\
                  .then_inc(x_loaded[par], 16)

            for n in range(f.shared):
                if n == 0:
                    load_weights(0, 0, E)
                    load_weights(1, 1, E)
                with sp.Fori(0 if n else 1, XT // 2) as i:
                    for par in range(2):
                        load_weights(n * XT + 2 * i + par, par, E + n)
            sp.wait_ge(placed, 2)
            sp.wait_ge(dispatched, 16 * TK * NT)

            def routed_pair(i):
                for par in range(2):
                    expert = sp.value_load(te[0:1, bass.ds(2 * i + par, 1)], min_val=0, max_val=E - 1)
                    load_tile(2 * i + par, par)
                    load_weights(JS + 2 * i + par, par, expert)
            routed_pair(0)
            with sp.Fori(1, RT // 2) as i:
                routed_pair(i)
            for par in range(2):
                sp.wait_ge(y_sent[par], 16 * RT)

            for q in range(4):
                for c in range(TK):
                    sp.dma_start(rows[:, c, 4 * q:4 * q + 4, 0:D], yk[c * T + 4 * q * P:c * T + 4 * (q + 1) * P, :]
                                 .rearrange("(t p) w -> p t w", p=P)).then_inc(back_loaded[q], 16)

        @block.gpsimd
        def _(gp):
            gp.iota(rows[:, :, :, D:D + 1].bitcast(I32), [[T, TK], [P, NT], [1, 1]], base=0, channel_multiplier=1)\
              .then_inc(second, 1)
            for q in range(4):
                gp.wait_ge(xn_ready, 4 * (q + 1))
                gp.tensor_copy(rows[:, 1, 4 * q:4 * q + 4, 0:D], rows[:, 0, 4 * q:4 * q + 4, 0:D]).then_inc(second, 1)
            last_slot, rows_out = gp.to_reg(RT * ST - 1), gp.to_reg(TK * T)
            bound = gp.alloc_register(f.name + "_row_bound")
            gp.wait_ge(second, 5)
            gp.wait_ge(placed, 1)
            for c in range(TK):
                for t in range(NT):
                    gp.indirect_dma_start(xs[:, :], bass.IndirectOffsetOnAxis(ap=pos[:, c, t:t + 1], axis=0),
                                          rows[:, c, t, :], None, bounds_check=last_slot,
                                          oob_is_err=False).then_inc(dispatched, 16)

            def send(j, par):
                gp.wait_ge(y_copied, 2 * (j + 1))
                gp.reg_add(bound, rows_out, -1)
                for t in range(2):
                    gp.indirect_dma_start(yk[:, :], bass.IndirectOffsetOnAxis(
                        ap=meta[par][:, t, 0:1].bitcast(I32), axis=0), yy[par][:, t, :], None,
                        bounds_check=bound, oob_is_err=False).then_inc(y_sent[par], 16)
            with gp.Fori(JS // 2, J // 2) as i:
                send(2 * i, 0)
                send(2 * i + 1, 1)
            gp.free_register(bound)

        @block.tensor
        def _(pe):
            pe.wait_ge(small_loaded, 16 * (1 + (L1 or L3) + L2))
            for t in range(NT + 1):
                if t < NT:
                    pe.wait_ge(xn_ready, t + 1)
                    if t >= 2:
                        pe.wait_ge(xt_copied, t - 1)
                    for c in range(KC):
                        last = nc.tensor.transpose(pU[t % 2][:, 0, c * P:(c + 1) * P],
                                                   rows[:, 0, t, c * P:(c + 1) * P], k.ident[:, :])
                    last.then_inc(xt_ready, 1)
                if t == 0:
                    continue
                pe.wait_ge(xt_copied, t)
                for c in range(KC):
                    last = nc.tensor.matmul(pR[:, E * (t - 1):E * t], xT[:, c, at_tile(t - 1)], wr[:, c, :],
                                            start=(c == 0), stop=(c == KC - 1), skip_group_check=True)
            last.then_inc(logits_ready, 1)
            pe.wait_ge(chosen, 1)
            nc.tensor.matmul(pR[:, 0:P], sc[:, :, :].rearrange("p t e -> p (t e)"), k.ones[:, :],
                             start=True, stop=True).then_inc(counted, 1)
            pe.wait_ge(counted_c, 1)
            nc.tensor.matmul(pR[:, 0:P], k.before[:, :], sc[:, :, :].rearrange("p t e -> p (t e)"),
                             start=True, stop=False, skip_group_check=True)
            nc.tensor.matmul(pR[:, 0:P], tot[:, :], k.earlier[:, :, :].rearrange("p t e -> p (t e)"),
                             start=False, stop=True, skip_group_check=True)
            nc.tensor.matmul(pR[:, P:P + E], tot[:, :], k.same[:, :], start=False, stop=True,
                             skip_group_check=True).then_inc(ranked, 1)

            def transpose_tile(r, par):
                pe.wait_ge(x_loaded[par], nth(r, par))
                if not (is_int(r) and r == 0):
                    pe.wait_ge(tT_copied, r)
                for t in range(2):
                    for c in range(KC):
                        last = nc.tensor.transpose(pX[:, c, t * P:(t + 1) * P], xin[par][:, t, c * P:(c + 1) * P],
                                                   k.ident[:, :])
                last.then_inc(tT_ready, 1)

            def up(j, par, tile, routed):
                if routed:
                    pe.wait_ge(tT_copied, tile + 1)
                pe.wait_ge(w_loaded[par], nth(j, par))
                for g in range(G):
                    if not (is_int(j) and j * G + g < NB):
                        pe.wait_ge(h_ready, (1 if f.gated else 2) * (j * G + g - NB + 1))
                    bank = pU[(par * G + g) % NB]
                    for half in range(2):
                        m, blk = (half, g) if f.gated else (0, 2 * g + half)
                        for c in range(KC):
                            at = ((m * KC + c) * f.blocks + blk) * P
                            src = tT[par][:, c, :] if routed else xT[:, c, bass.ds(tile * ST, ST)]
                            last = nc.tensor.matmul(bank[:, half, :], wt[par][:, at:at + P], src,
                                                    start=(c == 0), stop=(c == KC - 1))
                    last.then_inc(up_ready, 1)

            def down(j, par):
                if not (is_int(j) and j < 2):
                    pe.wait_ge(y_copied, 2 * (j - 1))
                for t in range(2):
                    for blk in range(f.blocks):
                        if t == 0 and (f.gated or blk % 2 == 0):
                            n = blk if f.gated else blk // 2
                            pe.wait_ge(h_ready, (1 if f.gated else 2) * (j * G + n + 1))
                        last = nc.tensor.matmul(pY[par][:, t, :], hid[par][:, blk, t * P:(t + 1) * P],
                                                wt[par][:, f.up + blk * D:f.up + (blk + 1) * D],
                                                start=(blk == 0), stop=(blk == f.blocks - 1 and not L1))
                    if L1:
                        pe.wait_ge(b2_loaded[par], nth(j, par))
                        last = nc.tensor.matmul(pY[par][:, t, :], k.ones[0:1, :], b2[par][0:1, :],
                                                start=False, stop=True)
                last.then_inc(y_ready, 1)

            def pair(j0, tile0, routed, next_routed, last=False):
                for par in range(2):
                    up(j0 + par, par, tile0 + par, routed)
                    if routed and not (last and par):
                        transpose_tile(tile0 + par + 1, 1 - par)
                    elif not routed and next_routed and par:
                        transpose_tile(0, 0)
                    down(j0 + par, par)

            if not f.shared:
                transpose_tile(0, 0)
            for n in range(f.shared):
                if n == 0:
                    pair(0, 0, False, False)
                with pe.Fori(0 if n else 1, XT // 2 - 1) as i:
                    pair(n * XT + 2 * i, 2 * i, False, False)
                pair((n + 1) * XT - 2, XT - 2, False, n == f.shared - 1)
            pair(JS, 0, True, True)
            with pe.Fori(1, RT // 2 - 1) as i:
                pair(JS + 2 * i, 2 * i, True, True)
            pair(J - 2, RT - 2, True, True, last=True)

        @block.vector
        def _(v):
            link = Chain(v, dve_step)
            layer_norm_scale(nc, k, v, link, mv, sq_ready, sq_done, twice=L2)

            def normalise(src, done):
                with v.Fori(0, NT) as t:
                    at = bass.ds(t, 1)
                    nc.vector.tensor_scalar(rows[:, 0, at, 0:D], src[:, at, 0:D], mv[:, 0, at], mv[:, 1, at],
                                            ALU.mult, ALU.add).then_inc(done, 1)
            if L2:
                normalise(k.x, second_norm)
                v.wait_ge(second_norm, NT)
                v.wait_ge(small_loaded, 32)
                for q in range(4):
                    at = rows[:, 0, 4 * q:4 * q + 4, 0:D]
                    link(nc.vector.tensor_tensor(at, at, gb[:, 0:1, :].to_broadcast([P, 4, D]), ALU.mult))
                    nc.vector.tensor_tensor(at, at, gb[:, 1:2, :].to_broadcast([P, 4, D]), ALU.add)\
                      .then_inc(xn_ready, 4)
            else:
                normalise(k.x, xn_ready)

            v.wait_ge(logits_ready, 1)
            pr = pR[:, 0:P].rearrange("p (t e) -> p t e", e=E)
            if L1 or L3:
                link(nc.vector.tensor_tensor(lg[:, :, :], pr, bc8(rb[:, :]), ALU.add))
            elif L2:
                link(nc.vector.tensor_scalar(lg[:, :, :], pr, 10000.0, -10000.0, ALU.min, ALU.max))
            else:
                link(nc.vector.tensor_copy(lg[:, :, :], pr))
            m, val, e1, e2, z = r16[0], r16[1], r16[2], r16[3], r16[4]
            link(nc.vector.tensor_reduce(m[:, :], lg[:, :, :], AX.X, ALU.max))
            nc.vector.tensor_tensor(ex[:, :, :], lg[:, :, :], bc16(m[:, :]), ALU.subtract).then_inc(exp_in, 1)

            def choose(c):
                link(nc.vector.tensor_tensor(sc[:, :, :], lg[:, :, :], bc16(m[:, :]), ALU.is_equal))
                link(nc.vector.tensor_tensor(sc[:, :, :], sc[:, :, :], k.expert[:, :, :], ALU.mult))
                link(nc.vector.tensor_reduce(val[:, :], sc[:, :, :], AX.X, ALU.max))
                link(nc.vector.tensor_tensor(one[c][:, :, :], sc[:, :, :], bc16(val[:, :]), ALU.is_equal))
            choose(0)
            link(nc.vector.scalar_tensor_tensor(out=lg[:, :, :], in0=one[0][:, :, :], scalar=-1e30, in1=lg[:, :, :],
                                                op0=ALU.mult, op1=ALU.add))
            link(nc.vector.tensor_reduce(m[:, :], lg[:, :, :], AX.X, ALU.max))
            choose(1)
            nc.vector.tensor_tensor(sc[:, :, :], one[0][:, :, :], one[1][:, :, :], ALU.add).then_inc(chosen, 1)
            v.wait_ge(exp_out, 1)
            for c, out in ((0, e1), (1, e2)):
                link(nc.vector.tensor_tensor(lg[:, :, :], ex[:, :, :], one[c][:, :, :], ALU.mult))
                link(nc.vector.tensor_reduce(out[:, :], lg[:, :, :], AX.X, ALU.add))
            if not L3:
                link(nc.vector.tensor_reduce(z[:, :], ex[:, :, :], AX.X, ALU.add))
                if L2:
                    link(nc.vector.tensor_scalar(z[:, :], z[:, :], 1e-12, None, ALU.add))
                link(nc.vector.reciprocal(z[:, :], z[:, :]))
                for out in (e1, e2):
                    link(nc.vector.tensor_tensor(out[:, :], out[:, :], z[:, :], ALU.mult))
            if not L2:
                link(nc.vector.tensor_tensor(z[:, :], e1[:, :], e2[:, :], ALU.add))
                if f.name == "L0f":
                    link(nc.vector.tensor_scalar(z[:, :], z[:, :], 1e-20, None, ALU.add))
                link(nc.vector.reciprocal(z[:, :], z[:, :]))
                for out in (e1, e2):
                    link(nc.vector.tensor_tensor(out[:, :], out[:, :], z[:, :], ALU.mult))
            v.wait_ge(counted, 1)
            nc.vector.tensor_copy(tot[:, :], pR[:, 0:P]).then_inc(counted_c, 1)
            v.wait_ge(ranked, 1)
            count, tiles, end, start, ones8 = r8[0], r8[1], r8[2], r8[3], r8[4]
            link(nc.vector.tensor_scalar(count[:, :], pR[:, P:P + E], float(CAP if L2 else T), None, ALU.min))
            link(nc.vector.tensor_tensor(big8[:, :, :], count[:, :].unsqueeze(2).to_broadcast([P, E, E]),
                                         k.threshold[:, :, :], ALU.is_gt))
            link(nc.vector.tensor_reduce(tiles[:, :], big8[:, :, :], AX.X, ALU.add))
            link(nc.vector.memset(ones8[:, :], 1.0))
            link(nc.vector.tensor_tensor_scan(end[:, :], ones8[:, :], tiles[:, :], 0.0, ALU.mult, ALU.add))
            link(nc.vector.tensor_tensor(start[:, :], end[:, :], tiles[:, :], ALU.subtract))
            link(nc.vector.tensor_scalar(start[:, :], start[:, :], float(ST), None, ALU.mult))
            for c in range(TK):
                rk, seg, w = r16[5], r16[6], (e1, e2)[c]
                link(nc.vector.tensor_tensor(lg[:, :, :], pr, one[c][:, :, :], ALU.mult))
                link(nc.vector.tensor_reduce(rk[:, :], lg[:, :, :], AX.X, ALU.add))
                link(nc.vector.tensor_tensor(lg[:, :, :], one[c][:, :, :], bc8(start[:, :]), ALU.mult))
                link(nc.vector.tensor_reduce(seg[:, :], lg[:, :, :], AX.X, ALU.add))
                link(nc.vector.tensor_tensor(seg[:, :], seg[:, :], rk[:, :], ALU.add))
                if L2:
                    link(nc.vector.tensor_scalar(rk[:, :], rk[:, :], float(CAP), float(NOWHERE), ALU.is_ge, ALU.mult))
                    link(nc.vector.tensor_tensor(seg[:, :], seg[:, :], rk[:, :], ALU.add))
                link(nc.vector.tensor_copy(pos[:, c, :], seg[:, :]))
                ins = nc.vector.tensor_copy(rows[:, c, :, D + 1], w[:, :])
                if c == 0:
                    link(ins)
            ins.then_inc(placed, 1)
            link(nc.vector.tensor_tensor(bigt[:, :, :], end[:, :].unsqueeze(1).to_broadcast([P, RT, E]),
                                         k.tile_no[:, :, :], ALU.is_le))
            link(nc.vector.tensor_reduce(tef[:, :], bigt[:, :, :], AX.X, ALU.add))
            link(nc.vector.tensor_scalar(tef[:, :], tef[:, :], float(E - 1), None, ALU.min))
            nc.vector.tensor_copy(te[:, :], tef[:, :]).then_inc(placed, 1)

            def copy_tile(r, par):
                v.wait_ge(x_loaded[par], nth(r, par))
                if not (is_int(r) and r < 2):
                    v.wait_ge(y_sent[par], nth2(r, par))
                nc.vector.tensor_copy(meta[par][:, :, :], xin[par][:, :, D:XW]).then_inc(meta_copied, 1)
                v.wait_ge(tT_ready, r + 1)
                nc.vector.tensor_copy(tT[par][:, :, :], pX[:, :, :]).then_inc(tT_copied, 1)

            def gates_times(j, par):
                for g in range(G):
                    v.wait_ge(act_done, j * G + g + 1)
                    nc.vector.tensor_tensor(hid[par][:, g, :], gate[(par * G + g) % 2][:, :],
                                            pU[(par * G + g) % NB][:, 1, :], ALU.mult).then_inc(h_ready, 1)

            def take(j, par, n, routed):
                v.wait_ge(y_ready, j + 1)
                if routed:
                    v.wait_ge(meta_copied, j - JS + 1)
                for t in range(2):
                    if routed:
                        ins = nc.vector.tensor_scalar(yy[par][:, t, :], pY[par][:, t, :], meta[par][:, t, 1:2], None,
                                                      ALU.mult)
                    else:
                        at = bass.ds(2 * n + t, 1)
                        ins = nc.vector.tensor_tensor(k.x[:, at, :], k.x[:, at, :], pY[par][:, t:t + 1, :], ALU.add)
                    ins.then_inc(y_copied, 1)

            def pair(j0, n0, routed, next_routed, last=False):
                for par in range(2):
                    if f.gated:
                        gates_times(j0 + par, par)
                    if routed and not (last and par):
                        copy_tile(n0 + par + 1, 1 - par)
                    elif not routed and next_routed and par:
                        copy_tile(0, 0)
                    take(j0 + par, par, n0 + par, routed)

            if not f.shared:
                copy_tile(0, 0)
            for n in range(f.shared):
                with v.Fori(0, XT // 2 - 1) as i:
                    pair(n * XT + 2 * i, 2 * i, False, False)
                pair((n + 1) * XT - 2, XT - 2, False, n == f.shared - 1)
            pair(JS, 0, True, True)
            with v.Fori(1, RT // 2 - 1) as i:
                pair(JS + 2 * i, 2 * i, True, True)
            pair(J - 2, RT - 2, True, True, last=True)

            for q in range(4):
                v.wait_ge(back_loaded[q], 16 * TK)
                at = k.x[:, 4 * q:4 * q + 4, :]
                for c in range(TK):
                    if c:
                        v.wait_ge(back_added, 2 * q + 1)
                    nc.vector.tensor_tensor(at, at, rows[:, c, 4 * q:4 * q + 4, 0:D], ALU.add).then_inc(back_added, 1)
                if not L3:
                    v.wait_ge(back_added, 2 * q + 2)
                    token_stats(nc, k, 4 * q)
                    token_stats(nc, k, 4 * q + 2)

        @block.scalar
        def _(act):
            layer_norm_root(nc, act, mv, sq_ready, sq_done)
            for t in range(NT):
                act.wait_ge(xt_ready, t + 1)
                nc.scalar.copy(xT[:, :, at_tile(t)], pU[t % 2][:, 0, :].rearrange("p (c n) -> p c n", c=KC))\
                  .then_inc(xt_copied, 1)
            act.wait_ge(exp_in, 1)
            nc.scalar.activation(ex[:, :, :], ex[:, :, :], ACT.Exp).then_inc(exp_out, 1)

            def activate(j, par):
                for g in range(G):
                    n = j * G + g
                    act.wait_ge(up_ready, n + 1)
                    bank = pU[(par * G + g) % NB]
                    if f.gated:
                        if not (is_int(n) and n < 2):
                            act.wait_ge(h_ready, n - 1)
                        nc.scalar.activation(gate[(par * G + g) % 2][:, :], bank[:, 0, :], f.func)\
                          .then_inc(act_done, 1)
                    else:
                        for half in range(2):
                            blk = 2 * g + half
                            at = f.up + f.blocks * D + blk
                            nc.scalar.activation(hid[par][:, blk, :], bank[:, half, :], f.func,
                                                 bias=wt[par][:, at:at + 1]).then_inc(h_ready, 1)

            activate(0, 0)
            activate(1, 1)
            with act.Fori(1, J // 2) as i:
                activate(2 * i, 0)
                activate(2 * i + 1, 1)
    st.close()


class Resident:

    def __init__(self, nc, ctx):
        def sb(name, shape, dt=F32):
            return ctx.enter_context(nc.sbuf_tensor(name, shape, dt))
        self.x = sb("x_sb", [P, NT, D])
        self.attn_w = sb("attn_w_sb", [P, NW * KC, D])
        self.attn_bcol = sb("attn_bcol_sb", [P, 8])
        self.attn_brow = sb("attn_brow_sb", [1, 5, D])
        self.ident, self.ident16 = sb("ident", [P, P]), sb("ident16", [P, P], BF16)
        self.ones, self.before = sb("ones", [P, P]), sb("before", [P, P])
        self.earlier, self.same = sb("earlier", [P, NT, E]), sb("same", [P, E])
        self.expert, self.threshold = sb("expert_rev", [P, NT, E]), sb("threshold", [P, E, E])
        self.tile_no = sb("tile_no", [P, RT, E])
        self.stats = sb("stats", [P, NT, 6])
        self.row_expert = sb("row_expert", [P, 1])
        self.mask0 = sb("mask0_sb", [P, NT, S], BF16)
        self.mask2 = sb("mask2_sb", [P, B, S], BF16)
        self.causal = sb("causal", [P, QT, S], BF16)
        self.pad = sb("pad", [P, XW])


def store(nc, k, dram):
    with nc.semaphore("x_stored") as stored, nc.Block() as block:
        @block.sync
        def _(sp):
            sp.dma_start(dram["out"].rearrange("(t p) d -> p t d", p=P), k.x[:, :, :]).then_inc(stored, 16)
            sp.wait_ge(stored, 16)


STAGES = "a0 f0 a1 f1 a2 f2 a3 f3".split()


def program(nc, dram, stages=STAGES):
    for f in FFNS:
        dram[f.name + "_xs"] = nc.dram_tensor(f.name + "_xs", [RT * ST, XW], F32, kind="Internal").ap()
        dram[f.name + "_yk"] = nc.dram_tensor(f.name + "_yk", [TK * T, D], F32, kind="Internal").ap()
    dram["splits"] = nc.dram_tensor("splits", [2, 2, NPART, DH, H, S], BF16, kind="Internal").ap()
    with ExitStack() as mem:
        k = Resident(nc, mem)
        constants(nc, k, dram)
        for s in stages:
            if s == "a0":
                attention16(nc, k, dram, "L0a", L0Q, L0K, L0V, L0O, mask="pair", out_bias=4, ffn=FFNS[0])
            elif s == "a1":
                attention1(nc, k, dram, "L1a", L1Q, L1K, L1V)
            elif s == "a2":
                attention16(nc, k, dram, "L2a", L2Q, L2K, L2V, L2O, mask="batch", ffn=FFNS[2])
            elif s == "a3":
                with nc.sbuf_tensor("self_attended", [P, NT, D], F32) as h:
                    attention16(nc, k, dram, "L3a", AQ, AK, AV, AO, kv_self=True, mask="causal", bias=0, out_bias=2,
                                add=False, dst=h)
                    attention16(nc, k, dram, "L3b", BQ, BK, BV, BO, norm=False, bias=1, out_bias=3, src=h, ffn=FFNS[3])
            else:
                feed_forward(nc, k, dram, FFNS[int(s[1])])
        store(nc, k, dram)


def layout(inputs):
    import numpy as np
    a = {n: np.asarray(v) for n, v in inputs.items()}

    def chunks(w):
        return w.reshape(-1, P, w.shape[-1]).transpose(1, 0, 2)

    def heads(w):
        return w.transpose(1, 0, 2).reshape(D, D)

    out = {"x": a["x"].reshape(T, D), "mask0": a["mask_Bx1xSxS2_if1"].reshape(T, S),
           "mask1": a["mask_BxSxS2_ff0"].reshape(NT, P, S).transpose(1, 0, 2), "lens": a["_lenS2"].reshape(B),
           "ctxT": chunks(a["ctx_1024"].reshape(T, D).T)}
    mats = [a[f"L0_xattn_W{m}"].T for m in "qkvo"] + [a[f"L1_xattn_W{m}"].T for m in "qkv"] \
        + [a[f"L2_xattn_W{m}"].T for m in "qkvo"]
    for n in "12":
        mats += [heads(a[f"L3_xattn_W{m}{n}"]) for m in "qkv"] + [a[f"L3_xattn_Wo{n}"]]
    out["attn_w"] = np.concatenate([chunks(m) for m in mats], axis=1)
    cols = [a[f"L3_xattn_b{m}{n}"].reshape(KC, P).T for n in "12" for m in "qk"]
    out["attn_bcol"] = np.concatenate(cols, axis=1)
    brow = [a[f"L3_xattn_b{m}{n}"].reshape(D) for m in "vo" for n in "12"] + [a["L0_xattn_bo"]]
    out["attn_brow"] = np.stack(brow)[None]

    def ups(w, f):
        w = np.pad(w, ((0, 0), (0, f.blocks * P - w.shape[1])))
        return chunks(w).reshape(P, -1)

    def downs(w, f):
        return chunks(np.pad(w, ((0, f.blocks * P - w.shape[0]), (0, 0)))).reshape(P, -1)

    def gated(g, u, d, f):
        return np.concatenate([ups(g, f), ups(u, f), downs(d, f)], axis=1)

    f0, f1, f2, f3 = FFNS
    e0 = [gated(a["L0_ffn_wg"][e], a["L0_ffn_wu"][e], a["L0_ffn_wd"][e], f0) for e in range(E)]
    n = a["L0_ffn_swd"].shape[0] // f0.shared
    e0 += [gated(a["L0_ffn_swg"][:, n * i:n * i + n], a["L0_ffn_swu"][:, n * i:n * i + n],
                 a["L0_ffn_swd"][n * i:n * i + n], f0) for i in range(f0.shared)]
    out["L0f_w"] = np.stack(e0)
    w1 = list(a["L1_ffn_spec_w1"]) + [a["L1_ffn_shared_w1"]]
    w2 = list(a["L1_ffn_spec_w2"]) + [a["L1_ffn_shared_w2"]]
    b1 = list(a["L1_ffn_spec_b1"]) + [a["L1_ffn_shared_b1"]]
    out["L1f_w"] = np.stack([np.concatenate([ups(u.T, f1), downs(d.T, f1), b.reshape(f1.blocks, P).T], axis=1)
                             for u, d, b in zip(w1, w2, b1)])
    out["L1f_b2"] = np.concatenate([a["L1_ffn_spec_b2"], a["L1_ffn_shared_b2"][None]])
    F = f2.blocks * P
    out["L2f_w"] = np.stack([gated(w[:F].T, w[F:].T, d.T, f2) for w, d in zip(a["L2_ffn_W12"], a["L2_ffn_W3"])])
    out["L2f_gb"] = np.stack([a["L2_ffn_ln_gamma"], a["L2_ffn_ln_beta"]])
    names = [("routed_w", e) for e in range(E)] + [("shared_w", e) for e in range(f3.shared)]
    out["L3f_w"] = np.stack([gated(a[f"L3_ffn_{n}1"][e], a[f"L3_ffn_{n}3"][e], a[f"L3_ffn_{n}2"][e], f3)
                             for n, e in names])
    for f, w in zip(FFNS, (a["L0_ffn_gate_w"].T, a["L1_ffn_router_w"].T, a["L2_ffn_Wr"].T, a["L3_ffn_router_w"])):
        out[f.name + "_router"] = chunks(w)
    out["L1f_rb"], out["L3f_rb"] = a["L1_ffn_router_b"], a["L3_ffn_router_b"]
    return {n: np.ascontiguousarray(v) for n, v in out.items()}


def kernel(**inputs):
    import concourse.bacc as bacc
    from concourse.bass_utils import run_bass_kernel_spmd

    nc = bacc.Bacc("TRN2", target_bir_lowering=False, num_devices=1)
    arrays = layout(inputs)
    dram = {n: nc.dram_tensor("in_" + n, v.shape, mybir.dt.from_np(v.dtype), kind="ExternalInput").ap()
            for n, v in arrays.items()}
    dram["out"] = nc.dram_tensor("x_out", [T, D], F32, kind="ExternalOutput").ap()
    program(nc, dram)
    r = run_bass_kernel_spmd(nc, [{"in_" + n: v for n, v in arrays.items()}], core_ids=[0])
    return r.results[0]["x_out"].reshape(B, S, D)
```

```python
import concourse.bass as bass
from concourse import mybir
from contextlib import ExitStack

F32 = mybir.dt.float32
BF16 = mybir.dt.bfloat16
I32 = mybir.dt.int32
ALU = mybir.AluOpType
ACT = mybir.ActivationFunctionType
AX = mybir.AxisListType

P = 128
B, S, D = 8, 256, 256
T = B * S
NT = T // P
KC = D // P
QT = S // P
H, DH = 16, 16
HG = 4
NG = H // HG
NPART, NPROD = 3, 6
HP = 32
EPS = 1e-5
MASKED = -1e20

E = 8
TK = 2
ST = 256
RT = TK * T // ST + E
XT = T // ST
XW = D + 2
NOWHERE = 1 << 20

L0Q, L0K, L0V, L0O, L1Q, L1K, L1V, L2Q, L2K, L2V, L2O = range(11)
AQ, AK, AV, AO, BQ, BK, BV, BO = range(11, 19)
NW = 19


class Ffn:

    def __init__(self, name, blocks, gated, shared, func):
        self.name = name
        self.blocks = blocks
        self.gated = gated
        self.shared = shared
        self.func = func
        self.up = (2 if gated else 1) * KC * blocks * P
        self.b1 = 0 if gated else blocks
        self.cols = self.up + blocks * D + self.b1
        self.groups = blocks if gated else blocks // 2
        self.banks = {4: 4, 3: 3, 8: 4, 1: 2}[self.groups]
        self.tiles = shared * XT + RT
        self.capacity = None


FFNS = [Ffn("L0f", 3, True, 2, ACT.Silu), Ffn("L1f", 8, False, 1, ACT.Gelu_apprx_tanh),
        Ffn("L2f", 8, True, 0, ACT.Silu), Ffn("L3f", 1, True, 2, ACT.Silu)]
CAP = -(-(-(-T * TK * 5 // 4)) // E)
FFNS[2].capacity = CAP
FFNS[2].tiles = None


def capacity_tiles():
    out = []
    for e in range(2):
        for at in range(0, CAP, ST):
            out.append((e, e * CAP + at, min(ST, CAP - at) // P))
    return out


PAIR = capacity_tiles()
PAIR_TILES = len(PAIR)


def clear_semaphores(nc):
    nc.clear_and_free_semaphores(Stage.handles)
    Stage.handles = []
    nc.all_engine_barrier()


def is_int(n):
    return isinstance(n, int)


def nth(n, par):
    return 8 * (n - par) + 16


def nth2(n, par):
    return 16 * (n - par)


class Chain:

    def __init__(self, eng, sem):
        self.eng, self.sem, self.n = eng, sem, 0

    def __call__(self, ins):
        self.n += 1
        ins.then_inc(self.sem, 1)
        self.eng.wait_ge(self.sem, self.n)


class Stage:

    handles = []

    def __init__(self, nc, name):
        self.nc, self.name, self.ctx = nc, name, ExitStack()

    def sb(self, name, shape, dt=F32):
        return self.ctx.enter_context(self.nc.sbuf_tensor(f"{self.name}_{name}", shape, dt))

    def pb(self, name, shape, dt=F32):
        return self.ctx.enter_context(self.nc.psum_tensor(f"{self.name}_{name}", shape, dt))

    def sem(self, name):
        handle = self.nc.alloc_semaphore(name=f"{self.name}_{name}")
        Stage.handles.append(handle)
        return handle



def token_stats(nc, k, tile):
    for t in range(QT):
        at = bass.ds(tile + t, 1)
        ins = nc.vector.bn_stats(k.stats[:, at, :], k.x[:, at, :])
    return ins


def layer_norm_scale(nc, k, v, link, mv, sq_ready, sq_done, twice=False):
    gain, floor = (1.0 + EPS, EPS * EPS) if twice else (1.0, EPS)
    me, mo = k.stats[:, :, 1], k.stats[:, :, 4]
    link(nc.vector.tensor_tensor(mv[:, 2, :], me, mo, ALU.subtract))
    nc.vector.tensor_tensor(mv[:, 1, :], me, mo, ALU.add)
    link(nc.vector.tensor_tensor(mv[:, 0, :], k.stats[:, :, 2], k.stats[:, :, 5], ALU.add))
    nc.vector.tensor_tensor(mv[:, 2, :], mv[:, 2, :], mv[:, 2, :], ALU.mult)
    link(nc.vector.tensor_scalar(mv[:, 0, :], mv[:, 0, :], gain / D, floor, ALU.mult, ALU.add))
    nc.vector.scalar_tensor_tensor(out=mv[:, 3, :], in0=mv[:, 2, :], scalar=0.25 * gain, in1=mv[:, 0, :],
                                   op0=ALU.mult, op1=ALU.add).then_inc(sq_ready, 1)
    v.wait_ge(sq_done, 1)
    link(nc.vector.reciprocal(mv[:, 0, :], mv[:, 3, :]))
    link(nc.vector.scalar_tensor_tensor(out=mv[:, 1, :], in0=mv[:, 1, :], scalar=-0.5, in1=mv[:, 0, :],
                                        op0=ALU.mult, op1=ALU.mult))


def layer_norm_root(nc, act, mv, sq_ready, sq_done):
    act.wait_ge(sq_ready, 1)
    nc.scalar.activation(mv[:, 3, :], mv[:, 3, :], ACT.Sqrt).then_inc(sq_done, 1)


def constants(nc, k, dram):
    st = Stage(nc, "const")
    built, link_v, loaded = st.sem("built"), st.sem("dve_step"), st.sem("loaded")
    mask_loaded = st.sem("mask_loaded")
    raw = st.sb("mask_raw", [P, NT, S], I32)
    bits, mod8 = st.sb("row_i", [P, 1], I32), st.sb("row_mod_8", [P, 1], I32)
    with st.ctx, nc.Block() as block:
        @block.sync
        def _(sp):
            sp.dma_start(raw[:, :, :], dram["mask0"].rearrange("(t p) s -> p t s", p=P)).then_inc(mask_loaded, 16)
            sp.dma_start(k.x[:, :, :], dram["x"].rearrange("(t p) d -> p t d", p=P)).then_inc(loaded, 16)
            n = 4 * KC
            sp.dma_start(k.attn_w[:, 0:n, :], dram["attn_w"][:, 0:n, :]).then_inc(loaded, 16)
            sp.dma_start(k.attn_brow[:, :, :], dram["attn_brow"]).then_inc(loaded, 16)
            sp.wait_ge(loaded, 3 * 16)

        @block.gpsimd
        def _(gp):
            link = Chain(gp, built)
            link(nc.gpsimd.iota(bits[:, :], [[0, 1]], base=0, channel_multiplier=1))
            link(nc.gpsimd.memset(k.ident[:, :], 0.0))
            link(nc.gpsimd.affine_select(out=k.ident[:, :], in_=k.ident[:, :], compare_op=ALU.not_equal, fill=1.0,
                                         base=0, pattern=[[-1, P]], channel_multiplier=1))
            link(nc.gpsimd.memset(k.ones[:, :], 1.0))
            link(nc.gpsimd.memset(k.pad[:, 0:D], 0.0))
            link(nc.gpsimd.memset(k.pad[:, D:D + 1].bitcast(I32), NOWHERE))
            link(nc.gpsimd.memset(k.pad[:, D + 1:XW], 0.0))

        @block.vector
        def _(v):
            link = Chain(v, link_v)
            v.wait_ge(built, 3)
            link(nc.vector.tensor_scalar(mod8[:, :], bits[:, :], E - 1, None, ALU.bitwise_and))
            link(nc.vector.tensor_copy(k.row_expert[:, :], mod8[:, :]))
            link(nc.vector.tensor_copy(k.ident16[:, :], k.ident[:, :]))
            v.wait_ge(loaded, 3 * 16)
            for t in range(NT):
                ins = nc.vector.bn_stats(k.stats[:, t, :], k.x[:, t, :])
            link(ins)
            v.wait_ge(mask_loaded, 16)
            link(nc.vector.tensor_scalar(k.mask0[:, :, :], raw[:, :, :], 0.0, MASKED, ALU.is_equal, ALU.mult))


def bias_parts(nc, k, gp, st, stacked):
    link = Chain(gp, st.sem("bias_step"))
    parts, left = st.sb("bias_parts", [1, NPART, 5, D], BF16), st.sb("bias_left", [1, 5, D])
    link(nc.gpsimd.memset(k.ones16[:, :], 1.0))
    link(nc.gpsimd.tensor_copy(parts[:, 0, :, :], k.attn_brow[:, :, :]))
    link(nc.gpsimd.tensor_tensor(left[:, :, :], k.attn_brow[:, :, :], parts[:, 0, :, :], ALU.subtract))
    link(nc.gpsimd.tensor_copy(parts[:, 1, :, :], left[:, :, :]))
    link(nc.gpsimd.tensor_tensor(parts[:, 2, :, :], left[:, :, :], parts[:, 1, :, :], ALU.subtract))
    for i in range(NPART):
        gp.dma_start(k.brow3[i:i + 1, :, :], parts[0:1, i, :, :]).then_inc(stacked, 16)
    gp.wait_ge(stacked, 16 * NPART)


def late_constants(nc, k, dram, gp, st, lens_loaded):
    built = st.sem("late_built")
    lens = st.sb("lens_raw", [P, B], I32)
    lensf = st.sb("lens", [P, B])
    keys = st.sb("key_index", [P, S], I32)
    keysf = st.sb("key_index_f", [P, S])
    expi = st.sb("expert_i", [P, NT, E], I32)
    thri = st.sb("threshold_i", [P, E, E], I32)
    tili = st.sb("tile_i", [P, RT, E], I32)
    link = Chain(gp, built)
    g = nc.gpsimd
    link(g.memset(k.before[:, :], 0.0))
    link(g.affine_select(out=k.before[:, :], in_=k.before[:, :], compare_op=ALU.is_ge, fill=1.0,
                         base=0, pattern=[[-1, P]], channel_multiplier=1))
    link(g.memset(k.causal[:, :, :], 0.0))
    for qt in range(QT):
        link(g.affine_select(out=k.causal[:, qt, :], in_=k.causal[:, qt, :], compare_op=ALU.is_ge,
                             fill=MASKED, base=P * qt, pattern=[[-1, S]], channel_multiplier=1))
    link(g.iota(keys[:, :], [[1, S]], base=0, channel_multiplier=0))
    link(g.iota(expi[:, :, :], [[0, NT], [1, E]], base=0, channel_multiplier=0))
    link(g.iota(thri[:, :, :], [[0, E], [ST, E]], base=0, channel_multiplier=0))
    link(g.iota(tili[:, :, :], [[1, RT], [0, E]], base=0, channel_multiplier=0))
    link(g.memset(k.earlier[:, :, :], 1.0))
    link(g.affine_select(out=k.earlier[:, :, :], in_=k.earlier[:, :, :], compare_op=ALU.is_gt,
                         fill=0.0, base=0, pattern=[[E, NT], [0, E]], channel_multiplier=-1))
    link(g.tensor_copy(k.expert[:, :, :], expi[:, :, :]))
    link(g.tensor_scalar(k.same[:, :], k.expert[:, 0, :], k.row_expert[:, 0:1], None, ALU.is_equal))
    link(g.tensor_tensor(k.earlier[:, :, :], k.earlier[:, :, :],
                         k.same[:, :].unsqueeze(1).to_broadcast([P, NT, E]), ALU.mult))
    link(g.tensor_scalar(k.expert[:, :, :], k.expert[:, :, :], -1.0, float(E), ALU.mult, ALU.add))
    link(g.tensor_copy(k.threshold[:, :, :], thri[:, :, :]))
    link(g.tensor_copy(k.tile_no[:, :, :], tili[:, :, :]))
    gp.dma_start(lens[:, :], dram["lens"].partition_broadcast(P)).then_inc(lens_loaded, 16)
    gp.wait_ge(lens_loaded, 16)
    link(g.tensor_copy(lensf[:, :], lens[:, :]))
    link(g.tensor_copy(keysf[:, :], keys[:, :]))
    for b in range(B):
        link(g.tensor_scalar(k.mask2[:, b, :], keysf[:, :], lensf[:, b:b + 1], MASKED, ALU.is_ge, ALU.mult))


def attention16(nc, k, dram, name, wq, wk, wv, wo, kv_self=False, norm=True, mask=None, bias=None, out_bias=None,
                add=True, src=None, dst=None, ffn=None):
    st = Stage(nc, name)
    sem = st.sem
    ln_step, sq_ready, sq_done = sem("ln_step"), sem("sq_ready"), sem("sq_done")
    ctx_loaded, xn_ready = [sem(f"ctx{i}_loaded") for i in range(2)], sem("xn_ready")
    xT_ready, xT_copied = sem("xT_ready"), sem("xT_copied")
    q_ready, q_copied = sem("q_ready"), sem("q_copied")
    k_ready, k_copied = sem("k_ready"), sem("k_copied")
    v_ready, v_copied = sem("v_ready"), sem("v_copied")
    split_step, split_done, parts_written = [sem("q_split_step"), sem("k_split_step")], [sem("q_split"), sem("k_split")], \
        [sem("q_parts_written"), sem("k_parts_written")]
    stacked = [[sem(f"{n}_stacked{i}") for i in range(2)] for n in "qk"]
    s_ready, max_ready, negmax_ready = sem("scores_ready"), sem("max_ready"), sem("negmax_ready")
    p_ready = sem("probs_ready")
    pt_ready, pt_copied_v, pt_copied_a = sem("probsT_ready"), sem("probsT0_copied"), sem("probsT1_copied")
    pv_ready, o_copied = sem("pv_ready"), sem("o_copied")
    ot_ready, rs_ready, on_ready = sem("otok_ready"), sem("recip_ready"), sem("onorm_ready")
    ont_ready, ont_copied = sem("onormT_ready"), sem("onormT_copied")
    y_ready, y_added = sem("y_ready"), sem("y_added")
    pads, v_padded = sem("pads_written"), sem("v_padded")
    first_stage = name == "L0a"
    if first_stage:
        late_loaded, lens_loaded, bias_stacked = sem("late_loaded"), sem("lens_loaded"), sem("bias_stacked")

    mask_row = mask == "batch"
    ROWS = NPROD * DH + mask_row

    def stacked_value(x, b, par):
        n = 3 + (mask_row and x == 1)
        return 8 * n * (b - par) + 16 * n

    def key_tiles(sl):
        return 1 if mask == "causal" and sl < NG else QT

    mv = st.sb("mv", [P, 4, NT])
    ctxT = [st.sb(f"ctxT{i}", [P, KC, S]) for i in range(2)]
    xn = [st.sb(f"xn{i}", [P, QT, D]) for i in range(2)]
    xT = st.sb("xT", [P, KC, S])
    qT = [st.sb(f"qT{i}", [P, 2, S]) for i in range(2)]
    kT = [st.sb(f"kT{i}", [P, 2, S]) for i in range(2)]
    rest = [st.sb(f"rest{i}", [P, 2, S]) for i in range(2)]
    parts = [st.sb(f"parts{i}", [P, NPART, 2, S], BF16) for i in range(2)]
    q6 = [st.sb(f"q6_{i}", [ROWS, H, S], BF16) for i in range(2)]
    k6 = [st.sb(f"k6_{i}", [ROWS, H, S], BF16) for i in range(2)]
    vv = [st.sb(f"v{i}", [P, QT, H, HP]) for i in range(2)]
    probs = [st.sb(f"probs{i}", [P, HG, S]) for i in range(2)]
    probsT = [st.sb(f"probsT{i}", [P, QT, HG, P]) for i in range(2)]
    rowmax = [st.sb(f"max{i}", [P, HG]) for i in range(2)]
    negmax = [st.sb(f"negmax{i}", [P, HG]) for i in range(2)]
    osum = st.sb("o", [P, NG, P])
    recip = st.sb("recip", [P, H])
    onorm = st.sb("onorm", [P, H, DH])
    onormT = st.sb("onormT", [P, KC, P])
    pS = [st.pb(f"pS{i}", [P, HG, S]) for i in range(2)]
    pT = [st.pb(f"pT{i}", [P, HG, P]) for i in range(2)]
    pO = st.pb("pO", [P, NG, P])
    pM = st.pb("pM", [P, 512])
    pM2 = pM[:, :].rearrange("p (a n) -> p a n", a=2)

    SLOTS = QT * NG
    scale = DH ** -0.5
    W = k.attn_w
    splits = dram["splits"]

    zero = k.pad[:, 0:S].unsqueeze(1).to_broadcast([P, 2, S])

    def split(eng, b, par, x):
        src, out, left, step = (qT, kT)[x][par][:, :, :], parts[x], rest[x][:, :, :], split_step[x]
        eng.wait_ge((q_copied, k_copied)[x], b + 1)
        if not (is_int(b) and b == 0):
            eng.wait_ge(parts_written[x], 48 * b)
        eng.tensor_tensor(out[:, 0, :, :], src, zero, ALU.add).then_inc(step, 1)
        eng.wait_ge(step, 3 * b + 1)
        eng.tensor_tensor(left, src, out[:, 0, :, :], ALU.subtract).then_inc(step, 1)
        eng.wait_ge(step, 3 * b + 2)
        eng.tensor_tensor(out[:, 1, :, :], left, zero, ALU.add).then_inc(step, 1)
        eng.wait_ge(step, 3 * b + 3)
        eng.tensor_tensor(out[:, 2, :, :], left, out[:, 1, :, :], ALU.subtract).then_inc(split_done[x], 1)

    with st.ctx, nc.Block() as block:
        @block.sync
        def _(sp):
            def load(b, par, waits):
                if waits:
                    sp.wait_ge(v_ready, b - 1)
                sp.dma_start(ctxT[par][:, :, :], dram["ctxT"][:, :, bass.ds(b * S, S)]).then_inc(ctx_loaded[par], 16)

            def stack(b, par, x):
                sp.wait_ge(split_done[x], b + 1)
                for part in range(NPART):
                    sp.dma_start(splits[x, par, part, :, :, :].rearrange("d (f h) s -> h d f s", f=2),
                                 parts[x][:, part, :, :]).then_inc(parts_written[x], 16)
                to = (q6, k6)[x][par]
                if mask_row and x:
                    row = k.mask2[0:1, bass.ds(b, 1), :].to_broadcast([1, H, S])
                    sp.dma_start(to[ROWS - 1:ROWS, :, :], row).then_inc(stacked[x][par], 16)
                sp.wait_ge(parts_written[x], 48 * (b + 1))
                at = 0
                for n in (3, 2, 1):
                    part = 0 if x else 3 - n
                    src = splits[x, par, part:part + n if x else part + 1].rearrange("r d h s -> r d (h s)")
                    if not x:
                        src = src.to_broadcast([n, DH, H * S])
                    sp.dma_start(to[at:at + n * DH, :, :].rearrange("p h s -> p (h s)"), src)\
                      .then_inc(stacked[x][par], 16)
                    at += n * DH

            if not kv_self:
                load(0, 0, False)
                load(1, 1, False)
                stack(0, 0, 1)
            stack(0, 0, 0)
            if kv_self:
                stack(0, 0, 1)
            def pair(i, pars=(1, 0)):
                for par in pars:
                    b = 2 * i + 2 - par
                    if not kv_self:
                        load(b + 1, 1 - par, True)
                    stack(b, par, 1)
                    stack(b, par, 0)

            for par in (1, 0):
                pair(0, (par,))
                if first_stage:
                    n = (NW - 4) * KC // 2
                    at = 4 * KC + (1 - par) * n
                    sp.dma_start(k.attn_w[:, at:at + n, :], dram["attn_w"][:, at:at + n, :]).then_inc(late_loaded, 16)
            if first_stage:
                sp.dma_start(k.attn_bcol[:, :], dram["attn_bcol"]).then_inc(late_loaded, 16)
            if ffn is not None:
                fills = [(dram[ffn.name + "_xs"], XW)]
                if ffn.name == "L2f":
                    fills.append((dram["L2f_yk"], D))
            with sp.Fori(1, B // 2 - 1) as i:
                for par in (1, 0):
                    pair(i, (par,))
                    if ffn is not None:
                        for rows, w in fills:
                            n = rows.shape[0] // 4
                            sp.dma_start(rows[bass.ds((2 * i - 1 - par) * n, n), :]
                                         .rearrange("(n p) w -> p n w", p=P),
                                         k.pad[:, 0:w].unsqueeze(1).to_broadcast([P, n // P, w])).then_inc(pads, 16)
            stack(B - 1, 1, 1)
            stack(B - 1, 1, 0)
            if ffn is not None:
                sp.wait_ge(pads, 4 * 16 * len(fills))
            if first_stage:
                sp.wait_ge(late_loaded, 3 * 16)

        @block.gpsimd
        def _(gp):
            if first_stage:
                bias_parts(nc, k, gp, st, bias_stacked)
            split(gp, 0, 0, 0)
            split(gp, 1, 1, 0)
            split(gp, 2, 0, 0)
            if first_stage:
                late_constants(nc, k, dram, gp, st, lens_loaded)
            with gp.Fori(1, B // 2 - 1) as i:
                split(gp, 2 * i + 1, 1, 0)
                split(gp, 2 * i + 2, 0, 0)
            split(gp, B - 1, 1, 0)

        @block.tensor
        def _(pe):
            def project_x(b, par):
                pe.wait_ge(xn_ready, b + 1)
                for t in range(QT):
                    for c in range(KC):
                        last = nc.tensor.transpose(pM2[:, c, t * P:(t + 1) * P],
                                                   xn[par][:, t, c * P:(c + 1) * P], k.ident[:, :])
                last.then_inc(xT_ready, 1)

            def project_q(b, par):
                pe.wait_ge(xT_copied, b + 1)
                for f in range(2):
                    for c in range(KC):
                        last = nc.tensor.matmul(pM2[:, f, :], W[:, wq * KC + c, f * P:(f + 1) * P], xT[:, c, :],
                                                start=(c == 0), stop=(c == KC - 1))
                last.then_inc(q_ready, 1)

            def project_k(b, par):
                if not kv_self:
                    pe.wait_ge(ctx_loaded[par], nth(b, par))
                kv = xT if kv_self else ctxT[par]
                for f in range(2):
                    for c in range(KC):
                        last = nc.tensor.matmul(pM2[:, f, :], W[:, wk * KC + c, f * P:(f + 1) * P], kv[:, c, :],
                                                start=(c == 0), stop=(c == KC - 1))
                last.then_inc(k_ready, 1)

            def project_v(b, par):
                kv = xT if kv_self else ctxT[par]
                for t in range(QT):
                    for c in range(KC):
                        last = nc.tensor.matmul(pM2[:, t, :], kv[:, c, t * P:(t + 1) * P], W[:, wv * KC + c, :],
                                                start=(c == 0), stop=(c == KC - 1 and bias is None))
                    if bias is not None:
                        last = nc.tensor.matmul(pM2[:, t, :], k.ones16[0:NPART, :], k.brow3[0:NPART, bias, :],
                                                start=False, stop=True)
                last.then_inc(v_ready, 1)

            def scores(s, b, par, sl):
                qt, g = divmod(sl, NG)
                if mask_row and is_int(s) and s < 1:
                    pe.wait_ge(v_padded, 6)
                if sl == 0:
                    for x in range(2):
                        pe.wait_ge(stacked[x][par], stacked_value(x, b, par))
                if not (is_int(s) and s < 2):
                    pe.wait_ge(p_ready, HG * (s - 1))
                out = pS[sl % 2]
                keys = key_tiles(sl) * P
                if mask == "pair":
                    for j in range(HG):
                        nc.tensor.matmul(out[:, j, :], k.ident16[:, :], k.mask0[:, bass.ds(b * QT + qt, 1), :],
                                         start=(j % 2 == 0), stop=False, skip_group_check=True)
                for j in range(HG):
                    h = HG * g + j
                    last = nc.tensor.matmul(out[:, j, 0:keys], q6[par][:, h, qt * P:(qt + 1) * P],
                                            k6[par][:, h, 0:keys], start=(mask != "pair" and j % 2 == 0),
                                            stop=(mask != "causal"), skip_group_check=True)
                if mask == "causal":
                    for j in range(HG):
                        diagonal = slice(qt * P, (qt + 1) * P)
                        last = nc.tensor.matmul(out[:, j, diagonal], k.ident16[:, :], k.causal[:, qt, diagonal],
                                                start=False, stop=True, skip_group_check=True)
                last.then_inc(s_ready, 1)

            def transpose_probs(s, sl, b):
                pe.wait_ge(p_ready, HG * (s + 1))
                for t in range(key_tiles(sl)):
                    if t == 1 and mask == "causal":
                        if not (is_int(b) and b == 0 and sl == NG):
                            pe.wait_ge(pt_copied_a, NG * b + sl - NG)
                    elif not (is_int(s) and s == 0):
                        pe.wait_ge(pt_copied_v if t == 0 else pt_copied_a, s)
                    for j in range(HG):
                        last = nc.tensor.transpose(pT[t][:, j, :], probs[sl % 2][:, j, t * P:(t + 1) * P],
                                                   k.ident[:, :])
                    last.then_inc(pt_ready, QT // key_tiles(sl))

            def weighted(s, u, sl, par):
                g = sl % NG
                pe.wait_ge(pt_copied_v, s + 1)
                if mask != "causal":
                    pe.wait_ge(pt_copied_a, s + 1)
                elif key_tiles(sl) == QT:
                    pe.wait_ge(pt_copied_a, 2 * u + g - 1)
                if is_int(s) and s == 0:
                    pe.wait_ge(v_padded, 4 + 2 * mask_row)
                if g == 0 and not (is_int(u) and u == 0):
                    pe.wait_ge(o_copied, u)
                for t in range(key_tiles(sl)):
                    for j in range(HG):
                        last = nc.tensor.matmul(pO[HP * j:HP * (j + 1), g, :], vv[par][:, t, HG * g + j, :],
                                                probsT[sl % 2][:, t, j, :], start=(g == 0 and t == 0),
                                                stop=(t == key_tiles(sl) - 1), skip_group_check=True)
                if g == NG - 1:
                    last.then_inc(pv_ready, 1)

            def tokens_of_o(u):
                pe.wait_ge(o_copied, u + 1)
                for g in range(NG):
                    last = nc.tensor.transpose(pM[:, g * P:(g + 1) * P], osum[:, g, :], k.ident[:, :])
                last.then_inc(ot_ready, 1)

            def features_of_o(u):
                pe.wait_ge(on_ready, u + 1)
                for c in range(KC):
                    last = nc.tensor.transpose(pM[:, c * P:(c + 1) * P],
                                               onorm[:, 8 * c:8 * c + 8, :].rearrange("p h d -> p (h d)"),
                                               k.ident[:, :])
                last.then_inc(ont_ready, 1)

            def output(u):
                pe.wait_ge(ont_copied, u + 1)
                for c in range(KC):
                    last = nc.tensor.matmul(pM2[:, 0, :], onormT[:, c, :], W[:, wo * KC + c, :],
                                            start=(c == 0), stop=(c == KC - 1 and out_bias is None))
                if first_stage and is_int(u) and u == 0:
                    pe.wait_ge(bias_stacked, 16 * NPART)
                if out_bias is not None:
                    last = nc.tensor.matmul(pM2[:, 0, :], k.ones16[0:NPART, :], k.brow3[0:NPART, out_bias, :],
                                            start=False, stop=True)
                last.then_inc(y_ready, 1)

            def batch(b, par, first, last):
                between = not first and not last
                x_ahead = not last and not (is_int(b) and b == B - 2)
                for sl in range(SLOTS):
                    s = b * SLOTS + sl
                    u = b * QT
                    if sl < SLOTS - 2:
                        scores(s + 2, b, par, sl + 2)
                    elif not last:
                        scores(s + 2, b + 1, 1 - par, sl + 2 - SLOTS)
                    transpose_probs(s, sl, b)
                    if sl == 0 and between:
                        pe.wait_ge(xT_copied, b + 2)
                        project_k(b + 1, 1 - par)
                    if sl == 1 and not first:
                        if last:
                            pe.wait_ge(y_added, u - 1)
                        else:
                            pe.wait_ge(q_copied, b + 2)
                        tokens_of_o(u - 1)
                    if sl == 2 and not first:
                        features_of_o(u - 1)
                    if sl == 3 and not first:
                        output(u - 1)
                    if sl == 5:
                        if first:
                            pe.wait_ge(v_copied, b + 2)
                        else:
                            pe.wait_ge(y_added, u)
                        tokens_of_o(u)
                    if sl == 6:
                        features_of_o(u)
                    if sl == 7:
                        if between:
                            pe.wait_ge(v_copied, b + 2)
                        output(u)
                    if not (first and sl == 0):
                        weighted(s - 1, u + (sl - 1) // NG, (sl - 1) % SLOTS, par if sl else 1 - par)
                    if sl == 0 and between:
                        pe.wait_ge(k_copied, b + 2)
                        project_q(b + 1, 1 - par)
                    if sl == SLOTS - 1 and x_ahead:
                        pe.wait_ge(y_added, u + 1)
                        project_x(b + 2, par)
                    if sl == 6 and between:
                        pe.wait_ge(ont_copied, u + 1)
                        project_v(b + 1, 1 - par)

            def project_kv():
                project_k(0, 0)
                pe.wait_ge(k_copied, 1)
                project_v(0, 0)

            if kv_self:
                project_x(0, 0)
                project_q(0, 0)
                pe.wait_ge(q_copied, 1)
                project_kv()
            else:
                project_kv()
                pe.wait_ge(v_copied, 1)
                project_x(0, 0)
                project_q(0, 0)
            pe.wait_ge(v_copied if kv_self else q_copied, 1)
            project_x(1, 1)
            pe.wait_ge(xT_copied, 2)
            project_k(1, 1)
            pe.wait_ge(k_copied, 2)
            project_q(1, 1)
            pe.wait_ge(q_copied, 2)
            project_v(1, 1)
            scores(0, 0, 0, 0)
            scores(1, 0, 0, 1)
            batch(0, 0, True, False)
            batch(1, 1, False, False)
            with pe.Fori(1, B // 2 - 1) as i:
                batch(2 * i, 0, False, False)
                batch(2 * i + 1, 1, False, False)
            batch(B - 2, 0, False, False)
            batch(B - 1, 1, False, True)
            U = B * QT
            weighted(B * SLOTS - 1, U - 1, SLOTS - 1, 1)
            pe.wait_ge(y_added, U - 1)
            tokens_of_o(U - 1)
            features_of_o(U - 1)
            output(U - 1)

        @block.vector
        def _(v):
            def normalise(b, par):
                if not (is_int(b) and b < 2):
                    v.wait_ge(xT_ready, b - 1)
                for t in range(QT):
                    at = bass.ds(b * QT + t, 1)
                    if norm:
                        ins = nc.vector.tensor_scalar(xn[par][:, t, :], k.x[:, at, :], mv[:, 0, at],
                                                      mv[:, 1, at], ALU.mult, ALU.add)
                    else:
                        ins = nc.vector.tensor_copy(xn[par][:, t, :], src[:, at, :])
                ins.then_inc(xn_ready, 1)

            def copy_xT(b, par):
                v.wait_ge(xT_ready, b + 1)
                nc.vector.tensor_copy(xT[:, :, :], pM2).then_inc(xT_copied, 1)

            def copy_k(b, par):
                v.wait_ge(k_ready, b + 1)
                if not (is_int(b) and b < 2):
                    v.wait_ge(split_done[1], b - 1)
                if bias is None:
                    nc.vector.tensor_copy(kT[par][:, :, :], pM2).then_inc(k_copied, 1)
                else:
                    for f in range(2):
                        at = 4 * bias + 2 + f
                        ins = nc.vector.tensor_scalar(kT[par][:, f, :], pM2[:, f, :], k.attn_bcol[:, at:at + 1], None,
                                                      ALU.add)
                    ins.then_inc(k_copied, 1)

            def maxima(s, sl):
                v.wait_ge(s_ready, s + 1)
                nc.vector.tensor_reduce(rowmax[sl % 2][:, :], pS[sl % 2][:, :, 0:key_tiles(sl) * P], AX.X, ALU.max)\
                  .then_inc(max_ready, 1)
                v.wait_ge(max_ready, s + 1)
                nc.vector.tensor_scalar(negmax[sl % 2][:, :], rowmax[sl % 2][:, :], -scale, None, ALU.mult)\
                  .then_inc(negmax_ready, 1)

            def copy_probsT(s, sl):
                v.wait_ge(pt_ready, 2 * s + 1)
                nc.vector.tensor_copy(probsT[sl % 2][:, 0, :, :], pT[0][:, :, :]).then_inc(pt_copied_v, 1)

            def normalise_o(u):
                v.wait_ge(ot_ready, u + 1)
                o = pM[:, :].rearrange("p (h d) -> p h d", d=HP)
                nc.vector.reciprocal(recip[:, :], o[:, :, DH]).then_inc(rs_ready, 1)
                v.wait_ge(rs_ready, u + 1)
                nc.vector.tensor_tensor(onorm[:, :, :], o[:, :, 0:DH],
                                        recip[:, :].unsqueeze(2).to_broadcast([P, H, DH]), ALU.mult)\
                  .then_inc(on_ready, 1)

            def take_output(u):
                v.wait_ge(y_ready, u + 1)
                at = bass.ds(u, 1)
                if add:
                    nc.vector.tensor_tensor(k.x[:, at, :], k.x[:, at, :], pM2[:, 0:1, :], ALU.add)\
                      .then_inc(y_added, 1)
                else:
                    nc.vector.tensor_copy(dst[:, at, :], pM2[:, 0:1, :]).then_inc(y_added, 1)

            def batch(b, par, first, last):
                for sl in range(SLOTS):
                    s = b * SLOTS + sl
                    u = b * QT
                    if not (last and sl >= SLOTS - 2):
                        maxima(s + 2, (sl + 2) % SLOTS)
                    if sl == 4 and add and not first:
                        v.wait_ge(y_added, u)
                    copy_probsT(s, sl)
                    if sl == 4 and add and not first:
                        token_stats(nc, k, u - QT)
                    if sl == 0 and not first and not last:
                        copy_k(b + 1, 1 - par)
                        split(v, b + 1, 1 - par, 1)
                    if sl == 1 and not first:
                        normalise_o(u - 1)
                    if sl == 3 and not first:
                        take_output(u - 1)
                    if sl == 5:
                        normalise_o(u)
                    if sl == 7:
                        take_output(u)
                        if not last and not (is_int(b) and b == B - 2):
                            copy_xT(b + 2, par)
                    if sl == 3 and not last and not (is_int(b) and b == B - 2):
                        normalise(b + 2, par)

            for par in range(2):
                if mask_row:
                    nc.vector.memset(q6[par][ROWS - 1:ROWS, :, :], 1.0).then_inc(v_padded, 1)
                nc.vector.memset(vv[par][:, :, :, DH + 1:HP], 0.0).then_inc(v_padded, 1)
                nc.vector.memset(vv[par][:, :, :, DH:DH + 1], 1.0).then_inc(v_padded, 1)
            if not kv_self:
                copy_k(0, 0)
                split(v, 0, 0, 1)
            if norm:
                layer_norm_scale(nc, k, v, Chain(v, ln_step), mv, sq_ready, sq_done)
            normalise(0, 0)
            normalise(1, 1)
            copy_xT(0, 0)
            if kv_self:
                copy_k(0, 0)
                split(v, 0, 0, 1)
            copy_xT(1, 1)
            copy_k(1, 1)
            split(v, 1, 1, 1)
            maxima(0, 0)
            maxima(1, 1)
            batch(0, 0, True, False)
            batch(1, 1, False, False)
            with v.Fori(1, B // 2 - 1) as i:
                batch(2 * i, 0, False, False)
                batch(2 * i + 1, 1, False, False)
            batch(B - 2, 0, False, False)
            batch(B - 1, 1, False, True)
            normalise_o(B * QT - 1)
            take_output(B * QT - 1)
            if add:
                v.wait_ge(y_added, B * QT)
                token_stats(nc, k, (B - 1) * QT)

        @block.scalar
        def _(act):
            def copy_q(b, par):
                act.wait_ge(q_ready, b + 1)
                if not (is_int(b) and b < 2):
                    act.wait_ge(split_done[0], b - 1)
                if bias is None:
                    nc.scalar.copy(qT[par][:, :, :], pM2).then_inc(q_copied, 1)
                else:
                    for f in range(2):
                        at = 4 * bias + f
                        ins = nc.scalar.activation(qT[par][:, f, :], pM2[:, f, :], ACT.Identity,
                                                   bias=k.attn_bcol[:, at:at + 1])
                    ins.then_inc(q_copied, 1)

            def copy_v(b, par):
                act.wait_ge(v_ready, b + 1)
                nc.scalar.copy(vv[par][:, :, :, 0:DH].rearrange("p t h d -> p (t h) d"),
                               pM[:, :].rearrange("p (n d) -> p n d", d=DH)).then_inc(v_copied, 1)

            def probabilities(s, sl):
                act.wait_ge(negmax_ready, s + 1)
                if not (is_int(s) and s < 2):
                    act.wait_ge(pt_ready, 2 * (s - 1))
                n = key_tiles(sl) * P
                for j in range(HG):
                    nc.scalar.activation(probs[sl % 2][:, j, 0:n], pS[sl % 2][:, j, 0:n], ACT.Exp,
                                         bias=negmax[sl % 2][:, j:j + 1], scale=scale).then_inc(p_ready, 1)

            def copy_probsT(s, sl):
                if key_tiles(sl) < QT:
                    return
                act.wait_ge(pt_ready, 2 * (s + 1))
                nc.scalar.copy(probsT[sl % 2][:, 1, :, :], pT[1][:, :, :]).then_inc(pt_copied_a, 1)

            def copy_o(u):
                act.wait_ge(pv_ready, u + 1)
                nc.scalar.copy(osum[:, :, :], pO[:, :, :]).then_inc(o_copied, 1)

            def copy_onormT(u):
                act.wait_ge(ont_ready, u + 1)
                nc.scalar.copy(onormT[:, :, :], pM2[:, 0, :].rearrange("p (c n) -> p c n", c=KC))\
                  .then_inc(ont_copied, 1)

            def batch(b, par, first, last):
                for sl in range(SLOTS):
                    s = b * SLOTS + sl
                    u = b * QT
                    if not (last and sl == SLOTS - 1):
                        probabilities(s + 1, (sl + 1) % SLOTS)
                    copy_probsT(s, sl)
                    if sl == 2 and not first:
                        copy_onormT(u - 1)
                    if sl == 6:
                        copy_onormT(u)
                    if sl == 0 and not first:
                        copy_o(u - 1)
                        if not last:
                            copy_q(b + 1, 1 - par)
                    if sl == 4:
                        copy_o(u)
                    if sl == 6 and not first and not last:
                        copy_v(b + 1, 1 - par)

            if not kv_self:
                copy_v(0, 0)
            if norm:
                layer_norm_root(nc, act, mv, sq_ready, sq_done)
            copy_q(0, 0)
            if kv_self:
                copy_v(0, 0)
            copy_q(1, 1)
            copy_v(1, 1)
            probabilities(0, 0)
            batch(0, 0, True, False)
            batch(1, 1, False, False)
            with act.Fori(1, B // 2 - 1) as i:
                batch(2 * i, 0, False, False)
                batch(2 * i + 1, 1, False, False)
            batch(B - 2, 0, False, False)
            batch(B - 1, 1, False, True)
            copy_o(B * QT - 1)
            copy_onormT(B * QT - 1)


def attention1(nc, k, dram, name, wq, wk, wv):
    st = Stage(nc, name)
    sem = st.sem
    ln_step, sq_ready, sq_done = sem("ln_step"), sem("sq_ready"), sem("sq_done")
    ctx_loaded, mask_loaded = [sem(f"ctx{i}_loaded") for i in range(2)], [sem(f"mask{i}_loaded") for i in range(2)]
    xn_ready = sem("xn_ready")
    xT_ready, xT_copied = sem("xT_ready"), sem("xT_copied")
    q_ready, q_copied = sem("q_ready"), sem("q_copied")
    k_ready, k_copied = sem("k_ready"), sem("k_copied")
    v_ready, v_copied = sem("v_ready"), sem("v_copied")
    s_ready, s_masked, negmax_ready = sem("scores_ready"), sem("scores_masked"), sem("negmax_ready")
    p_ready, pt_ready, pt_copied = sem("probs_ready"), sem("probsT_ready"), sem("probsT_copied")
    o_ready, recip_ready, o_scaled, o_added = sem("o_ready"), sem("recip_ready"), sem("o_scaled"), sem("o_added")
    pads = sem("pads_written")

    mv = st.sb("mv", [P, 4, NT])
    ctxT = [st.sb(f"ctxT{i}", [P, KC, S]) for i in range(2)]
    bias = [st.sb(f"mask{i}", [P, QT, S]) for i in range(2)]
    xn = [st.sb(f"xn{i}", [P, QT, D]) for i in range(2)]
    xT = st.sb("xT", [P, KC, S])
    qT = [st.sb(f"qT{i}", [P, KC, S]) for i in range(2)]
    kT = [st.sb(f"kT{i}", [P, KC, S]) for i in range(2)]
    vv = [st.sb(f"v{i}", [P, QT, D]) for i in range(2)]
    sm = [st.sb(f"scores{i}", [P, S]) for i in range(QT)]
    probs = [st.sb(f"probs{i}", [P, S]) for i in range(QT)]
    probsT = [st.sb(f"probsT{i}", [P, QT, P]) for i in range(QT)]
    stat = [st.sb(f"stat{i}", [P, 4]) for i in range(QT)]
    pS = [st.pb(f"pS{i}", [P, 512]) for i in range(QT)]
    pT = [st.pb(f"pT{i}", [P, 512]) for i in range(QT)]
    pO = [st.pb(f"pO{i}", [P, 512]) for i in range(QT)]
    pM = [st.pb(f"pM{i}", [P, 2, S]) for i in range(2)]
    W = k.attn_w
    scale = D ** -0.5
    ffn = FFNS[1]

    with st.ctx, nc.Block() as block:
        @block.sync
        def _(sp):
            def load(b, par, waits):
                if waits:
                    sp.wait_ge(s_masked, QT * (b - 1))
                sp.dma_start(ctxT[par][:, :, :], dram["ctxT"][:, :, bass.ds(b * S, S)]).then_inc(ctx_loaded[par], 16)
                sp.dma_start(bias[par][:, :, :], dram["mask1"][:, bass.ds(b * QT, QT), :]).then_inc(mask_loaded[par], 16)
            load(0, 0, False)
            load(1, 1, False)
            rows = dram[ffn.name + "_xs"].rearrange("(n p) w -> p n w", p=P)
            sp.dma_start(rows, k.pad[:, :].unsqueeze(1).to_broadcast([P, rows.shape[1], XW])).then_inc(pads, 16)
            with sp.Fori(1, B // 2) as i:
                load(2 * i, 0, True)
                load(2 * i + 1, 1, True)
            sp.wait_ge(pads, 16)

        @block.tensor
        def _(pe):
            def project_x(b, par):
                pe.wait_ge(xn_ready, b + 1)
                if not (is_int(b) and b == 0):
                    pe.wait_ge(k_copied, b)
                for t in range(QT):
                    for c in range(KC):
                        last = nc.tensor.transpose(pM[0][:, c, t * P:(t + 1) * P],
                                                   xn[par][:, t, c * P:(c + 1) * P], k.ident[:, :])
                last.then_inc(xT_ready, 1)

            def project(out, w, src, ready):
                for f in range(KC):
                    for c in range(KC):
                        last = nc.tensor.matmul(out[:, f, :], W[:, w * KC + c, f * P:(f + 1) * P], src[:, c, :],
                                                start=(c == 0), stop=(c == KC - 1))
                last.then_inc(ready, 1)

            def project_q(b, par):
                pe.wait_ge(xT_copied, b + 1)
                if not (is_int(b) and b == 0):
                    pe.wait_ge(v_copied, b)
                project(pM[1], wq, xT, q_ready)

            def project_k(b, par):
                pe.wait_ge(ctx_loaded[par], nth(b, par))
                project(pM[0], wk, ctxT[par], k_ready)

            def project_v(b, par):
                pe.wait_ge(q_copied, b + 1)
                for t in range(QT):
                    for c in range(KC):
                        last = nc.tensor.matmul(pM[1][:, t, :], ctxT[par][:, c, t * P:(t + 1) * P],
                                                W[:, wv * KC + c, :], start=(c == 0), stop=(c == KC - 1))
                last.then_inc(v_ready, 1)

            def scores(b, par, qt):
                if not (is_int(b) and b == 0):
                    pe.wait_ge(s_masked, QT * b - 1 + qt)
                for c in range(KC):
                    last = nc.tensor.matmul(pS[qt][:, 0:S], qT[par][:, c, qt * P:(qt + 1) * P], kT[par][:, c, :],
                                            start=(c == 0), stop=(c == KC - 1))
                last.then_inc(s_ready, 1)

            def transpose_probs(b, qt):
                pe.wait_ge(p_ready, QT * b + qt + 1)
                for t in range(QT):
                    last = nc.tensor.transpose(pT[qt][:, t * P:(t + 1) * P], probs[qt][:, t * P:(t + 1) * P],
                                               k.ident[:, :])
                last.then_inc(pt_ready, 1)

            def weighted(b, par, qt):
                pe.wait_ge(pt_copied, QT * b + qt + 1)
                if not (is_int(b) and b == 0):
                    pe.wait_ge(o_scaled, QT * b - 1 + qt)
                for t in range(QT):
                    last = nc.tensor.matmul(pO[qt][:, 0:D], probsT[qt][:, t, :], vv[par][:, t, :],
                                            start=(t == 0), stop=(t == QT - 1))
                last.then_inc(o_ready, 1)

            def batch(b, par, last):
                pe.wait_ge(q_copied, b + 1)
                pe.wait_ge(k_copied, b + 1)
                scores(b, par, 0)
                scores(b, par, 1)
                if not last:
                    project_x(b + 1, 1 - par)
                transpose_probs(b, 0)
                if not last:
                    project_q(b + 1, 1 - par)
                transpose_probs(b, 1)
                if not last:
                    project_k(b + 1, 1 - par)
                pe.wait_ge(v_copied, b + 1)
                weighted(b, par, 0)
                if not last:
                    project_v(b + 1, 1 - par)
                weighted(b, par, 1)

            project_x(0, 0)
            project_q(0, 0)
            project_k(0, 0)
            project_v(0, 0)
            batch(0, 0, False)
            with pe.Fori(0, B // 2 - 1) as i:
                batch(2 * i + 1, 1, False)
                batch(2 * i + 2, 0, False)
            batch(B - 1, 1, True)

        @block.vector
        def _(v):
            layer_norm_scale(nc, k, v, Chain(v, ln_step), mv, sq_ready, sq_done)

            def normalise(b, par):
                if not (is_int(b) and b < 2):
                    v.wait_ge(xT_ready, b - 1)
                for t in range(QT):
                    at = bass.ds(b * QT + t, 1)
                    ins = nc.vector.tensor_scalar(xn[par][:, t, :], k.x[:, at, :], mv[:, 0, at], mv[:, 1, at],
                                                  ALU.mult, ALU.add)
                ins.then_inc(xn_ready, 1)

            def copy_xT(b):
                v.wait_ge(xT_ready, b + 1)
                nc.vector.tensor_copy(xT[:, :, :], pM[0][:, :, :]).then_inc(xT_copied, 1)

            def copy_k(b, par):
                v.wait_ge(k_ready, b + 1)
                nc.vector.tensor_copy(kT[par][:, :, :], pM[0][:, :, :]).then_inc(k_copied, 1)

            def mask_and_max(b, par, qt):
                n = QT * b + qt + 1
                v.wait_ge(mask_loaded[par], nth(b, par))
                v.wait_ge(s_ready, n)
                nc.vector.scalar_tensor_tensor(out=sm[qt][:, :], in0=pS[qt][:, 0:S], scalar=scale,
                                               in1=bias[par][:, qt, :], op0=ALU.mult, op1=ALU.add)\
                  .then_inc(s_masked, 1)
                v.wait_ge(s_masked, n)
                nc.vector.tensor_reduce(stat[qt][:, 0:1], sm[qt][:, :], AX.X, ALU.max).then_inc(negmax_ready, 1)
                v.wait_ge(negmax_ready, 2 * n - 1)
                nc.vector.tensor_scalar(stat[qt][:, 1:2], stat[qt][:, 0:1], -1.0, None, ALU.mult)\
                  .then_inc(negmax_ready, 1)

            def take_output(b, qt):
                n = QT * b + qt + 1
                v.wait_ge(o_ready, n)
                nc.vector.reciprocal(stat[qt][:, 3:4], stat[qt][:, 2:3]).then_inc(recip_ready, 1)
                v.wait_ge(recip_ready, n)
                at = bass.ds(b * QT + qt, 1)
                nc.vector.scalar_tensor_tensor(out=k.x[:, at, :], in0=pO[qt][:, 0:D].unsqueeze(1),
                                               scalar=stat[qt][:, 3:4], in1=k.x[:, at, :],
                                               op0=ALU.mult, op1=ALU.add).then_inc(o_scaled, 1)

            def batch(b, par, last):
                first = is_int(b) and b == 0
                if not first:
                    v.wait_ge(o_scaled, QT * b)
                mask_and_max(b, par, 0)
                mask_and_max(b, par, 1)
                if not first:
                    token_stats(nc, k, (b - 1) * QT)
                if not last:
                    copy_xT(b + 1)
                    copy_k(b + 1, 1 - par)
                    if not (is_int(b) and b == B - 2):
                        normalise(b + 2, par)
                take_output(b, 0)
                take_output(b, 1)

            normalise(0, 0)
            normalise(1, 1)
            copy_xT(0)
            copy_k(0, 0)
            batch(0, 0, False)
            with v.Fori(0, B // 2 - 2) as i:
                batch(2 * i + 1, 1, False)
                batch(2 * i + 2, 0, False)
            batch(B - 3, 1, False)
            batch(B - 2, 0, False)
            batch(B - 1, 1, True)
            v.wait_ge(o_scaled, QT * B)
            token_stats(nc, k, (B - 1) * QT)

        @block.scalar
        def _(act):
            layer_norm_root(nc, act, mv, sq_ready, sq_done)

            def copy_q(b, par):
                act.wait_ge(q_ready, b + 1)
                nc.scalar.copy(qT[par][:, :, :], pM[1][:, :, :]).then_inc(q_copied, 1)

            def copy_v(b, par):
                act.wait_ge(v_ready, b + 1)
                nc.scalar.copy(vv[par][:, :, :], pM[1][:, :, :]).then_inc(v_copied, 1)

            def probabilities(b, qt):
                act.wait_ge(negmax_ready, 2 * (QT * b + qt + 1))
                if not (is_int(b) and b == 0):
                    act.wait_ge(o_scaled, QT * b - 1 + qt)
                nc.scalar.activation(probs[qt][:, :], sm[qt][:, :], ACT.Exp, bias=stat[qt][:, 1:2],
                                     accum_out=stat[qt][:, 2:3]).then_inc(p_ready, 1)

            def copy_probsT(b, qt):
                act.wait_ge(pt_ready, QT * b + qt + 1)
                nc.scalar.copy(probsT[qt][:, :, :], pT[qt][:, 0:S].rearrange("p (t n) -> p t n", t=QT))\
                  .then_inc(pt_copied, 1)

            def batch(b, par, last):
                probabilities(b, 0)
                probabilities(b, 1)
                copy_probsT(b, 0)
                if not last:
                    copy_q(b + 1, 1 - par)
                copy_probsT(b, 1)
                if not last:
                    copy_v(b + 1, 1 - par)

            copy_q(0, 0)
            copy_v(0, 0)
            batch(0, 0, False)
            with act.Fori(0, B // 2 - 1) as i:
                batch(2 * i + 1, 1, False)
                batch(2 * i + 2, 0, False)
            batch(B - 1, 1, True)


def feed_forward(nc, k, dram, f):
    L1, L2, L3 = f.name == "L1f", f.name == "L2f", f.name == "L3f"
    st = Stage(nc, f.name)
    sem = st.sem
    sq_ready, sq_done, dve_step = sem("sq_ready"), sem("sq_done"), sem("dve_step")
    small_loaded, xn_ready = sem("small_loaded"), sem("xn_ready")
    xt_ready, xt_copied, logits_ready = sem("xT_ready"), sem("xT_copied"), sem("logits_ready")
    exp_in, exp_out = sem("exp_input_ready"), sem("exp_done")
    chosen, counted, counted_c = sem("experts_chosen"), sem("counts_ready"), sem("counts_copied")
    ranked, placed, dispatched = sem("ranks_ready"), sem("slots_placed"), sem("rows_dispatched")
    second = sem("second_copy")
    second_norm = sem("second_norm")
    b2_added, back_summed = sem("b2_added"), sem("back_summed")
    x_loaded, w_loaded = [sem(f"x_tile{i}_loaded") for i in range(2)], [sem(f"weights{i}_loaded") for i in range(2)]
    b2_loaded = [sem(f"b2_{i}_loaded") for i in range(2)]
    tT_ready, tT_copied, meta_copied = sem("tileT_ready"), sem("tileT_copied"), sem("meta_copied")
    up_ready, act_done, h_ready = sem("up_ready"), sem("activated"), sem("hidden_ready")
    y_ready, y_copied, y_sent = sem("y_ready"), sem("y_copied"), [sem(f"y{i}_sent") for i in range(2)]
    back_loaded, back_added = [sem(f"back{i}_loaded") for i in range(4)], sem("back_added")

    mv = st.sb("mv", [P, 4, NT])
    rows = st.sb("rows", [P, TK, NT, XW])
    wr = st.sb("router", [P, KC, E])
    rb = st.sb("router_b", [P, E])
    gb = st.sb("gamma_beta", [P, 2, D]) if L2 else None
    XTN = NT if f.shared else 2
    xT = st.sb("xT", [P, KC, XTN * P])
    at_tile = lambda t: slice(t % XTN * P, (t % XTN + 1) * P)
    lg = st.sb("logits", [P, NT, E])
    sc = st.sb("score", [P, NT, E])
    one = [st.sb(f"choice{i}", [P, NT, E]) for i in range(TK)]
    ex = st.sb("exp", [P, NT, E])
    tot = st.sb("totals", [P, P])
    r16 = [st.sb(f"row{i}", [P, NT]) for i in range(8)]
    r8 = [st.sb(f"seg{i}", [P, E]) for i in range(6)]
    big8 = st.sb("seg_cmp", [P, E, E])
    bigt = st.sb("tile_cmp", [P, RT, E])
    tef = st.sb("tile_expert_f", [P, RT])
    te = st.sb("tile_expert", [P, RT], I32)
    pos = st.sb("slot", [P, TK, NT], I32)
    xin = [st.sb(f"x_tile{i}", [P, 2, XW]) for i in range(2)]
    meta = st.sb("meta", [P, 2 * RT, 2])
    dest = [st.sb(f"destination{i}", [P, 2]) for i in range(2)]
    tT = [st.sb(f"tileT{i}", [P, KC, ST]) for i in range(2)]
    wt = [st.sb(f"weights{i}", [P, f.cols]) for i in range(2)]
    b2 = [st.sb(f"b2_{i}", [P, D]) for i in range(2)] if L1 else None
    hid = [st.sb(f"hidden{i}", [P, f.blocks, ST]) for i in range(2)]
    gate = [st.sb(f"gate{i}", [P, ST]) for i in range(2)] if f.gated else None
    yy = [st.sb(f"y{i}", [P, 2, D]) for i in range(2)]

    pU = [st.pb(f"pU{i}", [P, 2, ST]) for i in range(f.banks)]
    pX = st.pb("pX", [P, KC, ST])
    pY = [st.pb(f"pY{i}", [P, 2, D]) for i in range(2)]
    pR = st.pb("pR", [P, 512])

    G, NB = f.groups, f.banks
    J, JS = f.tiles, f.shared * XT
    if L2:
        J, PT = E // 2 * PAIR_TILES, PAIR_TILES
    sent_before = lambda q: sum(n for m, (_, _, n) in enumerate(PAIR[:q]) if m % 2 == q % 2)
    sent_pair = [sum(n for m, (_, _, n) in enumerate(PAIR) if m % 2 == p) for p in range(2)]
    xs = dram[f.name + "_xs"]
    yk = dram[f.name + "_yk"]
    wd = dram[f.name + "_w"]
    bc16 = lambda a: a.unsqueeze(2).to_broadcast([P, NT, E])
    bc8 = lambda a: a.unsqueeze(1).to_broadcast([P, NT, E])

    with st.ctx, nc.Block() as block:
        @block.sync
        def _(sp):
            sp.dma_start(wr[:, :, :], dram[f.name + "_router"]).then_inc(small_loaded, 16)
            n = 1
            if L1 or L3:
                sp.dma_start(rb[:, :], dram[f.name + "_rb"].partition_broadcast(P)).then_inc(small_loaded, 16)
            if L2:
                sp.dma_start(gb[:, :, :], dram["L2f_gb"].partition_broadcast(P)).then_inc(small_loaded, 16)

            def load_weights(j, par, expert):
                if not (is_int(j) and j < 2):
                    sp.wait_ge(y_copied if L1 else y_ready, j - 1)
                sp.dma_start(wt[par][:, :], wd[bass.ds(expert, 1), :, :].rearrange("a p n -> (a p) n"))\
                  .then_inc(w_loaded[par], 16)
                if L1:
                    row = dram["L1f_b2"][bass.ds(expert, 1), :].rearrange("a d -> (a d)")
                    sp.dma_start(b2[par][:, :], row.partition_broadcast(P)).then_inc(b2_loaded[par], 16)

            def load_tile(r, par, row=None, nt=2):
                if not (is_int(r) and r < 2):
                    sp.wait_ge(meta_copied, r - 1)
                row = r * ST if row is None else row
                sp.dma_start(xin[par][:, 0:nt, :], xs[bass.ds(row, nt * P), :].rearrange("(t p) w -> p t w", p=P))\
                  .then_inc(x_loaded[par], 16)

            for n in range(f.shared):
                if n == 0:
                    load_weights(0, 0, E)
                    load_weights(1, 1, E)
                with sp.Fori(0 if n else 1, XT // 2) as i:
                    for par in range(2):
                        load_weights(n * XT + 2 * i + par, par, E + n)
            def capacity_pair(i):
                for q, (e, row, nt) in enumerate(PAIR):
                    first_pair = is_int(i) and i == 0
                    if not first_pair and row == e * CAP:
                        sp.wait_ge(y_ready, PT * (i - 1) + PT // 2 * (e + 1))
                        sp.dma_start(wt[e][:, :], wd[bass.ds(2 * i + e, 1), :, :].rearrange("a p n -> (a p) n"))\
                          .then_inc(w_loaded[e], 16)
                    load_tile(PT * i + q, q % 2, 2 * CAP * i + row, nt)

            if L2:
                for e in range(2):
                    sp.dma_start(wt[e][:, :], wd[e, :, :]).then_inc(w_loaded[e], 16)
            else:
                sp.wait_ge(placed, 2)
            sp.wait_ge(dispatched, 16 * TK * NT)

            def routed_pair(i):
                for par in range(2):
                    expert = sp.value_load(te[0:1, bass.ds(2 * i + par, 1)], min_val=0, max_val=E - 1)
                    load_tile(2 * i + par, par)
                    load_weights(JS + 2 * i + par, par, expert)
            if L2:
                capacity_pair(0)
                with sp.Fori(1, E // 2) as i:
                    capacity_pair(i)
            else:
                routed_pair(0)
                with sp.Fori(1, RT // 2) as i:
                    routed_pair(i)
            for par in range(2):
                sp.wait_ge(y_sent[par], 16 * (E // 2 * sent_pair[par] if L2 else RT))

            for q in range(4):
                for c in range(TK):
                    sp.dma_start(rows[:, c, 4 * q:4 * q + 4, 0:D], yk[c * T + 4 * q * P:c * T + 4 * (q + 1) * P, :]
                                 .rearrange("(t p) w -> p t w", p=P)).then_inc(back_loaded[q], 16)

        @block.gpsimd
        def _(gp):
            gp.iota(rows[:, :, :, D:D + 1].bitcast(I32), [[T, TK], [P, NT], [1, 1]], base=0, channel_multiplier=1)\
              .then_inc(second, 1)
            for q in range(4):
                gp.wait_ge(xn_ready, 4 * (q + 1))
                gp.tensor_copy(rows[:, 1, 4 * q:4 * q + 4, 0:D], rows[:, 0, 4 * q:4 * q + 4, 0:D]).then_inc(second, 1)
            last_slot, rows_out = gp.to_reg(xs.shape[0] - 1), gp.to_reg(TK * T)
            bound = gp.alloc_register(f.name + "_row_bound")
            gp.wait_ge(second, 5)
            gp.wait_ge(placed, 1)
            for c in range(TK):
                for t in range(NT):
                    gp.indirect_dma_start(xs[:, :], bass.IndirectOffsetOnAxis(ap=pos[:, c, t:t + 1], axis=0),
                                          rows[:, c, t, :], None, bounds_check=last_slot,
                                          oob_is_err=False).then_inc(dispatched, 16)

            def send(j, par, nt=2):
                gp.wait_ge(y_copied, j + 1)
                gp.reg_add(bound, rows_out, -1)
                for t in range(nt):
                    gp.indirect_dma_start(yk[:, :], bass.IndirectOffsetOnAxis(
                        ap=dest[par][:, t:t + 1].bitcast(I32), axis=0), yy[par][:, t, :], None,
                        bounds_check=bound, oob_is_err=False).then_inc(y_sent[par], 16)
            if L2:
                with gp.Fori(0, E // 2) as i:
                    for q, (_, _, nt) in enumerate(PAIR):
                        send(PT * i + q, q % 2, nt)
            else:
                with gp.Fori(JS // 2, J // 2) as i:
                    send(2 * i, 0)
                    send(2 * i + 1, 1)
            gp.free_register(bound)
            for q in (1, 3):
                at = slice(4 * q, 4 * q + 4)
                gp.wait_ge(back_loaded[q], 16 * TK)
                gp.tensor_tensor(rows[:, 0, at, 0:D], rows[:, 0, at, 0:D], rows[:, 1, at, 0:D], ALU.add)\
                  .then_inc(back_summed, 1)

        @block.tensor
        def _(pe):
            pe.wait_ge(small_loaded, 16 * (1 + (L1 or L3) + L2))
            for t in range(NT + 1):
                if t < NT:
                    pe.wait_ge(xn_ready, t + 1)
                    if t >= 2:
                        pe.wait_ge(xt_copied, t - 1)
                    for c in range(KC):
                        last = nc.tensor.transpose(pU[t % 2][:, 0, c * P:(c + 1) * P],
                                                   rows[:, 0, t, c * P:(c + 1) * P], k.ident[:, :])
                    last.then_inc(xt_ready, 1)
                if t == 0:
                    continue
                pe.wait_ge(xt_copied, t)
                for c in range(KC):
                    last = nc.tensor.matmul(pR[:, E * (t - 1):E * t], xT[:, c, at_tile(t - 1)], wr[:, c, :],
                                            start=(c == 0), stop=(c == KC - 1), skip_group_check=True)
            last.then_inc(logits_ready, 1)
            pe.wait_ge(chosen, 1)
            nc.tensor.matmul(pR[:, 0:P], sc[:, :, :].rearrange("p t e -> p (t e)"), k.ones[:, :],
                             start=True, stop=True).then_inc(counted, 1)
            pe.wait_ge(counted_c, 1)
            nc.tensor.matmul(pR[:, 0:P], k.before[:, :], sc[:, :, :].rearrange("p t e -> p (t e)"),
                             start=True, stop=False, skip_group_check=True)
            nc.tensor.matmul(pR[:, 0:P], tot[:, :], k.earlier[:, :, :].rearrange("p t e -> p (t e)"),
                             start=False, stop=True, skip_group_check=True)
            nc.tensor.matmul(pR[:, P:P + E], tot[:, :], k.same[:, :], start=False, stop=True,
                             skip_group_check=True).then_inc(ranked, 1)

            def transpose_tile(r, par, nt=2):
                pe.wait_ge(x_loaded[par], nth(r, par))
                if not (is_int(r) and r == 0):
                    pe.wait_ge(tT_copied, r)
                for t in range(nt):
                    for c in range(KC):
                        last = nc.tensor.transpose(pX[:, c, t * P:(t + 1) * P], xin[par][:, t, c * P:(c + 1) * P],
                                                   k.ident[:, :])
                last.then_inc(tT_ready, 1)

            def up(j, par, tile, routed, weights=None, nt=2):
                if routed:
                    pe.wait_ge(tT_copied, tile + 1)
                wpar, loaded = (par, nth(j, par)) if weights is None else weights
                pe.wait_ge(w_loaded[wpar], loaded)
                for g in range(G):
                    if not (is_int(j) and j * G + g < NB):
                        pe.wait_ge(h_ready, (1 if f.gated else 2) * (j * G + g - NB + 1))
                    bank = pU[(par * G + g) % NB]
                    for half in range(2):
                        m, blk = (half, g) if f.gated else (0, 2 * g + half)
                        for c in range(KC):
                            at = ((m * KC + c) * f.blocks + blk) * P
                            src = tT[par][:, c, 0:nt * P] if routed else xT[:, c, bass.ds(tile * ST, ST)]
                            last = nc.tensor.matmul(bank[:, half, 0:nt * P], wt[wpar][:, at:at + P], src,
                                                    start=(c == 0), stop=(c == KC - 1))
                    last.then_inc(up_ready, 1)

            def down(j, par, wpar=None, nt=2):
                wpar = par if wpar is None else wpar
                if not (is_int(j) and j < 2):
                    pe.wait_ge(y_copied, j - 1)
                for t in range(nt):
                    for blk in range(f.blocks):
                        if t == 0 and (f.gated or blk % 2 == 0):
                            n = blk if f.gated else blk // 2
                            pe.wait_ge(h_ready, (1 if f.gated else 2) * (j * G + n + 1))
                        last = nc.tensor.matmul(pY[par][:, t, :], hid[par][:, blk, t * P:(t + 1) * P],
                                                wt[wpar][:, f.up + blk * D:f.up + (blk + 1) * D],
                                                start=(blk == 0), stop=(blk == f.blocks - 1))
                last.then_inc(y_ready, 1)

            def pair(j0, tile0, routed, next_routed, last=False):
                if G == 1 and not routed:
                    for par in range(2):
                        up(j0 + par, par, tile0 + par, routed)
                    if next_routed:
                        transpose_tile(0, 0)
                    for par in range(2):
                        down(j0 + par, par)
                    return
                for par in range(2):
                    early = G == 1 and not (last and par)
                    if early:
                        transpose_tile(tile0 + par + 1, 1 - par)
                    up(j0 + par, par, tile0 + par, routed)
                    if routed and not early and not (last and par):
                        transpose_tile(tile0 + par + 1, 1 - par)
                    elif not routed and next_routed and par:
                        transpose_tile(0, 0)
                    down(j0 + par, par)

            def capacity_pair(i, last):
                for q, (e, _, nt) in enumerate(PAIR):
                    j = PT * i + q
                    up(j, q % 2, j, True, (e, 16 * (i + 1)), nt)
                    if not (last and q == PT - 1):
                        transpose_tile(j + 1, 1 - q % 2, PAIR[(q + 1) % PT][2])
                    down(j, q % 2, e, nt)

            if L2:
                transpose_tile(0, 0)
                capacity_pair(0, False)
                with pe.Fori(1, E // 2 - 1) as i:
                    capacity_pair(i, False)
                capacity_pair(E // 2 - 1, True)
            for n in range(f.shared):
                if n == 0:
                    pair(0, 0, False, False)
                with pe.Fori(0 if n else 1, XT // 2 - 1) as i:
                    pair(n * XT + 2 * i, 2 * i, False, False)
                pair((n + 1) * XT - 2, XT - 2, False, n == f.shared - 1)
            if not L2:
                pair(JS, 0, True, True)
                with pe.Fori(1, RT // 2 - 1) as i:
                    pair(JS + 2 * i, 2 * i, True, True)
                pair(J - 2, RT - 2, True, True, last=True)

        @block.vector
        def _(v):
            link = Chain(v, dve_step)
            layer_norm_scale(nc, k, v, link, mv, sq_ready, sq_done, twice=L2)

            def normalise(src, done):
                with v.Fori(0, NT) as t:
                    at = bass.ds(t, 1)
                    nc.vector.tensor_scalar(rows[:, 0, at, 0:D], src[:, at, 0:D], mv[:, 0, at], mv[:, 1, at],
                                            ALU.mult, ALU.add).then_inc(done, 1)
            if L2:
                normalise(k.x, second_norm)
                v.wait_ge(second_norm, NT)
                v.wait_ge(small_loaded, 32)
                for q in range(4):
                    at = rows[:, 0, 4 * q:4 * q + 4, 0:D]
                    link(nc.vector.tensor_tensor(at, at, gb[:, 0:1, :].to_broadcast([P, 4, D]), ALU.mult))
                    nc.vector.tensor_tensor(at, at, gb[:, 1:2, :].to_broadcast([P, 4, D]), ALU.add)\
                      .then_inc(xn_ready, 4)
            else:
                normalise(k.x, xn_ready)

            v.wait_ge(logits_ready, 1)
            pr = pR[:, 0:P].rearrange("p (t e) -> p t e", e=E)
            if L1 or L3:
                link(nc.vector.tensor_tensor(lg[:, :, :], pr, bc8(rb[:, :]), ALU.add))
            elif L2:
                link(nc.vector.tensor_scalar(lg[:, :, :], pr, 10000.0, -10000.0, ALU.min, ALU.max))
            else:
                link(nc.vector.tensor_copy(lg[:, :, :], pr))
            m, val, e1, e2, z = r16[0], r16[1], r16[2], r16[3], r16[4]
            link(nc.vector.tensor_reduce(m[:, :], lg[:, :, :], AX.X, ALU.max))
            nc.vector.tensor_tensor(ex[:, :, :], lg[:, :, :], bc16(m[:, :]), ALU.subtract).then_inc(exp_in, 1)

            def choose(c):
                link(nc.vector.tensor_tensor(sc[:, :, :], lg[:, :, :], bc16(m[:, :]), ALU.is_equal))
                link(nc.vector.tensor_tensor(sc[:, :, :], sc[:, :, :], k.expert[:, :, :], ALU.mult))
                link(nc.vector.tensor_reduce(val[:, :], sc[:, :, :], AX.X, ALU.max))
                link(nc.vector.tensor_tensor(one[c][:, :, :], sc[:, :, :], bc16(val[:, :]), ALU.is_equal))
            choose(0)
            link(nc.vector.scalar_tensor_tensor(out=lg[:, :, :], in0=one[0][:, :, :], scalar=-1e30, in1=lg[:, :, :],
                                                op0=ALU.mult, op1=ALU.add))
            link(nc.vector.tensor_reduce(m[:, :], lg[:, :, :], AX.X, ALU.max))
            choose(1)
            nc.vector.tensor_tensor(sc[:, :, :], one[0][:, :, :], one[1][:, :, :], ALU.add).then_inc(chosen, 1)
            v.wait_ge(exp_out, 1)
            for c, out in ((0, e1), (1, e2)):
                link(nc.vector.tensor_tensor(lg[:, :, :], ex[:, :, :], one[c][:, :, :], ALU.mult))
                link(nc.vector.tensor_reduce(out[:, :], lg[:, :, :], AX.X, ALU.add))
            if not L3:
                link(nc.vector.tensor_reduce(z[:, :], ex[:, :, :], AX.X, ALU.add))
                if L2:
                    link(nc.vector.tensor_scalar(z[:, :], z[:, :], 1e-12, None, ALU.add))
                link(nc.vector.reciprocal(z[:, :], z[:, :]))
                for out in (e1, e2):
                    link(nc.vector.tensor_tensor(out[:, :], out[:, :], z[:, :], ALU.mult))
            if not L2:
                link(nc.vector.tensor_tensor(z[:, :], e1[:, :], e2[:, :], ALU.add))
                if f.name == "L0f":
                    link(nc.vector.tensor_scalar(z[:, :], z[:, :], 1e-20, None, ALU.add))
                link(nc.vector.reciprocal(z[:, :], z[:, :]))
                for out in (e1, e2):
                    link(nc.vector.tensor_tensor(out[:, :], out[:, :], z[:, :], ALU.mult))
            v.wait_ge(counted, 1)
            nc.vector.tensor_copy(tot[:, :], pR[:, 0:P]).then_inc(counted_c, 1)
            v.wait_ge(ranked, 1)
            count, tiles, end, start, ones8 = r8[0], r8[1], r8[2], r8[3], r8[4]
            if L2:
                link(nc.vector.tensor_scalar(start[:, :], k.expert[:, 0, :], -float(CAP), float(E * CAP),
                                             ALU.mult, ALU.add))
            else:
                link(nc.vector.tensor_copy(count[:, :], pR[:, P:P + E]))
                link(nc.vector.tensor_tensor(big8[:, :, :], count[:, :].unsqueeze(2).to_broadcast([P, E, E]),
                                             k.threshold[:, :, :], ALU.is_gt))
                link(nc.vector.tensor_reduce(tiles[:, :], big8[:, :, :], AX.X, ALU.add))
                link(nc.vector.memset(ones8[:, :], 1.0))
                link(nc.vector.tensor_tensor_scan(end[:, :], ones8[:, :], tiles[:, :], 0.0, ALU.mult, ALU.add))
                link(nc.vector.tensor_tensor(start[:, :], end[:, :], tiles[:, :], ALU.subtract))
                link(nc.vector.tensor_scalar(start[:, :], start[:, :], float(ST), None, ALU.mult))
            for c in range(TK):
                rk, seg, w = r16[5], r16[6], (e1, e2)[c]
                link(nc.vector.tensor_tensor(lg[:, :, :], pr, one[c][:, :, :], ALU.mult))
                link(nc.vector.tensor_reduce(rk[:, :], lg[:, :, :], AX.X, ALU.add))
                link(nc.vector.tensor_tensor(lg[:, :, :], one[c][:, :, :], bc8(start[:, :]), ALU.mult))
                link(nc.vector.tensor_reduce(seg[:, :], lg[:, :, :], AX.X, ALU.add))
                link(nc.vector.tensor_tensor(seg[:, :], seg[:, :], rk[:, :], ALU.add))
                if L2:
                    link(nc.vector.tensor_scalar(rk[:, :], rk[:, :], float(CAP), float(NOWHERE), ALU.is_ge, ALU.mult))
                    link(nc.vector.tensor_tensor(seg[:, :], seg[:, :], rk[:, :], ALU.add))
                link(nc.vector.tensor_copy(pos[:, c, :], seg[:, :]))
                ins = nc.vector.tensor_copy(rows[:, c, :, D + 1], w[:, :])
                if c == 0:
                    link(ins)
            ins.then_inc(placed, 1)
            if not L2:
                link(nc.vector.tensor_tensor(bigt[:, :, :], end[:, :].unsqueeze(1).to_broadcast([P, RT, E]),
                                             k.tile_no[:, :, :], ALU.is_le))
                link(nc.vector.tensor_reduce(tef[:, :], bigt[:, :, :], AX.X, ALU.add))
                link(nc.vector.tensor_scalar(tef[:, :], tef[:, :], float(E - 1), None, ALU.min))
                nc.vector.tensor_copy(te[:, :], tef[:, :]).then_inc(placed, 1)

            def copy_rows(r, par, nt=2):
                v.wait_ge(tT_ready, r + 1)
                nc.vector.tensor_copy(tT[par][:, :, 0:nt * P], pX[:, :, 0:nt * P]).then_inc(tT_copied, 1)

            def copy_meta(r, par, nt=2):
                nc.vector.tensor_copy(meta[:, bass.ds(2 * r, nt), :], xin[par][:, 0:nt, D:XW]).then_inc(meta_copied, 1)

            def copy_tile(r, par, nt=2):
                copy_rows(r, par, nt)
                copy_meta(r, par, nt)

            def gates_times(j, par, nt=2):
                for g in range(G):
                    v.wait_ge(act_done, j * G + g + 1)
                    nc.vector.tensor_tensor(hid[par][:, g, 0:nt * P], gate[(par * G + g) % 2][:, 0:nt * P],
                                            pU[(par * G + g) % NB][:, 1, 0:nt * P], ALU.mult).then_inc(h_ready, 1)

            def take(j, par, n, routed, nt=2, sent=None):
                v.wait_ge(y_ready, j + 1)
                if routed:
                    v.wait_ge(meta_copied, n + 1)
                    if not (is_int(n) and n < 2):
                        v.wait_ge(y_sent[par], nth2(n, par) if sent is None else sent)
                y = pY[par]
                if L1:
                    v.wait_ge(b2_loaded[par], nth(j, par))
                    bias = b2[par][:, :].unsqueeze(1).to_broadcast([P, 2, D])
                    if routed:
                        nc.vector.tensor_tensor(yy[par][:, :, :], y[:, :, :], bias, ALU.add).then_inc(b2_added, 1)
                        y = yy[par]
                    else:
                        at = bass.ds(2 * n, 2)
                        nc.vector.tensor_tensor(k.x[:, at, :], k.x[:, at, :], bias, ALU.add).then_inc(b2_added, 1)
                    v.wait_ge(b2_added, j + 1)
                for t in range(nt):
                    if routed:
                        ins = nc.vector.tensor_scalar(yy[par][:, t:t + 1, :], y[:, t:t + 1, :],
                                                      meta[:, bass.ds(2 * n + t, 1), 1], None, ALU.mult)
                    else:
                        at = bass.ds(2 * n + t, 1)
                        ins = nc.vector.tensor_tensor(k.x[:, at, :], k.x[:, at, :], pY[par][:, t:t + 1, :], ALU.add)
                if routed:
                    ins = nc.vector.tensor_copy(dest[par][:, 0:nt].unsqueeze(2), meta[:, bass.ds(2 * n, nt), 0:1])
                ins.then_inc(y_copied, 1)

            def pair(j0, n0, routed, next_routed, last=False):
                if G == 1 and not routed:
                    for par in range(2):
                        gates_times(j0 + par, par)
                    if next_routed:
                        copy_tile(0, 0)
                    for par in range(2):
                        take(j0 + par, par, n0 + par, routed)
                    return
                for par in range(2):
                    early = G == 1 and not (last and par)
                    if early:
                        copy_rows(n0 + par + 1, 1 - par)
                    if f.gated:
                        gates_times(j0 + par, par)
                    if early:
                        copy_meta(n0 + par + 1, 1 - par)
                    if routed and not early and not (last and par):
                        copy_tile(n0 + par + 1, 1 - par)
                    elif not routed and next_routed and par:
                        copy_tile(0, 0)
                    take(j0 + par, par, n0 + par, routed)

            def capacity_pair(i, last):
                for q, (_, _, nt) in enumerate(PAIR):
                    j, par = PT * i + q, q % 2
                    gates_times(j, par, nt)
                    if not (last and q == PT - 1):
                        copy_tile(j + 1, 1 - par, PAIR[(q + 1) % PT][2])
                    take(j, par, j, True, nt, 16 * (sent_pair[par] * i + sent_before(q)))

            if L2:
                copy_tile(0, 0)
                capacity_pair(0, False)
                with v.Fori(1, E // 2 - 1) as i:
                    capacity_pair(i, False)
                capacity_pair(E // 2 - 1, True)
            for n in range(f.shared):
                with v.Fori(0, XT // 2 - 1) as i:
                    pair(n * XT + 2 * i, 2 * i, False, False)
                pair((n + 1) * XT - 2, XT - 2, False, n == f.shared - 1)
            if not L2:
                pair(JS, 0, True, True)
                with v.Fori(1, RT // 2 - 1) as i:
                    pair(JS + 2 * i, 2 * i, True, True)
                pair(J - 2, RT - 2, True, True, last=True)

            for q in range(4):
                at = k.x[:, 4 * q:4 * q + 4, :]
                if q % 2:
                    v.wait_ge(back_summed, (q + 1) // 2)
                else:
                    v.wait_ge(back_loaded[q], 16 * TK)
                    nc.vector.tensor_tensor(at, at, rows[:, 1, 4 * q:4 * q + 4, 0:D], ALU.add).then_inc(back_added, 1)
                    v.wait_ge(back_added, 3 * q // 2 + 1)
                nc.vector.tensor_tensor(at, at, rows[:, 0, 4 * q:4 * q + 4, 0:D], ALU.add).then_inc(back_added, 1)
                if not L3:
                    v.wait_ge(back_added, (2, 3, 5, 6)[q])
                    token_stats(nc, k, 4 * q)
                    token_stats(nc, k, 4 * q + 2)

        @block.scalar
        def _(act):
            layer_norm_root(nc, act, mv, sq_ready, sq_done)
            for t in range(NT):
                act.wait_ge(xt_ready, t + 1)
                nc.scalar.copy(xT[:, :, at_tile(t)], pU[t % 2][:, 0, :].rearrange("p (c n) -> p c n", c=KC))\
                  .then_inc(xt_copied, 1)
            act.wait_ge(exp_in, 1)
            nc.scalar.activation(ex[:, :, :], ex[:, :, :], ACT.Exp).then_inc(exp_out, 1)

            def activate(j, par, nt=2):
                for g in range(G):
                    n = j * G + g
                    act.wait_ge(up_ready, n + 1)
                    bank = pU[(par * G + g) % NB]
                    if f.gated:
                        if not (is_int(n) and n < 2):
                            act.wait_ge(h_ready, n - 1)
                        nc.scalar.activation(gate[(par * G + g) % 2][:, 0:nt * P], bank[:, 0, 0:nt * P], f.func)\
                          .then_inc(act_done, 1)
                    else:
                        for half in range(2):
                            blk = 2 * g + half
                            at = f.up + f.blocks * D + blk
                            nc.scalar.activation(hid[par][:, blk, :], bank[:, half, :], f.func,
                                                 bias=wt[par][:, at:at + 1]).then_inc(h_ready, 1)

            def capacity_pair(i):
                for q, (_, _, nt) in enumerate(PAIR):
                    activate(PT * i + q, q % 2, nt)

            if L2:
                capacity_pair(0)
                with act.Fori(1, E // 2) as i:
                    capacity_pair(i)
            else:
                activate(0, 0)
                activate(1, 1)
                with act.Fori(1, J // 2) as i:
                    activate(2 * i, 0)
                    activate(2 * i + 1, 1)


class Resident:

    def __init__(self, nc, ctx):
        def sb(name, shape, dt=F32):
            return ctx.enter_context(nc.sbuf_tensor(name, shape, dt))
        self.x = sb("x_sb", [P, NT, D])
        self.attn_w = sb("attn_w_sb", [P, NW * KC, D])
        self.attn_bcol = sb("attn_bcol_sb", [P, 8])
        self.attn_brow = sb("attn_brow_sb", [1, 5, D])
        self.brow3 = sb("attn_brow_parts", [NPART, 5, D], BF16)
        self.ones16 = sb("ones16", [NPART, P], BF16)
        self.ident, self.ident16 = sb("ident", [P, P]), sb("ident16", [P, P], BF16)
        self.ones, self.before = sb("ones", [P, P]), sb("before", [P, P])
        self.earlier, self.same = sb("earlier", [P, NT, E]), sb("same", [P, E])
        self.expert, self.threshold = sb("expert_rev", [P, NT, E]), sb("threshold", [P, E, E])
        self.tile_no = sb("tile_no", [P, RT, E])
        self.stats = sb("stats", [P, NT, 6])
        self.row_expert = sb("row_expert", [P, 1])
        self.mask0 = sb("mask0_sb", [P, NT, S], BF16)
        self.mask2 = sb("mask2_sb", [P, B, S], BF16)
        self.causal = sb("causal", [P, QT, S], BF16)
        self.pad = sb("pad", [P, XW])


def store(nc, k, dram):
    with nc.semaphore("x_stored") as stored, nc.Block() as block:
        @block.sync
        def _(sp):
            sp.dma_start(dram["out"].rearrange("(t p) d -> p t d", p=P), k.x[:, :, :]).then_inc(stored, 16)
            sp.wait_ge(stored, 16)


STAGES = "a0 f0 a1 f1 a2 f2 a3 f3".split()


def program(nc, dram, stages=STAGES):
    for f in FFNS:
        dram[f.name + "_xs"] = nc.dram_tensor(f.name + "_xs", [E * CAP if f.capacity else RT * ST, XW], F32, kind="Internal").ap()
        dram[f.name + "_yk"] = nc.dram_tensor(f.name + "_yk", [TK * T, D], F32, kind="Internal").ap()
    dram["splits"] = nc.dram_tensor("splits", [2, 2, NPART, DH, H, S], BF16, kind="Internal").ap()
    with ExitStack() as mem:
        Stage.handles = []
        k = Resident(nc, mem)
        constants(nc, k, dram)
        for s in stages:
            if s == "a0":
                attention16(nc, k, dram, "L0a", L0Q, L0K, L0V, L0O, mask="pair", out_bias=4, ffn=FFNS[0])
            elif s == "a1":
                attention1(nc, k, dram, "L1a", L1Q, L1K, L1V)
            elif s == "a2":
                attention16(nc, k, dram, "L2a", L2Q, L2K, L2V, L2O, mask="batch", ffn=FFNS[2])
            elif s == "a3":
                with nc.sbuf_tensor("self_attended", [P, NT, D], F32) as h:
                    attention16(nc, k, dram, "L3a", AQ, AK, AV, AO, kv_self=True, mask="causal", bias=0, out_bias=2,
                                add=False, dst=h)
                    attention16(nc, k, dram, "L3b", BQ, BK, BV, BO, norm=False, bias=1, out_bias=3, src=h, ffn=FFNS[3])
            else:
                feed_forward(nc, k, dram, FFNS[int(s[1])])
                clear_semaphores(nc)
        store(nc, k, dram)


def layout(inputs):
    import numpy as np
    a = {n: np.asarray(v) for n, v in inputs.items()}

    def chunks(w):
        return w.reshape(-1, P, w.shape[-1]).transpose(1, 0, 2)

    def heads(w):
        return w.transpose(1, 0, 2).reshape(D, D)

    out = {"x": a["x"].reshape(T, D), "mask0": a["mask_Bx1xSxS2_if1"].reshape(T, S),
           "mask1": a["mask_BxSxS2_ff0"].reshape(NT, P, S).transpose(1, 0, 2), "lens": a["_lenS2"].reshape(B),
           "ctxT": chunks(a["ctx_1024"].reshape(T, D).T)}
    mats = [a[f"L0_xattn_W{m}"].T for m in "qkvo"] + [a[f"L1_xattn_W{m}"].T for m in "qkv"] \
        + [a[f"L2_xattn_W{m}"].T for m in "qkvo"]
    for n in "12":
        mats += [heads(a[f"L3_xattn_W{m}{n}"]) for m in "qkv"] + [a[f"L3_xattn_Wo{n}"]]
    out["attn_w"] = np.concatenate([chunks(m) for m in mats], axis=1)
    cols = [a[f"L3_xattn_b{m}{n}"].reshape(KC, P).T for n in "12" for m in "qk"]
    out["attn_bcol"] = np.concatenate(cols, axis=1)
    brow = [a[f"L3_xattn_b{m}{n}"].reshape(D) for m in "vo" for n in "12"] + [a["L0_xattn_bo"]]
    out["attn_brow"] = np.stack(brow)[None]

    def ups(w, f):
        w = np.pad(w, ((0, 0), (0, f.blocks * P - w.shape[1])))
        return chunks(w).reshape(P, -1)

    def downs(w, f):
        return chunks(np.pad(w, ((0, f.blocks * P - w.shape[0]), (0, 0)))).reshape(P, -1)

    def gated(g, u, d, f):
        return np.concatenate([ups(g, f), ups(u, f), downs(d, f)], axis=1)

    f0, f1, f2, f3 = FFNS
    e0 = [gated(a["L0_ffn_wg"][e], a["L0_ffn_wu"][e], a["L0_ffn_wd"][e], f0) for e in range(E)]
    n = a["L0_ffn_swd"].shape[0] // f0.shared
    e0 += [gated(a["L0_ffn_swg"][:, n * i:n * i + n], a["L0_ffn_swu"][:, n * i:n * i + n],
                 a["L0_ffn_swd"][n * i:n * i + n], f0) for i in range(f0.shared)]
    out["L0f_w"] = np.stack(e0)
    w1 = list(a["L1_ffn_spec_w1"]) + [a["L1_ffn_shared_w1"]]
    w2 = list(a["L1_ffn_spec_w2"]) + [a["L1_ffn_shared_w2"]]
    b1 = list(a["L1_ffn_spec_b1"]) + [a["L1_ffn_shared_b1"]]
    out["L1f_w"] = np.stack([np.concatenate([ups(u.T, f1), downs(d.T, f1), b.reshape(f1.blocks, P).T], axis=1)
                             for u, d, b in zip(w1, w2, b1)])
    out["L1f_b2"] = np.concatenate([a["L1_ffn_spec_b2"], a["L1_ffn_shared_b2"][None]])
    F = f2.blocks * P
    out["L2f_w"] = np.stack([gated(w[:F].T, w[F:].T, d.T, f2) for w, d in zip(a["L2_ffn_W12"], a["L2_ffn_W3"])])
    out["L2f_gb"] = np.stack([a["L2_ffn_ln_gamma"], a["L2_ffn_ln_beta"]])
    names = [("routed_w", e) for e in range(E)] + [("shared_w", e) for e in range(f3.shared)]
    out["L3f_w"] = np.stack([gated(a[f"L3_ffn_{n}1"][e], a[f"L3_ffn_{n}3"][e], a[f"L3_ffn_{n}2"][e], f3)
                             for n, e in names])
    for f, w in zip(FFNS, (a["L0_ffn_gate_w"].T, a["L1_ffn_router_w"].T, a["L2_ffn_Wr"].T, a["L3_ffn_router_w"])):
        out[f.name + "_router"] = chunks(w)
    out["L1f_rb"], out["L3f_rb"] = a["L1_ffn_router_b"], a["L3_ffn_router_b"]
    return {n: np.ascontiguousarray(v) for n, v in out.items()}


def kernel(**inputs):
    import concourse.bacc as bacc
    from concourse.bass_utils import run_bass_kernel_spmd

    nc = bacc.Bacc("TRN2", target_bir_lowering=False, num_devices=1)
    arrays = layout(inputs)
    dram = {n: nc.dram_tensor("in_" + n, v.shape, mybir.dt.from_np(v.dtype), kind="ExternalInput").ap()
            for n, v in arrays.items()}
    dram["out"] = nc.dram_tensor("x_out", [T, D], F32, kind="ExternalOutput").ap()
    program(nc, dram)
    r = run_bass_kernel_spmd(nc, [{"in_" + n: v for n, v in arrays.items()}], core_ids=[0])
    return r.results[0]["x_out"].reshape(B, S, D)
```
